# Optimizing a Trainium2 kernel written in Bass

```python
import numpy as np
import jax
import jax.numpy as jnp

def _softmax(x, axis=-1):
    return jax.nn.softmax(x, axis=axis)

def _gelu(x):
    return jax.nn.gelu(x, approximate=True)

def _silu(x):
    return jax.nn.silu(x)

def _sigmoid(x):
    return jax.nn.sigmoid(x)

def _layernorm(x, axis=-1, eps=1e-05):
    m = jnp.mean(x, axis=axis, keepdims=True)
    v = jnp.var(x, axis=axis, keepdims=True)
    return (x - m) / jnp.sqrt(v + eps)

def _scatter_add(tgt, idx, src, axis=0):
    return tgt.at[idx].add(src)

def _segment_sum(src, seg, n):
    return jax.ops.segment_sum(src, seg, n)
kernel_name = 'mk_adj_ffn_d1_adj_r2_227715'

def setup_inputs(seed: int=0):
    np.random.seed(seed)
    _w = jnp.asarray

    def _rec_inputs():
        import jax
        import jax.numpy as jnp
        _gk = jax.random.key(seed)
        x = -0.0002928 + 1 * jax.random.normal(jax.random.fold_in(_gk, 1), (32, 256, 128), jnp.float32)
        _a = jax.random.bernoulli(jax.random.fold_in(_gk, 2), 0.03125, (32, 256, 256))
        _a = jnp.logical_or(_a, jnp.swapaxes(_a, -1, -2))
        _a = jnp.logical_or(_a, jnp.eye(256, dtype=bool))
        _af = _a.astype(jnp.float32)
        _af = _af * jax.random.uniform(jax.random.fold_in(_gk, 3), (32, 256, 256), jnp.float32, 0.05, 1)
        adj = _af
        return (x, adj)
    x, adj = _rec_inputs()

    def _L0_gnn_setup():
        import jax, jax.numpy as jnp
        import numpy as np
        B, N, D, H = (8, 1024, 128, 512)
        RMS_EPS = 1e-06

        def _rmsnorm(h, w, eps=RMS_EPS):
            var = jnp.mean(jnp.square(h), axis=-1, keepdims=True)
            return h * jax.lax.rsqrt(var + eps) * w
        key = jax.random.key(seed)
        ks = jax.random.split(key, 5)
        x = jax.random.normal(ks[0], (B, N, D), dtype=jnp.float32)
        adjacency = jax.random.uniform(ks[1], (B, N, N), dtype=jnp.float32)
        epsilon = jnp.zeros((), dtype=jnp.float32)
        W1 = jax.random.normal(ks[2], (D, H), dtype=jnp.float32) * (1.0 / np.sqrt(D))
        b1 = jnp.zeros((H,), dtype=jnp.float32)
        rms_weight = jnp.ones((H,), dtype=jnp.float32)
        W2 = jax.random.normal(ks[3], (H, D), dtype=jnp.float32) * (1.0 / np.sqrt(H))
        b2 = jnp.zeros((D,), dtype=jnp.float32)
        return {'x': x, 'adjacency': adjacency, 'epsilon': epsilon, 'W1': W1, 'b1': b1, 'rms_weight': rms_weight, 'W2': W2, 'b2': b2}
    _L0_gnn_all = _L0_gnn_setup()
    _L0_gnn_in = {k: v for k, v in _L0_gnn_all.items() if k in ('epsilon', 'W1', 'b1', 'rms_weight', 'W2', 'b2')}
    del _L0_gnn_all

    def _L0_ffn_setup():
        import jax, jax.numpy as jnp
        import numpy as np
        B, N, D = (16, 2048, 128)
        NUM_EXPERTS, TOP_K, HEADS = (4, 2, 4)
        N_EDGES = 524288
        LN_EPS = 1e-05

        def _layernorm(x, g, b):
            mu = x.mean(-1, keepdims=True)
            var = ((x - mu) ** 2).mean(-1, keepdims=True)
            return (x - mu) * jax.lax.rsqrt(var + LN_EPS) * g + b

        def _forward(x, edge_index, W_gat, att_src, att_dst, b_gat, ln_gamma, ln_beta, W1, b1, W2, b2):
            Bc, Nc, Dc = x.shape
            M = Bc * Nc
            x_flat = x.reshape(M, Dc)
            h = (x_flat @ W_gat).reshape(M, HEADS, NUM_EXPERTS)
            loops = jnp.arange(M, dtype=edge_index.dtype)
            src = jnp.concatenate([edge_index[0], loops])
            dst = jnp.concatenate([edge_index[1], loops])
            a_src = (h * att_src).sum(-1)
            a_dst = (h * att_dst).sum(-1)
            e = jax.nn.leaky_relu(a_src[src] + a_dst[dst], negative_slope=0.2)
            e_max = jax.ops.segment_max(e, dst, num_segments=M)
            ee = jnp.exp(e - e_max[dst])
            denom = jax.ops.segment_sum(ee, dst, num_segments=M)
            alpha = ee / (denom[dst] + 1e-16)
            msg = h[src] * alpha[:, :, None]
            agg = jax.ops.segment_sum(msg, dst, num_segments=M).reshape(M, HEADS * NUM_EXPERTS) + b_gat
            scores = _layernorm(agg, ln_gamma, ln_beta).reshape(M, HEADS, NUM_EXPERTS).mean(1)
            scores = scores.reshape(Bc, Nc, NUM_EXPERTS)
            topk_s, topk_i = jax.lax.top_k(scores, TOP_K)
            w = jax.nn.softmax(topk_s, axis=-1)
            out = jnp.zeros_like(x)
            for ei in range(NUM_EXPERTS):
                g = jnp.where(topk_i == ei, w, 0.0).sum(-1)
                hh = jax.nn.gelu(x @ W1[ei] + b1[ei], approximate=False)
                out = out + g[..., None] * (hh @ W2[ei] + b2[ei])
            return out
        key = jax.random.key(seed)
        ks = jax.random.split(key, 8)
        s = 0.05
        return {'x': jax.random.normal(ks[0], (B, N, D), jnp.float32), 'W_gat': jax.random.normal(ks[1], (D, HEADS * NUM_EXPERTS), jnp.float32) * s, 'att_src': jax.random.normal(ks[2], (HEADS, NUM_EXPERTS), jnp.float32) * s, 'att_dst': jax.random.normal(ks[3], (HEADS, NUM_EXPERTS), jnp.float32) * s, 'b_gat': jnp.zeros((HEADS * NUM_EXPERTS,), jnp.float32), 'ln_gamma': jnp.ones((HEADS * NUM_EXPERTS,), jnp.float32), 'ln_beta': jnp.zeros((HEADS * NUM_EXPERTS,), jnp.float32), 'W1': jax.random.normal(ks[4], (NUM_EXPERTS, D, 2 * D), jnp.float32) * s, 'b1': jnp.zeros((NUM_EXPERTS, 2 * D), jnp.float32), 'W2': jax.random.normal(ks[5], (NUM_EXPERTS, 2 * D, D), jnp.float32) * s, 'b2': jnp.zeros((NUM_EXPERTS, D), jnp.float32), 'edge_index': jax.random.randint(ks[6], (2, N_EDGES), 0, B * N, jnp.int32)}
    _L0_ffn_all = _L0_ffn_setup()
    _L0_ffn_in = {k: v for k, v in _L0_ffn_all.items() if k in ('W_gat', 'att_src', 'att_dst', 'b_gat', 'ln_gamma', 'ln_beta', 'W1', 'b1', 'W2', 'b2', 'edge_index')}
    del _L0_ffn_all
    return {'x': x, 'adj': adj, 'L0_gnn_epsilon': _L0_gnn_in['epsilon'], 'L0_gnn_W1': _L0_gnn_in['W1'], 'L0_gnn_b1': _L0_gnn_in['b1'], 'L0_gnn_rms_weight': _L0_gnn_in['rms_weight'], 'L0_gnn_W2': _L0_gnn_in['W2'], 'L0_gnn_b2': _L0_gnn_in['b2'], 'L0_ffn_W_gat': _L0_ffn_in['W_gat'], 'L0_ffn_att_src': _L0_ffn_in['att_src'], 'L0_ffn_att_dst': _L0_ffn_in['att_dst'], 'L0_ffn_b_gat': _L0_ffn_in['b_gat'], 'L0_ffn_ln_gamma': _L0_ffn_in['ln_gamma'], 'L0_ffn_ln_beta': _L0_ffn_in['ln_beta'], 'L0_ffn_W1': _L0_ffn_in['W1'], 'L0_ffn_b1': _L0_ffn_in['b1'], 'L0_ffn_W2': _L0_ffn_in['W2'], 'L0_ffn_b2': _L0_ffn_in['b2'], 'L0_ffn_edge_index': _L0_ffn_in['edge_index']}

def reference(x, adj, L0_gnn_epsilon, L0_gnn_W1, L0_gnn_b1, L0_gnn_rms_weight, L0_gnn_W2, L0_gnn_b2, L0_ffn_W_gat, L0_ffn_att_src, L0_ffn_att_dst, L0_ffn_b_gat, L0_ffn_ln_gamma, L0_ffn_ln_beta, L0_ffn_W1, L0_ffn_b1, L0_ffn_W2, L0_ffn_b2, L0_ffn_edge_index):
    import jax
    import jax.numpy as jnp

    def _L0_gnn_ref(x, adjacency, epsilon, W1, b1, rms_weight, W2, b2):
        import jax, jax.numpy as jnp
        import numpy as np
        B, N, D, H = (8, 1024, 128, 512)
        RMS_EPS = 1e-06

        def _rmsnorm(h, w, eps=RMS_EPS):
            var = jnp.mean(jnp.square(h), axis=-1, keepdims=True)
            return h * jax.lax.rsqrt(var + eps) * w
        neighbor_sum = jnp.einsum('bnm,bmd->bnd', adjacency, x)
        agg = epsilon * x + neighbor_sum
        h = jnp.einsum('bnd,dh->bnh', agg, W1) + b1
        h = jax.nn.silu(_rmsnorm(h, rms_weight))
        out = jnp.einsum('bnh,hd->bnd', h, W2) + b2
        return out

    def _L0_ffn_ref(x, W_gat, att_src, att_dst, b_gat, ln_gamma, ln_beta, W1, b1, W2, b2, edge_index):
        import jax, jax.numpy as jnp
        import numpy as np
        B, N, D = (16, 2048, 128)
        NUM_EXPERTS, TOP_K, HEADS = (4, 2, 4)
        N_EDGES = 524288
        LN_EPS = 1e-05

        def _layernorm(x, g, b):
            mu = x.mean(-1, keepdims=True)
            var = ((x - mu) ** 2).mean(-1, keepdims=True)
            return (x - mu) * jax.lax.rsqrt(var + LN_EPS) * g + b

        def _forward(x, edge_index, W_gat, att_src, att_dst, b_gat, ln_gamma, ln_beta, W1, b1, W2, b2):
            Bc, Nc, Dc = x.shape
            M = Bc * Nc
            x_flat = x.reshape(M, Dc)
            h = (x_flat @ W_gat).reshape(M, HEADS, NUM_EXPERTS)
            loops = jnp.arange(M, dtype=edge_index.dtype)
            src = jnp.concatenate([edge_index[0], loops])
            dst = jnp.concatenate([edge_index[1], loops])
            a_src = (h * att_src).sum(-1)
            a_dst = (h * att_dst).sum(-1)
            e = jax.nn.leaky_relu(a_src[src] + a_dst[dst], negative_slope=0.2)
            e_max = jax.ops.segment_max(e, dst, num_segments=M)
            ee = jnp.exp(e - e_max[dst])
            denom = jax.ops.segment_sum(ee, dst, num_segments=M)
            alpha = ee / (denom[dst] + 1e-16)
            msg = h[src] * alpha[:, :, None]
            agg = jax.ops.segment_sum(msg, dst, num_segments=M).reshape(M, HEADS * NUM_EXPERTS) + b_gat
            scores = _layernorm(agg, ln_gamma, ln_beta).reshape(M, HEADS, NUM_EXPERTS).mean(1)
            scores = scores.reshape(Bc, Nc, NUM_EXPERTS)
            topk_s, topk_i = jax.lax.top_k(scores, TOP_K)
            w = jax.nn.softmax(topk_s, axis=-1)
            out = jnp.zeros_like(x)
            for ei in range(NUM_EXPERTS):
                g = jnp.where(topk_i == ei, w, 0.0).sum(-1)
                hh = jax.nn.gelu(x @ W1[ei] + b1[ei], approximate=False)
                out = out + g[..., None] * (hh @ W2[ei] + b2[ei])
            return out
        return _forward(x, edge_index, W_gat, att_src, att_dst, b_gat, ln_gamma, ln_beta, W1, b1, W2, b2)
    x = x + _L0_gnn_ref(_layernorm(x, axis=-1), adj, L0_gnn_epsilon, L0_gnn_W1, L0_gnn_b1, L0_gnn_rms_weight, L0_gnn_W2, L0_gnn_b2)
    x = x + _L0_ffn_ref(_layernorm(x, axis=-1), L0_ffn_W_gat, L0_ffn_att_src, L0_ffn_att_dst, L0_ffn_b_gat, L0_ffn_ln_gamma, L0_ffn_ln_beta, L0_ffn_W1, L0_ffn_b1, L0_ffn_W2, L0_ffn_b2, L0_ffn_edge_index)
    return x

_drawn_inputs = setup_inputs


def setup_inputs(seed=0):
    import zlib

    import numpy as np

    out = dict(_drawn_inputs(seed))
    spreads = {'L0_gnn_b1': (0.0, 0.1),
     'L0_gnn_rms_weight': (1.0, 0.2),
     'L0_gnn_b2': (0.0, 0.1),
     'L0_ffn_b_gat': (0.0, 0.1),
     'L0_ffn_ln_gamma': (1.0, 0.2),
     'L0_ffn_ln_beta': (0.0, 0.1),
     'L0_ffn_b1': (0.0, 0.1),
     'L0_ffn_b2': (0.0, 0.1)}
    factors = {'L0_ffn_att_src': 4.377, 'L0_ffn_att_dst': 5.727}
    for name, (base, spread) in spreads.items():
        noise = np.random.default_rng([zlib.crc32(name.encode()), seed]).standard_normal(out[name].shape)
        drawn = base * np.exp(spread * noise) if base else spread * noise
        out[name] = jnp.asarray(drawn.astype(out[name].dtype))
    for name, factor in factors.items():
        out[name] = (out[name] * factor).astype(out[name].dtype)
    return out
```

```python
from contextlib import ExitStack

import concourse.bass as bass
from concourse import mybir

P = 128
GRAPHS, NODES, D = 32, 256, 128
H = 512
M = GRAPHS * NODES
TILES = M // P
EXPERTS, HEADS, F = 4, 4, 256
HK = HEADS * EXPERTS
EDGES = 524288
ECOLS = EDGES // P
ETILES = ECOLS + TILES
ROW = 2 * HEADS + HK
ACC = HEADS + HK
LN_EPS, RMS_EPS = 1e-5, 1e-6
LOW = -1e30
HC = H // P
FC = EXPERTS * F // P
GROUP = 512
GROUPS = M // GROUP


def build(nc, x, adj, eps, W1, b1, rms_w, W2, b2, W_gat, att_src, att_dst, b_gat, ln_g, ln_b,
          We1, be1, We2, be2, edges, out):
    fp32, i32 = mybir.dt.float32, mybir.dt.int32
    ALU, ACT, AX = mybir.AluOpType, mybir.ActivationFunctionType, mybir.AxisListType
    ctx = ExitStack()
    with ctx:
        def sb(name, shape, dt=fp32):
            return ctx.enter_context(nc.sbuf_tensor("sb_" + name, shape, dt))

        def pb(name, shape, dt=fp32):
            return ctx.enter_context(nc.psum_tensor("ps_" + name, shape, dt))

        def sem(name):
            return ctx.enter_context(nc.semaphore(name))

        table = nc.dram_tensor("table", [M + 1, ROW], fp32, kind="Internal").ap()
        state = nc.dram_tensor("state", [M + 1, ROW], fp32, kind="Internal").ap()

        ident = sb("ident", [P, P])
        ones = sb("ones", [P, P])
        lower = sb("lower", [P, P])
        epsI = sb("epsI", [P, 4 * P])
        eps_c = sb("eps_c", [P, 1])
        w1 = sb("w1", [P, H])
        b1_c = sb("b1_c", [P, HC])
        rms_c = sb("rms_c", [P, HC])
        w2 = sb("w2", [P, HC, D])
        b2_r = sb("b2_r", [P, D])
        wcat = sb("wcat", [P, ROW])
        watt = sb("watt", [P, 2, HK])
        att_r = sb("att_r", [P, 2, HK])
        bgat_r = sb("bgat_r", [P, HK])
        lng_r = sb("lng_r", [P, HK])
        lnb_r = sb("lnb_r", [P, HK])
        we1 = sb("we1", [P, EXPERTS, F])
        be1_c = sb("be1_c", [P, FC])
        we2 = sb("we2", [P, FC, D])
        be2_r = sb("be2_r", [1, EXPERTS * D])
        xs = sb("xs", [P, TILES, D])
        x2nT = sb("x2nT", [P, M])
        adjs = sb("adjs", [P, 2, 2, NODES])
        st = sb("st", [P, 2, 6])
        mv = sb("mv", [P, 2, 2, 2])
        var = sb("var", [P, 6])
        root = sb("root", [P, 6])
        nhalf = sb("nhalf", [P, 6])
        newt = sb("newt", [P, 6])
        st2 = sb("st2", [P, 2, 6])
        mv2 = sb("mv2", [P, 2, 2, 2])
        xn = sb("xn", [P, 2, 2, D])
        adjT = sb("adjT", [P, 2, 2, NODES])
        aggT = sb("aggT", [P, 2, NODES])
        sq = sb("sq", [P, 2, HC, NODES])
        rb = sb("rb", [P, NODES])
        uu = sb("uu", [P, 2, HC, NODES])
        ss = sb("ss", [P, 2, HC, NODES])
        x2n = sb("x2n", [P, 2, 2, D])
        x2nTc = sb("x2nTc", [P, 2, NODES])
        tb = sb("tb", [P, 2, 2, ROW])
        srcs = sb("srcs", [P, ECOLS + TILES], i32)
        dsts = sb("dsts", [P, ECOLS + TILES], i32)
        idx = sb("idx", [P, 2], i32)
        zrow = sb("zrow", [P, ROW])
        st0 = sb("st0", [P, ROW])
        dstf = sb("dstf", [P, 1])
        srow = sb("srow", [P, ROW])
        drow = sb("drow", [P, ROW])
        strow = sb("strow", [P, ROW])
        newrow = sb("newrow", [P, ROW])
        eq = sb("eq", [P, P])
        pen = sb("pen", [P, P])
        masked = sb("masked", [P, HEADS, P])
        small = sb("small", [P, 8, HEADS])
        vals = sb("vals", [P, ACC])
        lead = sb("lead", [P, 4])
        sidx = sb("sidx", [P, 1], i32)
        agg = sb("agg", [P, TILES, ROW])
        gf = sb("gf", [P, TILES, HK])
        gw = sb("gw", [P, TILES, HK])
        gs = sb("gs", [P, 5, TILES])
        sc = sb("sc", [P, TILES, EXPERTS])
        gates = sb("gates", [P, TILES, EXPERTS])
        hh = [m[:, 0:ECOLS].bitcast(fp32).rearrange("p (c n) -> p c n", c=FC) for m in (srcs, dsts)]
        gcol = sb("gcol", [P, 2, EXPERTS])

        bank_T = pb("T", [P, 512])
        bank_A = pb("A", [P, 512])
        ps_H = pb("H", [P, 2, HC, NODES])
        bank_O = pb("O", [P, 512])
        bank_S = pb("S", [P, 512])
        ps_T = bank_T[:, :].rearrange("p (m n) -> p m n", m=2)
        ps_A, ps_Q = bank_A[:, 0:NODES], bank_A[:, NODES:NODES + 2]
        ps_O = bank_O[:, 0:2 * D].rearrange("p (u d) -> p u d", u=2)
        ps_B = bank_O[:, 2 * D:2 * D + 2 * ROW]
        ps_R, ps_X = bank_S[:, 0:NODES], bank_S[:, NODES:2 * NODES]
        halfH = [ps_H[:, k, 2 * j:2 * j + 2, :].rearrange("p a b -> p (a b)") for k in range(2) for j in range(2)]

        names = ["xn_ready", "adjT_in_psum", "adjT_ready", "aggT_in_psum", "aggT_ready",
                 "h_in_psum", "sq_ready", "ss_in_psum", "u_ready", "s_ready", "o_in_psum", "x1_ready",
                 "x2n_ready", "x2nT_in_psum", "x2nT_ready", "tb_in_psum", "tb_ready", "weights", "ld_gat",
                 "const_a", "const_b", "gat_w", "wcat_ready", "state_init", "pool_const",
                 "edges_loaded", "edges_ready", "idx_ready", "dstf_ready", "eq_ready", "as_in_psum",
                 "mnew_ready", "ee_in", "ee_ready", "vals_ready", "sum_in_psum", "newrow_ready",
                 "setup_chain", "edge_chain", "gate_chain", "comb_chain", "ln1_stats", "ln1_mv", "ln2_stats", "ln2_mv", "x_b2", "ms_ready", "newton", "root_ready", "rb_in_psum", "rb_ready", "gate_newton", "agg_in",
                 "gates_e", "gates_exp", "gates_ready", "hh_in_psum", "hh_ready", "eo_in_psum", "eo_used",
                 "iota_done", "zero_done", "sig_done"]
        s = {n: sem(n) for n in names}
        x_loaded = [sem(f"x_loaded{p}") for p in range(2)]
        adj_loaded = [sem(f"adj_loaded{p}") for p in range(2)]
        tb_stored = [sem(f"tb_stored{p}") for p in range(2)]
        src_in, dst_in, state_in, row_stored = ([sem(f"{n}{p}") for p in range(2)]
                                                for n in ("src_in", "dst_in", "state_in", "row_stored"))
        out_stored = [sem(f"out_stored{p}") for p in range(2)]

        x_t = x.rearrange("g (u q) d -> g q u d", q=P)
        adj_t = adj.rearrange("g (u q) m -> g q u m", q=P)
        out_t = out.rearrange("g (u q) d -> g q u d", q=P)
        tab_t = table[0:M, :].rearrange("(g u q) c -> g q u c", u=2, q=P)

        FIRST, LOOP_FROM, LOOP_TO, END = -2, 6, GRAPHS - 2, GRAPHS + 5

        def piped(eng, step):
            for i in range(FIRST, LOOP_FROM):
                step(i, i % 2)
            with eng.Fori(LOOP_FROM // 2, LOOP_TO // 2) as j:
                step(2 * j, 0)
                step(2 * j + 1, 1)
            for i in range(LOOP_TO, END):
                step(i, i % 2)

        def on(i, lag):
            return not isinstance(i, int) or 0 <= i - lag < GRAPHS

        def some(eng, semaphore, value, most=GRAPHS):
            if not isinstance(value, int):
                eng.wait_ge(semaphore, value)
            elif value > 0:
                eng.wait_ge(semaphore, value if most is None else min(value, most))

        def alone(eng):
            eng.wait_ge(s["pool_const"], 2)

        def half(i, p):
            return (i - p) // 2 if isinstance(i, int) else (i - p) >> 1

        block = ctx.enter_context(nc.Block())

        @block.sync
        def _(sp):
            n = 0
            for dst, src in (
                (w1[:, :], W1), (b1_c[:, :], b1.rearrange("(c p) -> p c", p=P)),
                (rms_c[:, :], rms_w.rearrange("(c p) -> p c", p=P)),
                (w2[:, :, :], W2.rearrange("(c p) d -> p c d", p=P)),
                (b2_r[:, :], b2[None, :].to_broadcast([P, D])),
                (eps_c[:, :], eps[None, :].to_broadcast([P, 1])),
                (we1[:, :, :], We1.rearrange("e d f -> d e f")),
                (be1_c[:, :], be1.rearrange("e (c p) -> p (e c)", p=P)),
                (we2[:, :, :], We2.rearrange("e (c p) d -> p (e c) d", p=P)),
                (be2_r[:, :], be2.rearrange("e d -> (e d)")[None, :]),
                (wcat[:, 2 * HEADS:ROW], W_gat),
                (att_r[:, 0, :], att_src.rearrange("h k -> (h k)")[None, :].to_broadcast([P, HK])),
                (att_r[:, 1, :], att_dst.rearrange("h k -> (h k)")[None, :].to_broadcast([P, HK])),
                (bgat_r[:, :], b_gat[None, :].to_broadcast([P, HK])),
                (lng_r[:, :], ln_g[None, :].to_broadcast([P, HK])),
                (lnb_r[:, :], ln_b[None, :].to_broadcast([P, HK])),
            ):
                with nc.allow_non_contiguous_dma(reason="small constants"):
                    sp.dma_start(dst, src).then_inc(s["weights"], 16)
                n += 1
            assert n == 16
            sp.dma_start(srcs[:, 0:ECOLS], edges[0, :].rearrange("(p c) -> p c", p=P)).then_inc(s["edges_loaded"], 16)
            sp.dma_start(dsts[:, 0:ECOLS], edges[1, :].rearrange("(p c) -> p c", p=P)).then_inc(s["edges_loaded"], 16)
            sp.wait_ge(s["zero_done"], 2)
            sp.dma_start(table[M:M + 1, :], zrow[0:1, :]).then_inc(s["state_init"], 16)
            sp.dma_start(state[M:M + 1, :], st0[0:1, :]).then_inc(s["state_init"], 16)
            for t in range(TILES):
                sp.dma_start(state[t * P:(t + 1) * P, :], st0[:, :]).then_inc(s["state_init"], 16)

            def step(i, p):
                q = 1 - p
                if on(i, -2):
                    some(sp, x_loaded[p], 16 * half(i + 2, p), None)
                    sp.dma_start(xs[:, bass.ds(2 * (i + 2), 2), :], x_t[bass.ds(i + 2, 1), :, :, :][0]).then_inc(x_loaded[p], 16)
                if on(i, -1):
                    some(sp, s["adjT_in_psum"], i)
                    sp.dma_start(adjs[:, q, :, :], adj_t[bass.ds(i + 1, 1), :, :, :][0]).then_inc(adj_loaded[q], 16)
                if on(i, 5):
                    sp.wait_ge(s["tb_ready"], i - 4)
                    sp.dma_start(tab_t[bass.ds(i - 5, 1), :, :, :][0], tb[:, q, :, :]).then_inc(tb_stored[q], 16)

            piped(sp, step)

            for p in range(2):
                sp.wait_ge(row_stored[p], 16 * ETILES // 2)
            sp.dma_start(agg[:, :, :], state[0:M, :].rearrange("(t q) c -> q t c", q=P)).then_inc(s["agg_in"], 16)

            def estore(g, p):
                sp.wait_ge(s["eo_used"], 4 * g + 4)
                sp.dma_start(out_t[bass.ds(2 * g, 2), :, :, :].rearrange("g q u d -> q g u d"),
                             xs[:, bass.ds(4 * g, 4), :].rearrange("q (g u) d -> q g u d", g=2)).then_inc(out_stored[p], 16)

            with sp.Fori(0, GROUPS // 2) as j:
                estore(2 * j, 0)
                estore(2 * j + 1, 1)
            for p in range(2):
                sp.wait_ge(out_stored[p], 16 * GROUPS // 2)
                sp.wait_ge(tb_stored[p], 16 * GRAPHS // 2)

        @block.gpsimd
        def _(pool):
            pool.memset(ident[:, :], 0.0).then_inc(s["const_a"], 1)
            pool.memset(ones[:, :], 1.0).then_inc(s["const_a"], 1)
            pool.wait_ge(s["const_a"], 2)
            pool.affine_select(out=ident[:, :], in_=ident[:, :], compare_op=ALU.not_equal, fill=1.0,
                               base=0, pattern=[[-1, P]], channel_multiplier=1).then_inc(s["pool_const"], 1)
            pool.affine_select(out=lower[:, :], in_=ones[:, :], compare_op=ALU.is_gt, fill=0.0,
                               base=0, pattern=[[-1, P]], channel_multiplier=1).then_inc(s["pool_const"], 1)
            pool.iota(srcs[:, ECOLS:ECOLS + TILES], pattern=[[P, TILES]], base=0, channel_multiplier=1).then_inc(s["iota_done"], 1)
            pool.iota(dsts[:, ECOLS:ECOLS + TILES], pattern=[[P, TILES]], base=0, channel_multiplier=1).then_inc(s["iota_done"], 1)
            pool.memset(zrow[:, :], 0.0).then_inc(s["zero_done"], 1)
            pool.memset(st0[:, 0:HEADS], LOW).then_inc(s["const_b"], 1)
            pool.memset(st0[:, HEADS:ROW], 0.0).then_inc(s["zero_done"], 1)

            pool.wait_ge(s["const_b"], 1)
            pool.wait_ge(s["state_init"], 16 * (TILES + 2))
            for p in range(2):
                pool.wait_ge(tb_stored[p], 16 * GRAPHS // 2)
            last_row = pool.to_reg(M)
            def gather(rows, source, column, signal):
                pool.indirect_dma_start(rows[:, :], None, source, bass.IndirectOffsetOnAxis(ap=idx[:, column:column + 1], axis=0),
                                        bounds_check=last_row, oob_is_err=False).then_inc(signal, 16)

            def edge_tile(t, p):
                done, indices = pool.to_reg(t + 1), pool.to_reg(2 * t + 2)
                alone(pool)
                pool.wait_ge(s["idx_ready"], indices)
                gather(srow, table, 0, src_in[p])
                gather(drow, table, 1, dst_in[p])
                gather(strow, state, 1, state_in[p])
                alone(pool)
                pool.wait_ge(s["newrow_ready"], done)
                pool.indirect_dma_start(state, bass.IndirectOffsetOnAxis(ap=sidx[:, 0:1], axis=0), newrow[:, :], None,
                                        bounds_check=last_row, oob_is_err=False).then_inc(row_stored[p], 16)

            with pool.Fori(0, ETILES // 2) as j:
                edge_tile(2 * j, 0)
                edge_tile(2 * j + 1, 1)

        @block.tensor
        def _(pe):
            pe.wait_ge(s["pool_const"], 2)
            pe.wait_ge(s["weights"], 16 * 16)

            def step(i, p):
                q = 1 - p
                if on(i, 0):
                    pe.wait_ge(adj_loaded[p], 16 * half(i, p) + 16)
                    some(pe, s["adjT_ready"], i)
                    for nt in range(2):
                        for mt in range(2):
                            last = nc.tensor.transpose(ps_T[:, mt, nt * P:(nt + 1) * P],
                                                       adjs[:, p, nt, mt * P:(mt + 1) * P], ident[:, :])
                    last.then_inc(s["adjT_in_psum"], 1)
                if on(i, 2):
                    pe.wait_ge(s["root_ready"], i + 2)
                    some(pe, s["x2nT_ready"], i - 4)
                    some(pe, s["rb_ready"], i - 2)
                    for u in range(2):
                        last = nc.tensor.matmul(ps_R[:, u * P:(u + 1) * P], root[:, 2 + u:3 + u].to_broadcast([P, P]),
                                                ident[:, :], start=True, stop=True)
                    last.then_inc(s["rb_in_psum"], 1)
                if on(i, 5):
                    pe.wait_ge(s["x2nT_ready"], i - 4)
                    pe.wait_ge(s["wcat_ready"], 2)
                    some(pe, s["tb_ready"], i - 5)
                    some(pe, s["x1_ready"], i - 3)
                    for u in range(2):
                        last = nc.tensor.matmul(ps_B[:, u * ROW:(u + 1) * ROW],
                                                x2nTc[:, q, u * P:(u + 1) * P], wcat[:, :], start=True, stop=True)
                    last.then_inc(s["tb_in_psum"], 1)
                if on(i, 4):
                    pe.wait_ge(s["x2n_ready"], i - 3)
                    some(pe, s["x2nT_ready"], i - 4)
                    for u in range(2):
                        last = nc.tensor.transpose(ps_X[:, u * P:(u + 1) * P], x2n[:, p, u, :], ident[:, :])
                    last.then_inc(s["x2nT_in_psum"], 1)
                if on(i, 1):
                    pe.wait_ge(s["aggT_ready"], i)
                    some(pe, s["u_ready"], i - 2)
                    for c in range(HC):
                        last = nc.tensor.matmul(ps_H[:, q, c, :], w1[:, c * P:(c + 1) * P], aggT[:, q, :], start=True, stop=True)
                    last.then_inc(s["h_in_psum"], 1)
                if on(i, 0):
                    pe.wait_ge(s["xn_ready"], i + 1)
                    pe.wait_ge(s["adjT_ready"], i + 1)
                    some(pe, s["aggT_ready"], i)
                    some(pe, s["ms_ready"], i + 3, None)
                    for mt in range(2):
                        last = nc.tensor.matmul(ps_A, xn[:, p, mt, :], adjT[:, p, mt, :],
                                                start=(mt == 0), stop=(mt == 1))
                    last.then_inc(s["aggT_in_psum"], 1)
                if on(i, 3):
                    pe.wait_ge(s["s_ready"], i - 2)
                    some(pe, s["x1_ready"], i - 3)
                    some(pe, s["tb_ready"], i - 4)
                    for nt in range(2):
                        for c in range(HC):
                            last = nc.tensor.matmul(ps_O[:, nt, :], ss[:, q, c, nt * P:(nt + 1) * P], w2[:, c, :],
                                                    start=(c == 0), stop=(c == HC - 1))
                    last.then_inc(s["o_in_psum"], 1)
                if on(i, 1):
                    pe.wait_ge(s["sq_ready"], i)
                    some(pe, s["ms_ready"], i + 3, None)
                    some(pe, s["aggT_ready"], i + 1)
                    for u in range(2):
                        for c in range(HC):
                            last = nc.tensor.matmul(ps_Q[:, u:u + 1], sq[:, q, c, u * P:(u + 1) * P], ones[:, 0:1],
                                                    start=(c == 0), stop=(c == HC - 1))
                    last.then_inc(s["ss_in_psum"], 1)

            piped(pe, step)

            def edge_tile(t, p, j):
                pe.wait_ge(s["dstf_ready"], t + 1)
                pe.wait_ge(src_in[p], 16 * j + 16)
                nc.tensor.matmul(bank_T[:, 0:P], dstf[:, 0:1].to_broadcast([P, P]), ident[:, :], start=True, stop=True)
                for h in range(HEADS):
                    last = nc.tensor.matmul(halfH[0][:, h * P:(h + 1) * P], srow[:, h:h + 1].to_broadcast([P, P]),
                                            ident[:, :], start=True, stop=True)
                last.then_inc(s["as_in_psum"], 1)
                pe.wait_ge(s["vals_ready"], t + 1)
                nc.tensor.matmul(bank_S[:, 0:ACC], eq[:, :], vals[:, :], start=True, stop=True).then_inc(s["sum_in_psum"], 1)

            with pe.Fori(0, ETILES // 2) as j:
                edge_tile(2 * j, 0, j)
                edge_tile(2 * j + 1, 1, j)

            bank = halfH
            obank = [bank_T[:, :], bank_A[:, :]]
            pe.wait_ge(s["gates_ready"], 1)

            def experts(g, p, outs):
                for c in range(FC):
                    if not isinstance(g, int) or g < GROUPS:
                        some(pe, s["hh_ready"], 8 * g + c - 3, None)
                        nc.tensor.matmul(bank[c % 4], we1[:, c // 2, (c % 2) * P:(c % 2) * P + P],
                                         x2nT[:, bass.ds(g * GROUP, GROUP)], start=True, stop=True).then_inc(s["hh_in_psum"], 1)
                    if outs and c % 2:
                        k = c // 2
                        pe.wait_ge(s["hh_ready"], 8 * g)
                        some(pe, s["eo_used"], 4 * (g - 1) + k - 1, None)
                        nc.tensor.matmul(obank[k % 2], ones[0:1, :], be2_r[:, :], start=True, stop=False)
                        for j in range(FC):
                            last = nc.tensor.matmul(obank[k % 2][:, (j // 2) * D:(j // 2 + 1) * D],
                                                    hh[1 - p][:, j, k * P:(k + 1) * P], we2[:, j, :],
                                                    start=False, stop=(j == FC - 1))
                        last.then_inc(s["eo_in_psum"], 1)

            experts(0, 0, False)
            experts(1, 1, True)
            with pe.Fori(1, GROUPS // 2) as j:
                experts(2 * j, 0, True)
                experts(2 * j + 1, 1, True)
            experts(GROUPS, 0, True)

        @block.scalar
        def _(act):
            act.wait_ge(s["weights"], 16 * 16)
            act.wait_ge(s["pool_const"], 2)

            def step(i, p):
                q = 1 - p
                if on(i, 2):
                    act.wait_ge(s["rb_in_psum"], i - 1)
                    some(act, s["x2nT_in_psum"], i - 3)
                    some(act, s["u_ready"], i - 2)
                    nc.scalar.activation(rb[:, :], ps_R, ACT.Identity).then_inc(s["rb_ready"], 1)
                if on(i, 4):
                    act.wait_ge(s["x2nT_in_psum"], i - 3)
                    some(act, s["tb_in_psum"], i - 5)
                    nc.scalar.activation(x2nTc[:, p, :], ps_X, ACT.Identity)
                    nc.scalar.activation(x2nT[:, bass.ds((i - 4) * NODES, NODES)], ps_X,
                                         ACT.Identity).then_inc(s["x2nT_ready"], 1)
                if on(i, 1):
                    act.wait_ge(s["h_in_psum"], i)
                    some(act, s["ss_in_psum"], i - 2)
                    for c in range(HC):
                        last = nc.scalar.activation(sq[:, q, c, :], ps_H[:, q, c, :], ACT.Square, bias=b1_c[:, c:c + 1])
                    last.then_inc(s["sq_ready"], 1)
                if on(i, 2):
                    act.wait_ge(s["u_ready"], i - 1)
                    some(act, s["o_in_psum"], i - 3)
                    for c in range(HC):
                        last = nc.scalar.activation(ss[:, p, c, :], uu[:, p, c, :], ACT.Silu, scale=rms_c[:, c:c + 1])
                    last.then_inc(s["s_ready"], 1)

            piped(act, step)

            with act.Fori(0, ETILES) as t:
                act.wait_ge(s["mnew_ready"], t + 1)
                nc.scalar.activation(small[:, 4:6, :], small[:, 2:4, :], ACT.Exp).then_inc(s["ee_ready"], 1)
            act.wait_ge(s["gates_e"], 1)
            nc.scalar.activation(gates[:, :, :], sc[:, :, :], ACT.Exp).then_inc(s["gates_exp"], 1)

            bank = halfH

            def experts(g, p):
                some(act, s["eo_in_psum"], 4 * g - 4, None)
                for c in range(FC):
                    act.wait_ge(s["hh_in_psum"], 8 * g + c + 1)
                    nc.scalar.activation(hh[p][:, c, :], bank[c % 4], ACT.Gelu, bias=be1_c[:, c:c + 1]).then_inc(s["hh_ready"], 1)

            experts(0, 0)
            experts(1, 1)
            with act.Fori(1, GROUPS // 2) as j:
                experts(2 * j, 0)
                experts(2 * j + 1, 1)

        @block.vector
        def _(dve):
            V = nc.vector
            setup = [0]

            def link1(ins):
                setup[0] += 1
                ins.then_inc(s["setup_chain"], 1)
                dve.wait_ge(s["setup_chain"], setup[0])

            dve.wait_ge(s["weights"], 16 * 16)
            dve.wait_ge(s["pool_const"], 2)
            link1(V.memset(epsI[:, :], 0.0))
            for k in (0, 3):
                link1(V.tensor_scalar(epsI[:, k * P:(k + 1) * P], ident[:, :], eps_c[:, 0:1], None, ALU.mult))
            for k in range(2):
                link1(V.tensor_tensor(watt[:, k, :], wcat[:, 2 * HEADS:ROW], att_r[:, k, :], ALU.mult))
                V.reduce_sum(wcat[:, k * HEADS:(k + 1) * HEADS],
                             watt[:, k, :].rearrange("p (h k) -> p h k", h=HEADS), AX.X).then_inc(s["wcat_ready"], 1)
            link1(V.memset(var[:, :], 1.0))
            dve.wait_ge(s["edges_loaded"], 32)
            V.tensor_scalar(srcs[:, 0:ECOLS], srcs[:, 0:ECOLS], M - 1, None, ALU.min).then_inc(s["edges_ready"], 1)
            V.tensor_scalar(dsts[:, 0:ECOLS], dsts[:, 0:ECOLS], M, None, ALU.min).then_inc(s["edges_ready"], 1)

            def link(name, value, ins):
                ins.then_inc(s[name], 1)
                dve.wait_ge(s[name], value)

            def mean_var(k, n, src, stats, mvs):
                for u in range(2):
                    last = V.bn_stats(stats[:, u, :], src[u])
                last.then_inc(s[f"{k}_stats"], 1)
                alone(dve)
                dve.wait_ge(s[f"{k}_stats"], n)
                for u in range(2):
                    last = V.bn_aggr(mvs[:, u, :], stats[:, u, :])
                last.then_inc(s[f"{k}_mv"], 1)

            def rsqrt(name, v, y, w, scratch, count, per):
                n = [0]

                def chain(ins):
                    n[0] += 1
                    ins.then_inc(s[name], 1)
                    dve.wait_ge(s[name], count * per + n[0])

                chain(V.tensor_scalar(y.bitcast(i32), v.bitcast(i32), 1, None, ALU.logical_shift_right))
                V.tensor_scalar(w, v, -0.5, None, ALU.mult)
                chain(V.tensor_scalar(y.bitcast(i32), y.bitcast(i32), -1.0, float(0x5F3759DF), ALU.mult, ALU.add))
                for it in range(4):
                    chain(V.tensor_tensor(scratch, y, y, ALU.mult))
                    chain(V.tensor_tensor(scratch, scratch, w, ALU.mult))
                    last = V.scalar_tensor_tensor(y, scratch, 1.5, y, ALU.add, ALU.mult)
                    if it < 3:
                        chain(last)
                assert n[0] == per
                return last

            def tiles(g):
                return [xs[:, bass.ds(2 * g + u, 1), :].squeeze(1) for u in range(2)]

            def step(i, p):
                q = 1 - p
                if on(i, -1):
                    dve.wait_ge(s["ln1_mv"], i + 2)
                    last = V.tensor_scalar(var[:, 0:2], mv[:, q, :, 1], LN_EPS, None, ALU.add)
                if on(i, 2):
                    dve.wait_ge(s["ss_in_psum"], i - 1)
                    last = V.tensor_scalar(var[:, 2:4], ps_Q, 1.0 / H, RMS_EPS, ALU.mult, ALU.add)
                if on(i, 4):
                    dve.wait_ge(s["ln2_mv"], i - 3)
                    last = V.tensor_scalar(var[:, 4:6], mv2[:, p, :, 1], LN_EPS, None, ALU.add)
                if on(i, -1) or on(i, 2) or on(i, 4):
                    link("ms_ready", i + 3, last)
                    some(dve, s["rb_in_psum"], i - 2)
                    rsqrt("newton", var[:, :], root[:, :], nhalf[:, :], newt[:, :], i + 1, 13).then_inc(s["root_ready"], 1)
                    dve.wait_ge(s["root_ready"], i + 2)
                else:
                    V.tensor_copy(newt[:, 0:1], var[:, 0:1]).then_inc(s["ms_ready"], 1)
                if on(i, -1):
                    some(dve, s["aggT_in_psum"], i)
                    for u in range(2):
                        last = V.tensor_scalar(xn[:, q, u, :], tiles(i + 1)[u], mv[:, q, u, 0:1], root[:, u:u + 1], ALU.subtract, ALU.mult)
                    last.then_inc(s["xn_ready"], 1)
                if on(i, 4):
                    some(dve, s["x2nT_in_psum"], i - 5)
                    for u in range(2):
                        last = V.tensor_scalar(x2n[:, p, u, :], tiles(i - 4)[u], mv2[:, p, u, 0:1], root[:, 4 + u:5 + u], ALU.subtract, ALU.mult)
                    last.then_inc(s["x2n_ready"], 1)
                if on(i, 5):
                    dve.wait_ge(s["tb_in_psum"], i - 4)
                    some(dve, tb_stored[q], 16 * half(i - 5, q), None)
                    V.tensor_copy(tb[:, q, :, :], ps_B.rearrange("p (u c) -> p u c", u=2)).then_inc(s["tb_ready"], 1)
                if on(i, -2):
                    alone(dve)
                    dve.wait_ge(x_loaded[p], 16 * half(i + 2, p) + 16)
                    mean_var("ln1", i + 3, tiles(i + 2), st, mv[:, p, :, :])
                if on(i, 0):
                    dve.wait_ge(s["adjT_in_psum"], i + 1)
                    some(dve, s["aggT_in_psum"], i - 1)
                    V.tensor_tensor(adjT[:, p, :, :].rearrange("p a b -> p (a b)"), bank_T[:, :], epsI[:, :], ALU.add).then_inc(s["adjT_ready"], 1)
                    dve.wait_ge(s["aggT_in_psum"], i + 1)
                    some(dve, s["h_in_psum"], i - 1)
                    V.tensor_copy(aggT[:, p, :], ps_A).then_inc(s["aggT_ready"], 1)
                if on(i, 3):
                    xg = xs[:, bass.ds(2 * (i - 3), 2), :]
                    link("x_b2", i - 2, V.tensor_tensor(xg, xg, b2_r[:, :].unsqueeze(1).to_broadcast([P, 2, D]), ALU.add))
                    dve.wait_ge(s["o_in_psum"], i - 2)
                    V.tensor_tensor(xg, xg, ps_O, ALU.add).then_inc(s["x1_ready"], 1)
                    alone(dve)
                    dve.wait_ge(s["x1_ready"], i - 2)
                    mean_var("ln2", i - 2, tiles(i - 3), st2, mv2[:, q, :, :])
                if on(i, 2):
                    dve.wait_ge(s["rb_ready"], i - 1)
                    some(dve, s["s_ready"], i - 3)
                    for c in range(HC):
                        last = V.scalar_tensor_tensor(uu[:, p, c, :], ps_H[:, p, c, :], b1_c[:, c:c + 1], rb[:, :], ALU.add, ALU.mult)
                    last.then_inc(s["u_ready"], 1)

            piped(dve, step)

            dve.wait_ge(s["edges_ready"], 2)
            dve.wait_ge(s["iota_done"], 2)
            LINKS = 11
            def edge_tile(t, p, j):
                k = [0]

                def chain(ins):
                    k[0] += 1
                    ins.then_inc(s["edge_chain"], 1)
                    dve.wait_ge(s["edge_chain"], LINKS * t + k[0])

                dve.wait_ge(row_stored[1 - p], 16 * j + 16 * p)
                V.tensor_copy(idx[:, 0:1], srcs[:, bass.ds(t, 1)]).then_inc(s["idx_ready"], 1)
                V.tensor_copy(idx[:, 1:2], dsts[:, bass.ds(t, 1)]).then_inc(s["idx_ready"], 1)
                V.tensor_copy(dstf[:, :], dsts[:, bass.ds(t, 1)]).then_inc(s["dstf_ready"], 1)
                dve.wait_ge(s["dstf_ready"], t + 1)
                dve.wait_ge(s["as_in_psum"], t + 1)
                V.tensor_scalar(eq[:, :], bank_T[:, 0:P], dstf[:, 0:1], None, ALU.is_equal).then_inc(s["eq_ready"], 1)
                dve.wait_ge(s["eq_ready"], t + 1)
                chain(V.tensor_scalar(pen[:, :], eq[:, :], -1.0, -LOW, ALU.add, ALU.mult))
                chain(V.tensor_tensor(masked[:, :, :], halfH[0].rearrange("p (h n) -> p h n", h=HEADS),
                                      pen[:, :].unsqueeze(1).to_broadcast([P, HEADS, P]), ALU.add))
                chain(V.reduce_max(small[:, 0, :], masked[:, :, :], AX.X))
                for signal in (src_in, dst_in, state_in):
                    dve.wait_ge(signal[p], 16 * j + 16)
                V.tensor_tensor(small[:, 1, :], srow[:, 0:HEADS], drow[:, HEADS:2 * HEADS], ALU.add)
                chain(V.tensor_tensor(small[:, 0, :], small[:, 0, :], drow[:, HEADS:2 * HEADS], ALU.add))
                chain(V.scalar_tensor_tensor(small[:, 6:8, :], small[:, 0:2, :], 0.2, small[:, 0:2, :], ALU.mult, ALU.max))
                chain(V.tensor_tensor(newrow[:, 0:HEADS], small[:, 6, :], strow[:, 0:HEADS], ALU.max))
                V.tensor_tensor(small[:, 2, :], small[:, 7, :], newrow[:, 0:HEADS], ALU.subtract)
                V.tensor_tensor(small[:, 3, :], strow[:, 0:HEADS], newrow[:, 0:HEADS], ALU.subtract).then_inc(s["mnew_ready"], 1)
                chain(V.tensor_tensor(masked[:, 0, :], eq[:, :], lower[:, :], ALU.mult))
                chain(V.reduce_sum(lead[:, 0:1], masked[:, 0, :], AX.X))
                chain(V.tensor_scalar(lead[:, 1:2], lead[:, 0:1], 1.0, float(1 << 20), ALU.min, ALU.mult))
                V.tensor_tensor(sidx[:, :], lead[:, 1:2], dstf[:, :], ALU.add)
                dve.wait_ge(s["ee_ready"], t + 1)
                V.tensor_copy(vals[:, 0:HEADS], small[:, 4, :])
                V.tensor_tensor(vals[:, HEADS:ACC].rearrange("p (h k) -> p h k", h=HEADS),
                                srow[:, 2 * HEADS:ROW].rearrange("p (h k) -> p h k", h=HEADS),
                                small[:, 4, :].unsqueeze(2).to_broadcast([P, HEADS, EXPERTS]), ALU.mult).then_inc(s["vals_ready"], 1)
                V.tensor_tensor(newrow[:, HEADS:2 * HEADS], strow[:, HEADS:2 * HEADS], small[:, 5, :], ALU.mult)
                chain(V.tensor_tensor(newrow[:, 2 * HEADS:ROW].rearrange("p (h k) -> p h k", h=HEADS),
                                      strow[:, 2 * HEADS:ROW].rearrange("p (h k) -> p h k", h=HEADS),
                                      small[:, 5, :].unsqueeze(2).to_broadcast([P, HEADS, EXPERTS]), ALU.mult))
                dve.wait_ge(s["sum_in_psum"], t + 1)
                chain(V.tensor_tensor(newrow[:, HEADS:ROW], newrow[:, HEADS:ROW], bank_S[:, 0:ACC], ALU.add))
                V.tensor_copy(lead[:, 2:3], lead[:, 0:1]).then_inc(s["newrow_ready"], 1)
                assert k[0] == LINKS, k[0]

            with dve.Fori(0, ETILES // 2) as j:
                edge_tile(2 * j, 0, j)
                edge_tile(2 * j + 1, 1, j)

            gates_n = [0]

            def glink(ins):
                gates_n[0] += 1
                ins.then_inc(s["gate_chain"], 1)
                dve.wait_ge(s["gate_chain"], gates_n[0])

            def heads(t):
                return t.rearrange("p t (h k) -> p t h k", h=HEADS)

            def over(t, shape, axis):
                return t.unsqueeze(axis).to_broadcast(shape)

            T16 = [P, TILES, HK]
            dve.wait_ge(s["agg_in"], 16)
            den = agg[:, :, HEADS:2 * HEADS]
            glink(V.tensor_scalar(den, den, 1e-16, None, ALU.add))
            glink(V.reciprocal(den, den))
            for t in range(HEADS):
                last = V.tensor_tensor(gf[:, :, t * EXPERTS:(t + 1) * EXPERTS], agg[:, :, 2 * HEADS + t * EXPERTS:2 * HEADS + (t + 1) * EXPERTS],
                                       over(agg[:, :, HEADS + t], [P, TILES, EXPERTS], 2), ALU.mult)
            glink(last)
            glink(V.tensor_tensor(gf[:, :, :], gf[:, :, :], over(bgat_r[:, :], T16, 1), ALU.add))
            mean, gvar, groot = gs[:, 0, :], gs[:, 1, :], gs[:, 2, :]
            glink(V.reduce_sum(mean, gf[:, :, :], AX.X))
            glink(V.tensor_scalar(mean, mean, 1.0 / HK, None, ALU.mult))
            glink(V.tensor_tensor(gf[:, :, :], gf[:, :, :], over(mean, T16, 2), ALU.subtract))
            glink(V.tensor_tensor(gw[:, :, :], gf[:, :, :], gf[:, :, :], ALU.mult))
            glink(V.reduce_sum(gvar, gw[:, :, :], AX.X))
            glink(V.tensor_scalar(gvar, gvar, 1.0 / HK, LN_EPS, ALU.mult, ALU.add))
            glink(rsqrt("gate_newton", gvar, groot, gs[:, 3, :], gs[:, 4, :], 0, 13))
            glink(V.tensor_tensor(gf[:, :, :], gf[:, :, :], over(groot, T16, 2), ALU.mult))
            glink(V.tensor_tensor(gf[:, :, :], gf[:, :, :], over(lng_r[:, :], T16, 1), ALU.mult))
            glink(V.tensor_tensor(gf[:, :, :], gf[:, :, :], over(lnb_r[:, :], T16, 1), ALU.add))
            glink(V.reduce_sum(sc[:, :, :], gf[:, :, :].rearrange("p t (h k) -> p t k h", h=HEADS), AX.X))
            glink(V.tensor_scalar(sc[:, :, :], sc[:, :, :], 1.0 / HEADS, None, ALU.mult))
            beaten = gw[:, :, 0:12].rearrange("p t (e f) -> p t e f", e=EXPERTS)
            for f in range(EXPERTS):
                for e in range(f + 1, EXPERTS):
                    V.tensor_tensor(beaten[:, :, e, f], sc[:, :, f], sc[:, :, e], ALU.is_ge)
                    last = V.tensor_tensor(beaten[:, :, f, e - 1], sc[:, :, e], sc[:, :, f], ALU.is_gt)
            glink(last)
            cnt = gf[:, :, 0:EXPERTS]
            glink(V.reduce_sum(cnt, beaten, AX.X))
            glink(V.tensor_scalar(cnt, cnt, 1.5, None, ALU.is_lt))
            glink(V.reduce_max(mean, sc[:, :, :], AX.X))
            V.tensor_tensor(sc[:, :, :], sc[:, :, :], over(mean, [P, TILES, EXPERTS], 2), ALU.subtract).then_inc(s["gates_e"], 1)
            dve.wait_ge(s["gates_exp"], 1)
            glink(V.tensor_tensor(gates[:, :, :], gates[:, :, :], cnt, ALU.mult))
            glink(V.reduce_sum(mean, gates[:, :, :], AX.X))
            glink(V.reciprocal(mean, mean))
            V.tensor_tensor(gates[:, :, :], gates[:, :, :], over(mean, [P, TILES, EXPERTS], 2), ALU.mult).then_inc(s["gates_ready"], 1)
            dve.wait_ge(s["gates_ready"], 1)

            ebank = [bank_T[:, :], bank_A[:, :]]
            with dve.Fori(0, GROUPS, 1) as g:
                for k in range(4):
                    t = 4 * g + k
                    row = xs[:, bass.ds(t, 1), :].squeeze(1)
                    gate = gcol[:, k % 2, :]
                    dve.wait_ge(s["eo_in_psum"], t + 1)
                    V.tensor_copy(gate, gates[:, bass.ds(t, 1), :].squeeze(1)).then_inc(s["comb_chain"], 1)
                    dve.wait_ge(s["comb_chain"], 4 * t + 1)
                    for e in range(EXPERTS):
                        ins = V.scalar_tensor_tensor(row, ebank[k % 2][:, e * D:(e + 1) * D], gate[:, e:e + 1], row, ALU.mult, ALU.add)
                        if e < EXPERTS - 1:
                            ins.then_inc(s["comb_chain"], 1)
                            dve.wait_ge(s["comb_chain"], 4 * t + 2 + e)
                    ins.then_inc(s["eo_used"], 1)


_INS = ["x", "adj", "L0_gnn_epsilon", "L0_gnn_W1", "L0_gnn_b1", "L0_gnn_rms_weight", "L0_gnn_W2", "L0_gnn_b2",
        "L0_ffn_W_gat", "L0_ffn_att_src", "L0_ffn_att_dst", "L0_ffn_b_gat", "L0_ffn_ln_gamma", "L0_ffn_ln_beta",
        "L0_ffn_W1", "L0_ffn_b1", "L0_ffn_W2", "L0_ffn_b2", "L0_ffn_edge_index"]


def kernel(**inputs):
    import numpy as np
    import concourse.bacc as bacc
    from concourse import mybir as mb
    from concourse.bass_utils import run_bass_kernel_spmd

    nc = bacc.Bacc("TRN2", target_bir_lowering=False, num_devices=1)
    arrays, args = {}, []
    for name in _INS:
        a = np.ascontiguousarray(inputs[name])
        if a.ndim == 0:
            a = a.reshape(1)
        arrays[f"in_{name}"] = a
        args.append(nc.dram_tensor(f"in_{name}", a.shape, mb.dt.from_np(a.dtype), kind="ExternalInput").ap())
    args.append(nc.dram_tensor("out_x", (GRAPHS, NODES, D), mb.dt.float32, kind="ExternalOutput").ap())
    build(nc, *args)
    r = run_bass_kernel_spmd(nc, [arrays], core_ids=[0])
    return r.results[0]["out_x"]
```

```python
from contextlib import ExitStack

import concourse.bass as bass
from concourse import mybir

P = 128
GRAPHS, NODES, D = 32, 256, 128
H = 512
M = GRAPHS * NODES
TILES = M // P
EXPERTS, HEADS, F = 4, 4, 256
HK = HEADS * EXPERTS
EDGES = 524288
ECOLS = EDGES // P
ETILES = ECOLS + TILES
ROW = 2 * HEADS + HK
TROW = ROW + 1
OWN = M // P
SEG, KEEP1, REAL1, GROUP2, KEEP2, SENT = 128, 56, 32, 4, 56, 320
CELL = 16
BKEYS = P * CELL
SEG_B, KEEP_B1, GROUP_B2, KEEP_B2, OWNED = 128, 48, 4, 104, 384
CHUNKS = OWNED // P
K_REAL, K_FAR = 2048, 1 << 23
SEND = SENT // GRAPHS
FARCOLS = (ECOLS // SEG) * KEEP1
FSTEP = FARCOLS // GRAPHS
FB = 14
GATHER = 16
ACC = HEADS + HK
LN_EPS, RMS_EPS = 1e-5, 1e-6
LOW = -1e30
HC = H // P
FC = EXPERTS * F // P
GROUP = 512
ARENA = 20800
GROUPS = M // GROUP


def build(nc, x, adj, eps, W1, b1, rms_w, W2, b2, W_gat, att_src, att_dst, b_gat, ln_g, ln_b,
          We1, be1, We2, be2, edges, out):
    fp32, i32, bf16 = mybir.dt.float32, mybir.dt.int32, mybir.dt.bfloat16
    ALU, ACT, AX = mybir.AluOpType, mybir.ActivationFunctionType, mybir.AxisListType
    ctx = ExitStack()
    with ctx:
        def sb(name, shape, dt=fp32):
            return ctx.enter_context(nc.sbuf_tensor("sb_" + name, shape, dt))

        def pb(name, shape, dt=fp32):
            return ctx.enter_context(nc.psum_tensor("ps_" + name, shape, dt))

        def sem(name):
            return ctx.enter_context(nc.semaphore(name))

        table = nc.dram_tensor("table", [M + 1, TROW], fp32, kind="Internal").ap()
        state = nc.dram_tensor("state", [M + 1, ROW], fp32, kind="Internal").ap()

        ident = sb("ident", [P, P])
        ones = sb("ones", [P, P])
        lower = sb("lower", [P, P])
        epsI = sb("epsI", [P, 4 * P])
        eps_c = sb("eps_c", [P, 1])
        w1 = sb("w1", [P, H])
        b1_c = sb("b1_c", [P, HC])
        rms_c = sb("rms_c", [P, HC])
        w2 = sb("w2", [P, HC, D])
        b2_r = sb("b2_r", [P, D])
        wcat = sb("wcat", [P, ROW])
        watt = sb("watt", [P, 2, HK])
        att_r = sb("att_r", [P, 2, HK])
        bgat_r = sb("bgat_r", [P, HK])
        lng_r = sb("lng_r", [P, HK])
        lnb_r = sb("lnb_r", [P, HK])
        we1 = sb("we1", [P, EXPERTS, F])
        be1_c = sb("be1_c", [P, FC])
        we2 = sb("we2", [P, FC, D])
        be2_r = sb("be2_r", [1, EXPERTS * D])
        xs = sb("xs", [P, TILES, D])
        x2nT = sb("x2nT", [P, M])
        bkeys = nc.dram_tensor("bkeys", [P * BKEYS, 1], i32, kind="Internal").ap()
        arena = sb("arena", [P, ARENA])

        def region(at):
            def take(shape, dt=fp32):
                n = 1
                for k in shape:
                    n *= k
                words = n if dt in (fp32, i32) else (n + 1) // 2
                t = arena[:, take.at:take.at + words]
                take.at += words
                assert take.at <= ARENA, take.at
                t = t if dt == fp32 else t.bitcast(dt)
                letters = "abcd"[:len(shape)]
                if len(shape) > 1:
                    t = t.rearrange(f"p ({' '.join(letters)}) -> p {' '.join(letters)}",
                                    **{c: k for c, k in zip(letters[1:], shape[1:])})
                return t
            take.at = at
            return take

        src = x2nT[:, 0:ECOLS].bitcast(i32)
        dst = x2nT[:, ECOLS:2 * ECOLS].bitcast(i32)
        take = region(0)
        far_lo = take([FARCOLS], bf16)
        far_hi = take([FARCOLS], bf16)
        sent = take([SENT])
        where = take([SENT], i32)
        adjs = take([2, 2, NODES])
        shared = take.at
        work = take([3, ECOLS // 4])
        lev1 = take([ECOLS // SEG, KEEP1])
        real1 = take([ECOLS // SEG, REAL1])
        lev2 = take([ECOLS // SEG // GROUP2, KEEP2])
        rank_w = take([4, SENT])
        far_i = take([FARCOLS], i32)
        take = region(shared)
        xn = take([2, 2, D])
        adjT = take([2, 2, NODES])
        aggT = take([2, NODES])
        sq = take([2, HC, NODES])
        rb = take([NODES])
        uu = take([2, HC, NODES])
        ss = take([2, HC, NODES])
        x2n = take([2, 2, D])
        x2nTc = take([2, NODES])
        tb = take([2, 2, ROW])
        hot_lo = take([FSTEP // FB, P, FB], bf16)
        hot_hi = take([FSTEP // FB, OWN, FB], bf16)
        take = region(0)
        terms = take([9, OWNED])
        ow = take([2, HEADS, OWNED])
        assert 2 * CHUNKS * 16 * OWN <= take.at
        own = take([OWNED])
        rows = take([OWNED, TROW])
        idxT = take([OWNED], i32)
        dloT = take([OWNED])
        bi = take([OWNED], i32)
        bw = take([8, OWNED])
        backT = ow.rearrange("p a h n -> p (a h) n")
        hot = region(0)([2, CHUNKS, 16, OWN])
        take = region(0)
        bk = take([BKEYS])
        blev1 = take([BKEYS // SEG_B, KEEP_B1])
        blev2 = take([BKEYS // SEG_B // GROUP_B2 * KEEP_B2 + OWN])
        take = region(0)
        srcs = take([ETILES], i32)
        dsts = take([ETILES], i32)
        take = region(0)
        hh = [take([FC, GROUP]) for _ in range(2)]
        iota_lo = sb("iota_lo", [P, P, FB], bf16)
        iota_hi = sb("iota_hi", [P, OWN, FB], bf16)
        iota_own = sb("iota_own", [P, OWN])
        bzeros = sb("bzeros", [P, 256], i32)
        self_keys = sb("self_keys", [P, OWN], i32)
        place0 = sb("place0", [P, 1])
        far = sb("far", [P, TILES])
        valid_n = sb("valid_n", [P, 4])
        count = sb("count", [P, 4])
        last_node = sb("last_node", [P, TROW])
        stage_k = sb("stage_k", [P, 2, SEND], i32)
        stage_w = sb("stage_w", [P, 2, SEND], i32)
        stage_i = sb("stage_i", [P, 2, GATHER], i32)
        stage_r = sb("stage_r", [P, 2, GATHER, TROW])
        odd = sb("odd", [OWN, TILES, ROW])
        redo = sb("redo", [P, 1], i32)
        zero2 = sb("zero2", [P, 1])
        st = sb("st", [P, 2, 6])
        mv = sb("mv", [P, 2, 2, 2])
        var = sb("var", [P, 6])
        root = sb("root", [P, 6])
        nhalf = sb("nhalf", [P, 6])
        newt = sb("newt", [P, 6])
        st2 = sb("st2", [P, 2, 6])
        mv2 = sb("mv2", [P, 2, 2, 2])
        idx = sb("idx", [P, 2], i32)
        zrow = sb("zrow", [P, TROW])
        st0 = sb("st0", [P, ROW])
        dstf = sb("dstf", [P, 1])
        srow = sb("srow", [P, TROW])
        drow = sb("drow", [P, TROW])
        strow = sb("strow", [P, ROW])
        newrow = sb("newrow", [P, ROW])
        eq = sb("eq", [P, P])
        pen = sb("pen", [P, P])
        masked = sb("masked", [P, HEADS, P])
        small = sb("small", [P, 8, HEADS])
        vals = sb("vals", [P, ACC])
        lead = sb("lead", [P, 4])
        sidx = sb("sidx", [P, 1], i32)
        agg = sb("agg", [P, TILES, ROW])
        gf = sb("gf", [P, TILES, HK])
        gw = sb("gw", [P, TILES, HK])
        gs = sb("gs", [P, 5, TILES])
        sc = sb("sc", [P, TILES, EXPERTS])
        gates = sb("gates", [P, TILES, EXPERTS])
        gcol = sb("gcol", [P, 2, EXPERTS])

        bank_T = pb("T", [P, 512])
        bank_A = pb("A", [P, 512])
        ps_H = pb("H", [P, 2, HC, NODES])
        bank_O = pb("O", [P, 512])
        bank_S = pb("S", [P, 512])
        ps_T = bank_T[:, :].rearrange("p (m n) -> p m n", m=2)
        ps_A, ps_Q, ps_F = bank_A[:, 0:NODES], bank_A[:, NODES:NODES + 2], bank_A[:, 320:320 + TILES]
        ps_O = bank_O[:, 0:2 * D].rearrange("p (u d) -> p u d", u=2)
        ps_B = bank_O[:, 2 * D:2 * D + 2 * ROW]
        ps_R, ps_X = bank_S[:, 0:NODES], bank_S[:, NODES:2 * NODES]
        halfH = [ps_H[:, k, 2 * j:2 * j + 2, :].rearrange("p a b -> p (a b)") for k in range(2) for j in range(2)]

        banks = [bank_T[:, :], bank_A[:, :]] + halfH + [bank_O[:, :], bank_S[:, :]]

        names = ["src_loaded", "prep", "sorted_", "far_ready", "sent_ready", "bzero", "iotas", "hot_built", "far_in_psum",
                 "far_added", "far_stored", "bk_loaded", "own_prep", "own_ready", "idx_in_psum", "idx_done", "last_loaded",
                 "terms_in_psum", "terms_ready", "own_math", "exp_in", "exp_done", "back_ready", "back_in_psum", "backT_ready",
                 "vals_made", "hots_built", "agg_in_psum", "agg_out", "odd_moved", "agg_fin", "diff_ready", "total_in_psum",
                 "redo_ready", "staged_k", "staged_i", "rows_moved", "bk_clear", "xn_ready", "adjT_in_psum", "adjT_ready", "aggT_in_psum", "aggT_ready",
                 "h_in_psum", "sq_ready", "ss_in_psum", "u_ready", "s_ready", "o_in_psum", "x1_ready",
                 "x2n_ready", "x2nT_in_psum", "x2nT_ready", "tb_in_psum", "tb_ready", "weights", "ld_gat",
                 "const_a", "const_b", "gat_w", "wcat_ready", "state_init", "pool_const",
                 "edges_loaded", "edges_ready", "zero2_done",  "idx_ready", "dstf_ready", "eq_ready", "as_in_psum",
                 "mnew_ready", "ee_in", "ee_ready", "vals_ready", "sum_in_psum", "newrow_ready",
                 "setup_chain", "edge_chain", "gate_chain", "comb_chain", "ln1_stats", "ln1_mv", "ln2_stats", "ln2_mv", "x_b2", "ms_ready", "newton", "root_ready", "rb_in_psum", "rb_ready", "gate_newton", "agg_in",
                 "gates_e", "gates_exp", "gates_ready", "hh_in_psum", "hh_ready", "eo_in_psum", "eo_used",
                 "iota_done", "zero_done", "sig_done"]
        s = {n: sem(n) for n in names}
        x_loaded = [sem(f"x_loaded{p}") for p in range(2)]
        adj_loaded = [sem(f"adj_loaded{p}") for p in range(2)]
        scattered = [sem(f"scattered{p}") for p in range(2)]
        gathered = [sem(f"gathered{p}") for p in range(2)]
        tb_stored = [sem(f"tb_stored{p}") for p in range(2)]
        src_in, dst_in, state_in, row_stored = ([sem(f"{n}{p}") for p in range(2)]
                                                for n in ("src_in", "dst_in", "state_in", "row_stored"))
        out_stored = [sem(f"out_stored{p}") for p in range(2)]

        x_t = x.rearrange("g (u q) d -> g q u d", q=P)
        adj_t = adj.rearrange("g (u q) m -> g q u m", q=P)
        out_t = out.rearrange("g (u q) d -> g q u d", q=P)
        tab_t = table[0:M, 0:ROW].rearrange("(g u q) c -> g q u c", u=2, q=P)

        FIRST, LOOP_FROM, LOOP_TO, END = -2, 6, GRAPHS - 2, GRAPHS + 5

        def piped(eng, step):
            for i in range(FIRST, LOOP_FROM):
                step(i, i % 2)
            with eng.Fori(LOOP_FROM // 2, LOOP_TO // 2) as j:
                step(2 * j, 0)
                step(2 * j + 1, 1)
            for i in range(LOOP_TO, END):
                step(i, i % 2)

        def on(i, lag):
            return not isinstance(i, int) or 0 <= i - lag < GRAPHS

        def some(eng, semaphore, value, most=GRAPHS):
            if not isinstance(value, int):
                eng.wait_ge(semaphore, value)
            elif value > 0:
                eng.wait_ge(semaphore, value if most is None else min(value, most))

        def alone(eng):
            eng.wait_ge(s["pool_const"], 2)

        def half(i, p):
            return (i - p) // 2 if isinstance(i, int) else (i - p) >> 1

        block = ctx.enter_context(nc.Block())

        @block.sync
        def _(sp):
            sp.dma_start(src, edges[0, :].rearrange("(p c) -> p c", p=P)).then_inc(s["src_loaded"], 16)
            sp.dma_start(dst, edges[1, :].rearrange("(p c) -> p c", p=P)).then_inc(s["src_loaded"], 16)
            n = 0
            for to, of in (
                (w1[:, :], W1), (b1_c[:, :], b1.rearrange("(c p) -> p c", p=P)),
                (rms_c[:, :], rms_w.rearrange("(c p) -> p c", p=P)),
                (w2[:, :, :], W2.rearrange("(c p) d -> p c d", p=P)),
                (b2_r[:, :], b2[None, :].to_broadcast([P, D])),
                (eps_c[:, :], eps[None, :].to_broadcast([P, 1])),
                (we1[:, :, :], We1.rearrange("e d f -> d e f")),
                (be1_c[:, :], be1.rearrange("e (c p) -> p (e c)", p=P)),
                (we2[:, :, :], We2.rearrange("e (c p) d -> p (e c) d", p=P)),
                (be2_r[:, :], be2.rearrange("e d -> (e d)")[None, :]),
                (wcat[:, 2 * HEADS:ROW], W_gat),
                (att_r[:, 0, :], att_src.rearrange("h k -> (h k)")[None, :].to_broadcast([P, HK])),
                (att_r[:, 1, :], att_dst.rearrange("h k -> (h k)")[None, :].to_broadcast([P, HK])),
                (bgat_r[:, :], b_gat[None, :].to_broadcast([P, HK])),
                (lng_r[:, :], ln_g[None, :].to_broadcast([P, HK])),
                (lnb_r[:, :], ln_b[None, :].to_broadcast([P, HK])),
            ):
                with nc.allow_non_contiguous_dma(reason="small constants"):
                    sp.dma_start(to, of).then_inc(s["weights"], 16)
                n += 1
            assert n == 16
            sp.wait_ge(s["bk_clear"], 1)
            for k in range(8):
                sp.dma_start(bkeys.rearrange("(p c) one -> p (c one)", p=P)[:, k * 256:(k + 1) * 256], bzeros[:, :]).then_inc(s["bzero"], 16)

            def step(i, p):
                q = 1 - p
                if on(i, -2):
                    some(sp, x_loaded[p], 16 * half(i + 2, p), None)
                    sp.dma_start(xs[:, bass.ds(2 * (i + 2), 2), :], x_t[bass.ds(i + 2, 1), :, :, :][0]).then_inc(x_loaded[p], 16)
                if on(i, -1):
                    some(sp, s["adjT_in_psum"], i)
                    sp.dma_start(adjs[:, q, :, :], adj_t[bass.ds(i + 1, 1), :, :, :][0]).then_inc(adj_loaded[q], 16)
                if on(i, 5):
                    sp.wait_ge(s["tb_ready"], i - 4)
                    sp.dma_start(tab_t[bass.ds(i - 5, 1), :, :, :][0], tb[:, q, :, :]).then_inc(tb_stored[q], 16)

            piped(sp, step)

            sp.wait_ge(s["far_added"], GRAPHS)
            with nc.allow_non_contiguous_dma(reason="one column of the table"):
                sp.dma_start(table[0:M, ROW:TROW].rearrange("(t q) c -> q t c", q=P), far[:, :].unsqueeze(2)).then_inc(s["far_stored"], 16)
            for p in range(2):
                sp.wait_ge(scattered[p], 16 * SENT // 2)
            sp.dma_start(bk, bkeys.rearrange("(p c) one -> p (c one)", p=P).bitcast(fp32)).then_inc(s["bk_loaded"], 16)
            for p in range(2):
                sp.wait_ge(tb_stored[p], 16 * GRAPHS // 2)
            sp.wait_ge(s["far_stored"], 16)
            sp.dma_start(last_node[:, :], table[M - 1:M, :].to_broadcast([P, TROW])).then_inc(s["last_loaded"], 16)
            sp.wait_ge(s["agg_out"], 8)
            sp.dma_start(agg[OWN:P, :, :], odd[:, :, :]).then_inc(s["odd_moved"], 16)

            sp.wait_ge(s["redo_ready"], 1)
            again = sp.value_load(redo[0:1, 0:1], min_val=0, max_val=1)
            with sp.If(again > 0):
                sp.wait_ge(s["zero2_done"], 1)
                sp.dma_start(srcs[:, 0:ECOLS], edges[0, :].rearrange("(p c) -> p c", p=P)).then_inc(s["edges_loaded"], 16)
                sp.dma_start(dsts[:, 0:ECOLS], edges[1, :].rearrange("(p c) -> p c", p=P)).then_inc(s["edges_loaded"], 16)
                sp.dma_start(table[M:M + 1, :], zrow[0:1, :]).then_inc(s["state_init"], 16)
                sp.dma_start(state[M:M + 1, :], st0[0:1, :]).then_inc(s["state_init"], 16)
                for t in range(TILES):
                    sp.dma_start(state[t * P:(t + 1) * P, :], st0[:, :]).then_inc(s["state_init"], 16)
                for p in range(2):
                    sp.wait_ge(row_stored[p], 16 * ETILES // 2)
                sp.dma_start(agg[:, :, :], state[0:M, :].rearrange("(t q) c -> q t c", q=P)).then_inc(s["agg_in"], 16)

            def estore(g, p):
                sp.wait_ge(s["eo_used"], 4 * g + 4)
                sp.dma_start(out_t[bass.ds(2 * g, 2), :, :, :].rearrange("g q u d -> q g u d"),
                             xs[:, bass.ds(4 * g, 4), :].rearrange("q (g u) d -> q g u d", g=2)).then_inc(out_stored[p], 16)

            with sp.Fori(0, GROUPS // 2) as j:
                estore(2 * j, 0)
                estore(2 * j + 1, 1)
            for p in range(2):
                sp.wait_ge(out_stored[p], 16 * GROUPS // 2)
                sp.wait_ge(tb_stored[p], 16 * GRAPHS // 2)

        @block.gpsimd
        def _(pool):
            pool.memset(ident[:, :], 0.0).then_inc(s["const_a"], 1)
            pool.memset(ones[:, :], 1.0).then_inc(s["const_a"], 1)
            pool.wait_ge(s["const_a"], 2)
            pool.affine_select(out=ident[:, :], in_=ident[:, :], compare_op=ALU.not_equal, fill=1.0,
                               base=0, pattern=[[-1, P]], channel_multiplier=1).then_inc(s["pool_const"], 1)
            pool.affine_select(out=lower[:, :], in_=ones[:, :], compare_op=ALU.is_gt, fill=0.0,
                               base=0, pattern=[[-1, P]], channel_multiplier=1).then_inc(s["pool_const"], 1)
            pool.memset(zrow[:, :], 0.0).then_inc(s["zero_done"], 1)
            pool.memset(st0[:, 0:HEADS], LOW).then_inc(s["zero_done"], 1)
            pool.memset(st0[:, HEADS:ROW], 0.0).then_inc(s["zero_done"], 1)
            pool.memset(bzeros[:, :], 0).then_inc(s["bk_clear"], 1)
            pool.iota(iota_lo[:, :, :], pattern=[[1, P], [0, FB]], base=0, channel_multiplier=0, allow_small_or_imprecise_dtypes=True).then_inc(s["iotas"], 1)
            pool.iota(iota_hi[:, :, :], pattern=[[1, OWN], [0, FB]], base=0, channel_multiplier=0, allow_small_or_imprecise_dtypes=True).then_inc(s["iotas"], 1)
            pool.iota(iota_own[:, :], pattern=[[1, OWN]], base=0, channel_multiplier=0, allow_small_or_imprecise_dtypes=True).then_inc(s["iotas"], 1)
            pool.iota(place0[:, :], pattern=[[0, 1]], base=0, channel_multiplier=CELL, allow_small_or_imprecise_dtypes=True).then_inc(s["iotas"], 1)
            pool.iota(self_keys[:, :], pattern=[[1 << 13, OWN]], base=(K_REAL << 13) + M - 1, channel_multiplier=OWN << 13).then_inc(s["iotas"], 1)

            last_place = pool.to_reg(P * BKEYS - 1)
            pool.wait_ge(s["sent_ready"], 1)
            pool.wait_ge(s["bzero"], 8 * 16)

            def send(j, p, n):
                if not isinstance(n, int):
                    pool.wait_ge(scattered[p], 16 * SEND * n)
                pool.tensor_copy(stage_k[:, p, :], sent.bitcast(i32)[:, bass.ds(j * SEND, SEND)]).then_inc(s["staged_k"], 1)
                pool.tensor_copy(stage_w[:, p, :], where[:, bass.ds(j * SEND, SEND)]).then_inc(s["staged_k"], 1)
                both = pool.to_reg(2 * j + 2)
                alone(pool)
                pool.wait_ge(s["staged_k"], both)
                for c in range(SEND):
                    pool.indirect_dma_start(bkeys, bass.IndirectOffsetOnAxis(ap=stage_w[:, p, c:c + 1], axis=0), stage_k[:, p, c:c + 1], None,
                                            bounds_check=last_place, oob_is_err=False).then_inc(scattered[p], 16)

            send(0, 0, 0)
            send(1, 1, 0)
            with pool.Fori(1, SENT // SEND // 2) as j:
                send(2 * j, 0, j)
                send(2 * j + 1, 1, j)

            last_source = pool.to_reg(M - 1)
            pool.wait_ge(s["idx_done"], 1)
            for p in range(2):
                pool.wait_ge(tb_stored[p], 16 * GRAPHS // 2)
            pool.wait_ge(s["far_stored"], 16)

            def fetch(j, p, n):
                pool.tensor_copy(stage_i[:, p, :], idxT[:, bass.ds(j * GATHER, GATHER)]).then_inc(s["staged_i"], 1)
                one = pool.to_reg(j + 1)
                alone(pool)
                pool.wait_ge(s["staged_i"], one)
                for c in range(GATHER):
                    pool.indirect_dma_start(stage_r[:, p, c, :], None, table[0:M, :], bass.IndirectOffsetOnAxis(ap=stage_i[:, p, c:c + 1], axis=0),
                                            bounds_check=last_source, oob_is_err=False).then_inc(gathered[p], 16)

            def move(j, p, n):
                pool.wait_ge(gathered[p], 16 * GATHER * (n + 1))
                pool.tensor_copy(rows[:, bass.ds(j * GATHER, GATHER), :], stage_r[:, p, :, :]).then_inc(s["rows_moved"], 1)
                pool.wait_ge(s["rows_moved"], j + 1)

            fetch(0, 0, 0)
            fetch(1, 1, 0)
            with pool.Fori(1, OWNED // GATHER // 2) as j:
                move(2 * j - 2, 0, j - 1)
                fetch(2 * j, 0, j)
                move(2 * j - 1, 1, j - 1)
                fetch(2 * j + 1, 1, j)
            move(OWNED // GATHER - 2, 0, OWNED // GATHER // 2 - 1)
            move(OWNED // GATHER - 1, 1, OWNED // GATHER // 2 - 1)

            pool.wait_ge(s["redo_ready"], 1)
            again = pool.value_load(redo[0:1, 0:1], min_val=0, max_val=1)
            with pool.If(again > 0):
                pool.iota(srcs[:, ECOLS:ETILES], pattern=[[P, TILES]], base=0, channel_multiplier=1).then_inc(s["iota_done"], 1)
                pool.iota(dsts[:, ECOLS:ETILES], pattern=[[P, TILES]], base=0, channel_multiplier=1).then_inc(s["iota_done"], 1)
                pool.wait_ge(s["state_init"], 16 * (TILES + 2))
                last_row = pool.to_reg(M)
                def gather(rows, source, column, signal):
                    pool.indirect_dma_start(rows[:, :], None, source, bass.IndirectOffsetOnAxis(ap=idx[:, column:column + 1], axis=0),
                                            bounds_check=last_row, oob_is_err=False).then_inc(signal, 16)

                def edge_tile(t, p):
                    done, indices = pool.to_reg(t + 1), pool.to_reg(2 * t + 2)
                    alone(pool)
                    pool.wait_ge(s["idx_ready"], indices)
                    gather(srow, table, 0, src_in[p])
                    gather(drow, table, 1, dst_in[p])
                    gather(strow, state, 1, state_in[p])
                    alone(pool)
                    pool.wait_ge(s["newrow_ready"], done)
                    pool.indirect_dma_start(state, bass.IndirectOffsetOnAxis(ap=sidx[:, 0:1], axis=0), newrow[:, :], None,
                                            bounds_check=last_row, oob_is_err=False).then_inc(row_stored[p], 16)

                with pool.Fori(0, ETILES // 2) as j:
                    edge_tile(2 * j, 0)
                    edge_tile(2 * j + 1, 1)

        @block.tensor
        def _(pe):
            pe.wait_ge(s["pool_const"], 2)
            pe.wait_ge(s["weights"], 16 * 16)

            def step(i, p):
                q = 1 - p
                if on(i, 0):
                    pe.wait_ge(adj_loaded[p], 16 * half(i, p) + 16)
                    some(pe, s["adjT_ready"], i)
                    for nt in range(2):
                        for mt in range(2):
                            last = nc.tensor.transpose(ps_T[:, mt, nt * P:(nt + 1) * P],
                                                       adjs[:, p, nt, mt * P:(mt + 1) * P], ident[:, :])
                    last.then_inc(s["adjT_in_psum"], 1)
                if on(i, 2):
                    pe.wait_ge(s["root_ready"], i + 2)
                    some(pe, s["x2nT_ready"], i - 4)
                    some(pe, s["rb_ready"], i - 2)
                    for u in range(2):
                        last = nc.tensor.matmul(ps_R[:, u * P:(u + 1) * P], root[:, 2 + u:3 + u].to_broadcast([P, P]),
                                                ident[:, :], start=True, stop=True)
                    last.then_inc(s["rb_in_psum"], 1)
                if on(i, 5):
                    pe.wait_ge(s["x2nT_ready"], i - 4)
                    pe.wait_ge(s["wcat_ready"], 2)
                    some(pe, s["tb_ready"], i - 5)
                    some(pe, s["x1_ready"], i - 3)
                    for u in range(2):
                        last = nc.tensor.matmul(ps_B[:, u * ROW:(u + 1) * ROW],
                                                x2nTc[:, q, u * P:(u + 1) * P], wcat[:, :], start=True, stop=True)
                    last.then_inc(s["tb_in_psum"], 1)
                if on(i, 4):
                    pe.wait_ge(s["x2n_ready"], i - 3)
                    some(pe, s["x2nT_ready"], i - 4)
                    for u in range(2):
                        last = nc.tensor.transpose(ps_X[:, u * P:(u + 1) * P], x2n[:, p, u, :], ident[:, :])
                    last.then_inc(s["x2nT_in_psum"], 1)
                if on(i, 1):
                    pe.wait_ge(s["aggT_ready"], i)
                    some(pe, s["u_ready"], i - 2)
                    for c in range(HC):
                        last = nc.tensor.matmul(ps_H[:, q, c, :], w1[:, c * P:(c + 1) * P], aggT[:, q, :], start=True, stop=True)
                    last.then_inc(s["h_in_psum"], 1)
                if on(i, 0):
                    pe.wait_ge(s["xn_ready"], i + 1)
                    pe.wait_ge(s["adjT_ready"], i + 1)
                    some(pe, s["far_added"], i)
                    some(pe, s["aggT_ready"], i)
                    some(pe, s["ms_ready"], i + 3, None)
                    for mt in range(2):
                        last = nc.tensor.matmul(ps_A, xn[:, p, mt, :], adjT[:, p, mt, :],
                                                start=(mt == 0), stop=(mt == 1))
                    last.then_inc(s["aggT_in_psum"], 1)
                if on(i, 3):
                    pe.wait_ge(s["s_ready"], i - 2)
                    some(pe, s["x1_ready"], i - 3)
                    some(pe, s["tb_ready"], i - 4)
                    for nt in range(2):
                        for c in range(HC):
                            last = nc.tensor.matmul(ps_O[:, nt, :], ss[:, q, c, nt * P:(nt + 1) * P], w2[:, c, :],
                                                    start=(c == 0), stop=(c == HC - 1))
                    last.then_inc(s["o_in_psum"], 1)
                if on(i, 0):
                    pe.wait_ge(s["hot_built"], i + 1)
                    some(pe, s["ms_ready"], i + 3, None)
                    some(pe, s["aggT_ready"], i + 1)
                    for c in range(FSTEP):
                        last = nc.tensor.matmul(ps_F, hot_lo[:, c // FB, :, c % FB], hot_hi[:, c // FB, :, c % FB],
                                                start=(c == 0), stop=(c == FSTEP - 1))
                    last.then_inc(s["far_in_psum"], 1)
                if on(i, 1):
                    pe.wait_ge(s["sq_ready"], i)
                    some(pe, s["ms_ready"], i + 3, None)
                    some(pe, s["aggT_ready"], i + 1)
                    for u in range(2):
                        for c in range(HC):
                            last = nc.tensor.matmul(ps_Q[:, u:u + 1], sq[:, q, c, u * P:(u + 1) * P], ones[:, 0:1],
                                                    start=(c == 0), stop=(c == HC - 1))
                    last.then_inc(s["ss_in_psum"], 1)

            piped(pe, step)

            pe.wait_ge(s["own_ready"], 1)
            for k in range(2):
                for c in range(CHUNKS):
                    last = nc.tensor.transpose(halfH[k][:, c * P:(c + 1) * P], bw[:, k, c * P:(c + 1) * P], ident[:, :])
            last.then_inc(s["idx_in_psum"], 1)
            pe.wait_ge(s["rows_moved"], OWNED // GATHER)
            pe.wait_ge(s["idx_done"], 1)
            cols = list(range(2 * HEADS)) + [ROW]
            for n, col in enumerate(cols):
                if n >= 8:
                    pe.wait_ge(s["terms_ready"], n - 7)
                for c in range(CHUNKS):
                    last = nc.tensor.transpose(banks[n % 8][:, c * P:(c + 1) * P], rows[:, c * P:(c + 1) * P, col], ident[:, :])
                last.then_inc(s["terms_in_psum"], 1)
            for k in range(2 * HEADS):
                pe.wait_ge(s["back_ready"], 1)
                pe.wait_ge(s["terms_ready"], 9)
                wt = terms[:, k, :]
                for c in range(CHUNKS):
                    last = nc.tensor.transpose(banks[k][:, c * P:(c + 1) * P], wt[:, c * P:(c + 1) * P], ident[:, :])
                last.then_inc(s["back_in_psum"], 1)
            pe.wait_ge(s["vals_made"], 1)
            for k in range(8):
                pe.wait_ge(s["hots_built"], k + 1)
                for b in range(16):
                    for c in range(CHUNKS):
                        last = nc.tensor.matmul(banks[k][0:OWN, b * ROW:(b + 1) * ROW], hot[:, k % 2, c, b, :],
                                                rows[:, c * P + 16 * k + b, 0:ROW], start=(c == 0), stop=(c == CHUNKS - 1))
                last.then_inc(s["agg_in_psum"], 1)
            pe.wait_ge(s["diff_ready"], 1)
            nc.tensor.matmul(banks[0][:, 0:1], ones[:, :], count[:, 3:4], start=True, stop=True).then_inc(s["total_in_psum"], 1)

            pe.wait_ge(s["redo_ready"], 1)
            again = pe.value_load(redo[0:1, 0:1], min_val=0, max_val=1)
            with pe.If(again > 0):
                def edge_tile(t, p, j):
                    pe.wait_ge(s["dstf_ready"], t + 1)
                    pe.wait_ge(src_in[p], 16 * j + 16)
                    nc.tensor.matmul(bank_T[:, 0:P], dstf[:, 0:1].to_broadcast([P, P]), ident[:, :], start=True, stop=True)
                    for h in range(HEADS):
                        last = nc.tensor.matmul(halfH[0][:, h * P:(h + 1) * P], srow[:, h:h + 1].to_broadcast([P, P]),
                                                ident[:, :], start=True, stop=True)
                    last.then_inc(s["as_in_psum"], 1)
                    pe.wait_ge(s["vals_ready"], t + 1)
                    nc.tensor.matmul(bank_S[:, 0:ACC], eq[:, :], vals[:, :], start=True, stop=True).then_inc(s["sum_in_psum"], 1)

                with pe.Fori(0, ETILES // 2) as j:
                    edge_tile(2 * j, 0, j)
                    edge_tile(2 * j + 1, 1, j)

            bank = halfH
            obank = [bank_T[:, :], bank_A[:, :]]
            pe.wait_ge(s["gates_ready"], 1)

            def experts(g, p, outs):
                for c in range(FC):
                    if not isinstance(g, int) or g < GROUPS:
                        some(pe, s["hh_ready"], 8 * g + c - 3, None)
                        nc.tensor.matmul(bank[c % 4], we1[:, c // 2, (c % 2) * P:(c % 2) * P + P],
                                         x2nT[:, bass.ds(g * GROUP, GROUP)], start=True, stop=True).then_inc(s["hh_in_psum"], 1)
                    if outs and c % 2:
                        k = c // 2
                        pe.wait_ge(s["hh_ready"], 8 * g)
                        some(pe, s["eo_used"], 4 * (g - 1) + k - 1, None)
                        nc.tensor.matmul(obank[k % 2], ones[0:1, :], be2_r[:, :], start=True, stop=False)
                        for j in range(FC):
                            last = nc.tensor.matmul(obank[k % 2][:, (j // 2) * D:(j // 2 + 1) * D],
                                                    hh[1 - p][:, j, k * P:(k + 1) * P], we2[:, j, :],
                                                    start=False, stop=(j == FC - 1))
                        last.then_inc(s["eo_in_psum"], 1)

            experts(0, 0, False)
            experts(1, 1, True)
            with pe.Fori(1, GROUPS // 2) as j:
                experts(2 * j, 0, True)
                experts(2 * j + 1, 1, True)
            experts(GROUPS, 0, True)

        @block.scalar
        def _(act):
            act.wait_ge(s["weights"], 16 * 16)
            act.wait_ge(s["pool_const"], 2)

            def step(i, p):
                q = 1 - p
                if on(i, 2):
                    act.wait_ge(s["rb_in_psum"], i - 1)
                    some(act, s["x2nT_in_psum"], i - 3)
                    some(act, s["u_ready"], i - 2)
                    nc.scalar.activation(rb[:, :], ps_R, ACT.Identity).then_inc(s["rb_ready"], 1)
                if on(i, 4):
                    act.wait_ge(s["x2nT_in_psum"], i - 3)
                    some(act, s["tb_in_psum"], i - 5)
                    nc.scalar.activation(x2nTc[:, p, :], ps_X, ACT.Identity)
                    nc.scalar.activation(x2nT[:, bass.ds((i - 4) * NODES, NODES)], ps_X,
                                         ACT.Identity).then_inc(s["x2nT_ready"], 1)
                if on(i, 1):
                    act.wait_ge(s["h_in_psum"], i)
                    some(act, s["ss_in_psum"], i - 2)
                    for c in range(HC):
                        last = nc.scalar.activation(sq[:, q, c, :], ps_H[:, q, c, :], ACT.Square, bias=b1_c[:, c:c + 1])
                    last.then_inc(s["sq_ready"], 1)
                if on(i, 2):
                    act.wait_ge(s["u_ready"], i - 1)
                    some(act, s["o_in_psum"], i - 3)
                    for c in range(HC):
                        last = nc.scalar.activation(ss[:, p, c, :], uu[:, p, c, :], ACT.Silu, scale=rms_c[:, c:c + 1])
                    last.then_inc(s["s_ready"], 1)

            piped(act, step)

            for n in range(9):
                act.wait_ge(s["terms_in_psum"], n + 1)
                nc.scalar.activation(terms[:, n, :], banks[n % 8][:, 0:OWNED], ACT.Identity).then_inc(s["terms_ready"], 1)
            act.wait_ge(s["exp_in"], 1)
            nc.scalar.activation(terms[:, 0:8, :], terms[:, 0:8, :], ACT.Exp).then_inc(s["exp_done"], 1)
            for k in range(2 * HEADS):
                act.wait_ge(s["back_in_psum"], k + 1)
                nc.scalar.activation(backT[:, k, :], banks[k][:, 0:OWNED], ACT.Identity).then_inc(s["backT_ready"], 1)

            act.wait_ge(s["redo_ready"], 1)
            again = act.value_load(redo[0:1, 0:1], min_val=0, max_val=1)
            with act.If(again > 0):
                with act.Fori(0, ETILES) as t:
                    act.wait_ge(s["mnew_ready"], t + 1)
                    nc.scalar.activation(small[:, 4:6, :], small[:, 2:4, :], ACT.Exp).then_inc(s["ee_ready"], 1)

            act.wait_ge(s["gates_e"], 1)
            nc.scalar.activation(gates[:, :, :], sc[:, :, :], ACT.Exp).then_inc(s["gates_exp"], 1)

            bank = halfH

            def experts(g, p):
                some(act, s["eo_in_psum"], 4 * g - 4, None)
                for c in range(FC):
                    act.wait_ge(s["hh_in_psum"], 8 * g + c + 1)
                    nc.scalar.activation(hh[p][:, c, :], bank[c % 4], ACT.Gelu, bias=be1_c[:, c:c + 1]).then_inc(s["hh_ready"], 1)

            experts(0, 0)
            experts(1, 1)
            with act.Fori(1, GROUPS // 2) as j:
                experts(2 * j, 0)
                experts(2 * j + 1, 1)

        @block.vector
        def _(dve):
            V = nc.vector
            setup = [0]

            def link1(ins):
                setup[0] += 1
                ins.then_inc(s["setup_chain"], 1)
                dve.wait_ge(s["setup_chain"], setup[0])

            dve.wait_ge(s["weights"], 16 * 16)
            dve.wait_ge(s["pool_const"], 2)
            link1(V.memset(epsI[:, :], 0.0))
            for k in (0, 3):
                link1(V.tensor_scalar(epsI[:, k * P:(k + 1) * P], ident[:, :], eps_c[:, 0:1], None, ALU.mult))
            for k in range(2):
                link1(V.tensor_tensor(watt[:, k, :], wcat[:, 2 * HEADS:ROW], att_r[:, k, :], ALU.mult))
                V.reduce_sum(wcat[:, k * HEADS:(k + 1) * HEADS],
                             watt[:, k, :].rearrange("p (h k) -> p h k", h=HEADS), AX.X).then_inc(s["wcat_ready"], 1)
            link1(V.memset(var[:, :], 1.0))
            prep_n = [0]

            def plink(ins):
                prep_n[0] += 1
                ins.then_inc(s["prep"], 1)
                dve.wait_ge(s["prep"], prep_n[0])

            dve.wait_ge(s["src_loaded"], 32)
            w = [work[:, k, :] for k in range(3)]
            for c in range(4):
                sc_, dc = (m[:, c * ECOLS // 4:(c + 1) * ECOLS // 4] for m in (src, dst))
                plink(V.tensor_scalar(w[0], dc, float(M), None, ALU.is_lt))
                V.reduce_sum(valid_n[:, c:c + 1], w[0], AX.X)
                plink(V.scalar_tensor_tensor(w[1], sc_, float(M - 1), w[0], ALU.is_lt, ALU.mult))
                plink(V.tensor_tensor(w[2], w[0], w[1], ALU.subtract))
                plink(V.scalar_tensor_tensor(w[2], dc, float(K_FAR), w[2], ALU.add, ALU.mult))
                plink(V.tensor_tensor(w[0], sc_, w[1], ALU.mult))
                plink(V.tensor_tensor(w[2].bitcast(i32), w[2], w[0], ALU.add))
                plink(V.scalar_tensor_tensor(dc, dc, float(K_REAL), w[1], ALU.add, ALU.mult))
                plink(V.scalar_tensor_tensor(sc_, dc, 13, w[2].bitcast(i32), ALU.logical_shift_left, ALU.bitwise_or))

            sorts = [0]

            def top(sources, outs, passes):
                for n in range(passes):
                    marks = []
                    for x_, o in zip(sources, outs):
                        V.max(o[:, 8 * n:8 * n + 8], x_).then_inc(s["sorted_"], 1)
                        sorts[0] += 1
                        marks.append(sorts[0])
                    for x_, o, mark in zip(sources, outs, marks):
                        dve.wait_ge(s["sorted_"], mark)
                        V.match_replace(x_, o[:, 8 * n:8 * n + 8], x_, 0.0).then_inc(s["sorted_"], 1)
                        sorts[0] += 1
                    dve.wait_ge(s["sorted_"], sorts[0])

            keys = src.bitcast(fp32).rearrange("p (g n) -> p g n", n=SEG)
            for g in range(0, ECOLS // SEG, 4):
                top([keys[:, g + u, :] for u in range(4)], [lev1[:, g + u, :] for u in range(4)], KEEP1 // 8)
            first_real = 2.0 ** -125
            assert K_REAL << 13 == 1 << 24
            plink(V.scalar_tensor_tensor(real1, lev1[:, :, 0:REAL1], first_real, lev1[:, :, 0:REAL1], ALU.is_ge, ALU.mult))
            for g in range(0, 8, 4):
                top([real1[:, GROUP2 * (g + u):GROUP2 * (g + u + 1), :].rearrange("p a b -> p (a b)") for u in range(4)],
                    [lev2[:, g + u, :] for u in range(4)], KEEP2 // 8)
            top([lev2.rearrange("p a b -> p (a b)")], [sent], SENT // 8)
            owner, same, rank, bad = (rank_w[:, k, :] for k in range(4))
            plink(V.tensor_scalar(where, sent.bitcast(i32), 19, None, ALU.logical_shift_right))
            plink(V.tensor_scalar(owner, where, -float(K_REAL // OWN), None, ALU.add))
            V.memset(same[:, 0:1], 0.0)
            plink(V.tensor_tensor(same[:, 1:SENT], owner[:, 1:SENT], owner[:, 0:SENT - 1], ALU.is_equal))
            plink(V.tensor_tensor_scan(rank, same, same, 0.0, ALU.mult, ALU.add))
            plink(V.tensor_scalar(bad, rank, CELL - 0.5, float(1 << 22), ALU.is_gt, ALU.mult))
            plink(V.tensor_tensor(rank, rank, bad, ALU.add))
            plink(V.tensor_scalar(bad, owner, 0.0, float(1 << 22), ALU.is_lt, ALU.mult))
            plink(V.tensor_tensor(rank, rank, bad, ALU.add))
            dve.wait_ge(s["iotas"], 5)
            plink(V.scalar_tensor_tensor(rank, owner, float(BKEYS), rank, ALU.mult, ALU.add))
            V.tensor_scalar(where, rank, place0[:, 0:1], None, ALU.add).then_inc(s["sent_ready"], 1)
            k1 = lev1.rearrange("p a b -> p (a b)").bitcast(i32)
            plink(V.tensor_scalar(far_i, k1, P - 1, None, ALU.bitwise_and))
            plink(V.tensor_copy(far_lo, far_i))
            plink(V.tensor_scalar(far_i, k1, 7, None, ALU.logical_shift_right))
            plink(V.tensor_scalar(far_hi, far_i, -float(K_FAR >> 7), None, ALU.add))
            plink(V.memset(far[:, :], 0.0))

            def link(name, value, ins):
                ins.then_inc(s[name], 1)
                dve.wait_ge(s[name], value)

            def mean_var(k, n, src, stats, mvs):
                for u in range(2):
                    last = V.bn_stats(stats[:, u, :], src[u])
                last.then_inc(s[f"{k}_stats"], 1)
                alone(dve)
                dve.wait_ge(s[f"{k}_stats"], n)
                for u in range(2):
                    last = V.bn_aggr(mvs[:, u, :], stats[:, u, :])
                last.then_inc(s[f"{k}_mv"], 1)

            def rsqrt(name, v, y, w, scratch, count, per):
                n = [0]

                def chain(ins):
                    n[0] += 1
                    ins.then_inc(s[name], 1)
                    dve.wait_ge(s[name], count * per + n[0])

                chain(V.tensor_scalar(y.bitcast(i32), v.bitcast(i32), 1, None, ALU.logical_shift_right))
                V.tensor_scalar(w, v, -0.5, None, ALU.mult)
                chain(V.tensor_scalar(y.bitcast(i32), y.bitcast(i32), -1.0, float(0x5F3759DF), ALU.mult, ALU.add))
                for it in range(4):
                    chain(V.tensor_tensor(scratch, y, y, ALU.mult))
                    chain(V.tensor_tensor(scratch, scratch, w, ALU.mult))
                    last = V.scalar_tensor_tensor(y, scratch, 1.5, y, ALU.add, ALU.mult)
                    if it < 3:
                        chain(last)
                assert n[0] == per
                return last

            def tiles(g):
                return [xs[:, bass.ds(2 * g + u, 1), :].squeeze(1) for u in range(2)]

            def step(i, p):
                q = 1 - p
                if on(i, 1):
                    some(dve, s["ss_in_psum"], i - 1)
                    dve.wait_ge(s["far_in_psum"], i)
                    V.tensor_tensor(far[:, :], far[:, :], ps_F, ALU.add).then_inc(s["far_added"], 1)
                if on(i, -1):
                    dve.wait_ge(s["ln1_mv"], i + 2)
                    last = V.tensor_scalar(var[:, 0:2], mv[:, q, :, 1], LN_EPS, None, ALU.add)
                if on(i, 2):
                    dve.wait_ge(s["ss_in_psum"], i - 1)
                    last = V.tensor_scalar(var[:, 2:4], ps_Q, 1.0 / H, RMS_EPS, ALU.mult, ALU.add)
                if on(i, 4):
                    dve.wait_ge(s["ln2_mv"], i - 3)
                    last = V.tensor_scalar(var[:, 4:6], mv2[:, p, :, 1], LN_EPS, None, ALU.add)
                if on(i, -1) or on(i, 2) or on(i, 4):
                    link("ms_ready", i + 3, last)
                    some(dve, s["rb_in_psum"], i - 2)
                    rsqrt("newton", var[:, :], root[:, :], nhalf[:, :], newt[:, :], i + 1, 13).then_inc(s["root_ready"], 1)
                    dve.wait_ge(s["root_ready"], i + 2)
                else:
                    V.tensor_copy(newt[:, 0:1], var[:, 0:1]).then_inc(s["ms_ready"], 1)
                if on(i, -1):
                    some(dve, s["aggT_in_psum"], i)
                    for u in range(2):
                        last = V.tensor_scalar(xn[:, q, u, :], tiles(i + 1)[u], mv[:, q, u, 0:1], root[:, u:u + 1], ALU.subtract, ALU.mult)
                    last.then_inc(s["xn_ready"], 1)
                if on(i, 4):
                    some(dve, s["x2nT_in_psum"], i - 5)
                    for u in range(2):
                        last = V.tensor_scalar(x2n[:, p, u, :], tiles(i - 4)[u], mv2[:, p, u, 0:1], root[:, 4 + u:5 + u], ALU.subtract, ALU.mult)
                    last.then_inc(s["x2n_ready"], 1)
                if on(i, 5):
                    dve.wait_ge(s["tb_in_psum"], i - 4)
                    some(dve, tb_stored[q], 16 * half(i - 5, q), None)
                    V.tensor_copy(tb[:, q, :, :], ps_B.rearrange("p (u c) -> p u c", u=2)).then_inc(s["tb_ready"], 1)
                if on(i, -2):
                    alone(dve)
                    dve.wait_ge(x_loaded[p], 16 * half(i + 2, p) + 16)
                    mean_var("ln1", i + 3, tiles(i + 2), st, mv[:, p, :, :])
                if on(i, 0):
                    dve.wait_ge(s["adjT_in_psum"], i + 1)
                    some(dve, s["aggT_in_psum"], i - 1)
                    V.tensor_tensor(adjT[:, p, :, :].rearrange("p a b -> p (a b)"), bank_T[:, :], epsI[:, :], ALU.add).then_inc(s["adjT_ready"], 1)
                    dve.wait_ge(s["aggT_in_psum"], i + 1)
                    some(dve, s["h_in_psum"], i - 1)
                    V.tensor_copy(aggT[:, p, :], ps_A).then_inc(s["aggT_ready"], 1)
                if on(i, 3):
                    xg = xs[:, bass.ds(2 * (i - 3), 2), :]
                    link("x_b2", i - 2, V.tensor_tensor(xg, xg, b2_r[:, :].unsqueeze(1).to_broadcast([P, 2, D]), ALU.add))
                    dve.wait_ge(s["o_in_psum"], i - 2)
                    V.tensor_tensor(xg, xg, ps_O, ALU.add).then_inc(s["x1_ready"], 1)
                    alone(dve)
                    dve.wait_ge(s["x1_ready"], i - 2)
                    mean_var("ln2", i - 2, tiles(i - 3), st2, mv2[:, q, :, :])
                if on(i, 2):
                    dve.wait_ge(s["rb_ready"], i - 1)
                    some(dve, s["s_ready"], i - 3)
                    for c in range(HC):
                        last = V.scalar_tensor_tensor(uu[:, p, c, :], ps_H[:, p, c, :], b1_c[:, c:c + 1], rb[:, :], ALU.add, ALU.mult)
                    last.then_inc(s["u_ready"], 1)
                if on(i, -1):
                    some(dve, s["far_in_psum"], i + 1)
                    for b in range(FSTEP // FB):
                        at = (i + 1) * FSTEP + b * FB
                        V.tensor_tensor(hot_lo[:, b, :, :], far_lo[:, bass.ds(at, FB)].unsqueeze(1).to_broadcast([P, P, FB]),
                                        iota_lo[:, :, :], ALU.is_equal)
                        last = V.tensor_tensor(hot_hi[:, b, :, :], far_hi[:, bass.ds(at, FB)].unsqueeze(1).to_broadcast([P, OWN, FB]),
                                               iota_hi[:, :, :], ALU.is_equal)
                    last.then_inc(s["hot_built"], 1)

            piped(dve, step)

            def slink(ins):
                own_n[0] += 1
                ins.then_inc(s["own_prep"], 1)
                dve.wait_ge(s["own_prep"], own_n[0])

            own_n = [0]
            dve.wait_ge(s["bk_loaded"], 16)
            segs = bk.rearrange("p (g n) -> p g n", n=SEG_B)
            for g in range(0, BKEYS // SEG_B, 4):
                top([segs[:, g + u, :] for u in range(4)], [blev1[:, g + u, :] for u in range(4)], KEEP_B1 // 8)
            top([blev1[:, GROUP_B2 * u:GROUP_B2 * (u + 1), :].rearrange("p a b -> p (a b)") for u in range(4)],
                [blev2[:, u * KEEP_B2:(u + 1) * KEEP_B2] for u in range(4)], KEEP_B2 // 8)
            slink(V.tensor_copy(blev2[:, 4 * KEEP_B2:4 * KEEP_B2 + OWN], self_keys[:, :].bitcast(fp32)))
            top([blev2], [own], OWNED // 8)
            ki = own.bitcast(i32)
            index, dlo, self_, nself, empty, lastw, nlast, tmp = (bw[:, k, :] for k in range(8))
            slink(V.tensor_scalar(bi, ki, M - 1, None, ALU.bitwise_and))
            slink(V.tensor_copy(index, bi))
            slink(V.tensor_scalar(self_, index, float(M - 1), None, ALU.is_equal))
            slink(V.tensor_scalar(bi, ki, 13, None, ALU.logical_shift_right))
            slink(V.tensor_scalar(tmp, bi, -float(K_REAL + M - 1), None, ALU.add))
            slink(V.tensor_tensor(tmp, tmp, self_, ALU.mult))
            slink(V.tensor_tensor(index, index, tmp, ALU.add))
            slink(V.tensor_scalar(bi, bi, OWN - 1, None, ALU.bitwise_and))
            slink(V.tensor_copy(dlo, bi)) if False else V.tensor_copy(dlo, bi).then_inc(s["own_ready"], 1)
            slink(V.tensor_scalar(empty, own, 0.0, None, ALU.is_equal))
            V.reduce_sum(count[:, 0:1], empty, AX.X)
            slink(V.tensor_scalar(nself, self_, -1.0, 1.0, ALU.mult, ALU.add))
            V.memset(lastw[:, OWNED - 1:OWNED], 1.0)
            slink(V.tensor_copy(lastw[:, 0:OWNED - 1], self_[:, 1:OWNED]))
            slink(V.tensor_scalar(nlast, lastw, -1.0, 1.0, ALU.mult, ALU.add))
            V.reduce_sum(count[:, 1:2], valid_n[:, :], AX.X)
            slink(V.reduce_sum(count[:, 2:3], far[:, :], AX.X))
            slink(V.tensor_tensor(count[:, 3:4], count[:, 0:1], count[:, 1:2], ALU.add))
            slink(V.tensor_tensor(count[:, 3:4], count[:, 3:4], count[:, 2:3], ALU.subtract))
            V.tensor_scalar(count[:, 3:4], count[:, 3:4], float(OWN - OWNED), None, ALU.add).then_inc(s["diff_ready"], 1)
            dve.wait_ge(s["idx_in_psum"], 1)
            V.tensor_copy(dloT, halfH[1][:, 0:OWNED]).then_inc(s["idx_ready"], 0) if False else V.tensor_copy(dloT, halfH[1][:, 0:OWNED])
            V.tensor_copy(idxT, halfH[0][:, 0:OWNED]).then_inc(s["idx_done"], 1)

            SH = [P, HEADS, OWNED]

            def each(m):
                return m.unsqueeze(1).to_broadcast(SH)

            def term(m):
                return m.unsqueeze(2).to_broadcast(SH)

            a_s, a_d, n_far = terms[:, 0:HEADS, :], terms[:, HEADS:2 * HEADS, :], terms[:, 8, :]
            w0, w1_ = (ow[:, k, :, :] for k in range(2))
            w2_ = w3 = a_d
            w4 = a_s
            far_s, far_h = last_node[:, 0:HEADS], last_node[:, 2 * HEADS:ROW]
            dve.wait_ge(s["terms_ready"], 9)
            dve.wait_ge(s["last_loaded"], 16)
            slink(V.tensor_tensor(n_far, n_far, self_, ALU.mult))
            slink(V.tensor_tensor(a_d, a_d, each(self_), ALU.mult))
            for h in range(HEADS):
                last = V.tensor_tensor_scan(w0[:, h, :], nself, a_d[:, h, :], 0.0, ALU.mult, ALU.add)
            slink(last)
            slink(V.tensor_scalar(tmp, empty, LOW, None, ALU.mult))
            slink(V.tensor_tensor(a_s, a_s, each(tmp), ALU.add))
            slink(V.tensor_scalar(tmp, n_far, 0.5, None, ALU.is_gt))
            slink(V.tensor_scalar(tmp, tmp, -1.0, -LOW, ALU.add, ALU.mult))
            slink(V.tensor_tensor(w1_, each(tmp), term(far_s), ALU.add))
            slink(V.tensor_tensor(w1_, w1_, a_s, ALU.max))
            slink(V.tensor_scalar(tmp, self_, LOW, None, ALU.mult))
            for h in range(HEADS):
                last = V.tensor_tensor_scan(w2_[:, h, :], tmp, w1_[:, h, :], LOW, ALU.add, ALU.max)
            slink(last)
            slink(V.tensor_tensor(w2_, w2_, each(lastw), ALU.mult))
            for h in range(HEADS):
                last = V.tensor_tensor_scan(w1_[:, h, ::-1], nlast[:, ::-1], w2_[:, h, ::-1], 0.0, ALU.mult, ALU.add)
            slink(last)
            slink(V.tensor_tensor(w3, w1_, term(far_s), ALU.min))
            slink(V.tensor_tensor(w3, w3, w0, ALU.add))
            slink(V.tensor_tensor(w4, a_s, w0, ALU.add))
            slink(V.tensor_tensor(w1_, w1_, w0, ALU.add))
            slink(V.scalar_tensor_tensor(w1_, w1_, 0.2, w1_, ALU.mult, ALU.max))
            slink(V.scalar_tensor_tensor(w3, w3, 0.2, w3, ALU.mult, ALU.max))
            slink(V.scalar_tensor_tensor(w4, w4, 0.2, w4, ALU.mult, ALU.max))
            slink(V.tensor_tensor(w3, w3, w1_, ALU.subtract))
            V.tensor_tensor(w4, w4, w1_, ALU.subtract).then_inc(s["exp_in"], 1)
            dve.wait_ge(s["exp_done"], 1)
            V.tensor_tensor(w3, w3, each(n_far), ALU.mult).then_inc(s["back_ready"], 1)
            dve.wait_ge(s["backT_ready"], 8)
            V.tensor_tensor(rows[:, :, 2 * HEADS:ROW].rearrange("p n (h k) -> p h n k", h=HEADS)[:, 0, :, :] if False else rows[:, :, 8:12],
                            rows[:, :, 8:12], backT[:, 0, :].unsqueeze(2).to_broadcast([P, OWNED, EXPERTS]), ALU.mult)
            for h in range(1, HEADS):
                V.tensor_tensor(rows[:, :, 8 + 4 * h:12 + 4 * h], rows[:, :, 8 + 4 * h:12 + 4 * h],
                                backT[:, h, :].unsqueeze(2).to_broadcast([P, OWNED, EXPERTS]), ALU.mult)
            V.tensor_copy(rows[:, :, 0:2 * HEADS].rearrange("p n k -> p k n"), backT).then_inc(s["vals_made"], 1)
            dve.wait_ge(s["vals_made"], 1)

            def take_bank(k):
                dve.wait_ge(s["agg_in_psum"], k + 1)
                pairs = banks[k][0:OWN, 0:16 * ROW].rearrange("p (t u c) -> p t u c", u=2, c=ROW)
                V.tensor_copy(agg[0:OWN, 8 * k:8 * k + 8, :], pairs[:, :, 0, :])
                V.tensor_copy(odd[:, 8 * k:8 * k + 8, :], pairs[:, :, 1, :]).then_inc(s["agg_out"], 1)

            for k in range(8):
                if k >= 2:
                    dve.wait_ge(s["agg_in_psum"], k - 1)
                for c in range(CHUNKS):
                    last = V.tensor_tensor(hot[:, k % 2, c, :, :],
                                           dloT[:, c * P + 16 * k:c * P + 16 * k + 16].unsqueeze(2).to_broadcast([P, 16, OWN]),
                                           iota_own[:, :].unsqueeze(1).to_broadcast([P, 16, OWN]), ALU.is_equal)
                last.then_inc(s["hots_built"], 1)
                if k >= 1:
                    take_bank(k - 1)
            take_bank(7)
            dve.wait_ge(s["odd_moved"], 16)
            dve.wait_ge(s["agg_out"], 8)
            for h in range(HEADS):
                last = V.tensor_tensor(gf[:, :, 4 * h:4 * h + 4], agg[:, :, HEADS + h].unsqueeze(2).to_broadcast([P, TILES, EXPERTS]),
                                       far_h[:, 4 * h:4 * h + 4].unsqueeze(1).to_broadcast([P, TILES, EXPERTS]), ALU.mult)
            slink(last)
            slink(V.tensor_tensor(agg[:, :, 2 * HEADS:ROW], agg[:, :, 2 * HEADS:ROW], gf[:, :, :], ALU.add))
            slink(V.tensor_tensor(agg[:, :, HEADS:2 * HEADS], agg[:, :, HEADS:2 * HEADS], agg[:, :, 0:HEADS], ALU.add))

            dve.wait_ge(s["total_in_psum"], 1)
            V.tensor_scalar(redo[:, :], banks[0][:, 0:1], 0.5, None, ALU.is_gt).then_inc(s["redo_ready"], 1)
            dve.wait_ge(s["redo_ready"], 1)
            again = dve.value_load(redo[0:1, 0:1], min_val=0, max_val=1)
            with dve.If(again > 0):
                V.memset(zero2[:, :], 0.0).then_inc(s["zero2_done"], 1)
                dve.wait_ge(s["edges_loaded"], 32)
                V.tensor_scalar(srcs[:, 0:ECOLS], srcs[:, 0:ECOLS], M - 1, None, ALU.min).then_inc(s["edges_ready"], 1)
                V.tensor_scalar(dsts[:, 0:ECOLS], dsts[:, 0:ECOLS], M, None, ALU.min).then_inc(s["edges_ready"], 1)
                dve.wait_ge(s["edges_ready"], 2)
                dve.wait_ge(s["iota_done"], 2)
                LINKS = 11
                def edge_tile(t, p, j):
                    k = [0]

                    def chain(ins):
                        k[0] += 1
                        ins.then_inc(s["edge_chain"], 1)
                        dve.wait_ge(s["edge_chain"], LINKS * t + k[0])

                    dve.wait_ge(row_stored[1 - p], 16 * j + 16 * p)
                    V.tensor_copy(idx[:, 0:1], srcs[:, bass.ds(t, 1)]).then_inc(s["idx_ready"], 1)
                    V.tensor_copy(idx[:, 1:2], dsts[:, bass.ds(t, 1)]).then_inc(s["idx_ready"], 1)
                    V.tensor_copy(dstf[:, :], dsts[:, bass.ds(t, 1)]).then_inc(s["dstf_ready"], 1)
                    dve.wait_ge(s["dstf_ready"], t + 1)
                    dve.wait_ge(s["as_in_psum"], t + 1)
                    V.tensor_scalar(eq[:, :], bank_T[:, 0:P], dstf[:, 0:1], None, ALU.is_equal).then_inc(s["eq_ready"], 1)
                    dve.wait_ge(s["eq_ready"], t + 1)
                    chain(V.tensor_scalar(pen[:, :], eq[:, :], -1.0, -LOW, ALU.add, ALU.mult))
                    chain(V.tensor_tensor(masked[:, :, :], halfH[0].rearrange("p (h n) -> p h n", h=HEADS),
                                          pen[:, :].unsqueeze(1).to_broadcast([P, HEADS, P]), ALU.add))
                    chain(V.reduce_max(small[:, 0, :], masked[:, :, :], AX.X))
                    for signal in (src_in, dst_in, state_in):
                        dve.wait_ge(signal[p], 16 * j + 16)
                    V.tensor_tensor(small[:, 1, :], srow[:, 0:HEADS], drow[:, HEADS:2 * HEADS], ALU.add)
                    chain(V.tensor_tensor(small[:, 0, :], small[:, 0, :], drow[:, HEADS:2 * HEADS], ALU.add))
                    chain(V.scalar_tensor_tensor(small[:, 6:8, :], small[:, 0:2, :], 0.2, small[:, 0:2, :], ALU.mult, ALU.max))
                    chain(V.tensor_tensor(newrow[:, 0:HEADS], small[:, 6, :], strow[:, 0:HEADS], ALU.max))
                    V.tensor_tensor(small[:, 2, :], small[:, 7, :], newrow[:, 0:HEADS], ALU.subtract)
                    V.tensor_tensor(small[:, 3, :], strow[:, 0:HEADS], newrow[:, 0:HEADS], ALU.subtract).then_inc(s["mnew_ready"], 1)
                    chain(V.tensor_tensor(masked[:, 0, :], eq[:, :], lower[:, :], ALU.mult))
                    chain(V.reduce_sum(lead[:, 0:1], masked[:, 0, :], AX.X))
                    chain(V.tensor_scalar(lead[:, 1:2], lead[:, 0:1], 1.0, float(1 << 20), ALU.min, ALU.mult))
                    V.tensor_tensor(sidx[:, :], lead[:, 1:2], dstf[:, :], ALU.add)
                    dve.wait_ge(s["ee_ready"], t + 1)
                    V.tensor_copy(vals[:, 0:HEADS], small[:, 4, :])
                    V.tensor_tensor(vals[:, HEADS:ACC].rearrange("p (h k) -> p h k", h=HEADS),
                                    srow[:, 2 * HEADS:ROW].rearrange("p (h k) -> p h k", h=HEADS),
                                    small[:, 4, :].unsqueeze(2).to_broadcast([P, HEADS, EXPERTS]), ALU.mult).then_inc(s["vals_ready"], 1)
                    V.tensor_tensor(newrow[:, HEADS:2 * HEADS], strow[:, HEADS:2 * HEADS], small[:, 5, :], ALU.mult)
                    chain(V.tensor_tensor(newrow[:, 2 * HEADS:ROW].rearrange("p (h k) -> p h k", h=HEADS),
                                          strow[:, 2 * HEADS:ROW].rearrange("p (h k) -> p h k", h=HEADS),
                                          small[:, 5, :].unsqueeze(2).to_broadcast([P, HEADS, EXPERTS]), ALU.mult))
                    dve.wait_ge(s["sum_in_psum"], t + 1)
                    chain(V.tensor_tensor(newrow[:, HEADS:ROW], newrow[:, HEADS:ROW], bank_S[:, 0:ACC], ALU.add))
                    V.tensor_copy(lead[:, 2:3], lead[:, 0:1]).then_inc(s["newrow_ready"], 1)
                    assert k[0] == LINKS, k[0]

                with dve.Fori(0, ETILES // 2) as j:
                    edge_tile(2 * j, 0, j)
                    edge_tile(2 * j + 1, 1, j)
                dve.wait_ge(s["agg_in"], 16)


            gates_n = [0]

            def glink(ins):
                gates_n[0] += 1
                ins.then_inc(s["gate_chain"], 1)
                dve.wait_ge(s["gate_chain"], gates_n[0])

            def heads(t):
                return t.rearrange("p t (h k) -> p t h k", h=HEADS)

            def over(t, shape, axis):
                return t.unsqueeze(axis).to_broadcast(shape)

            T16 = [P, TILES, HK]
            den = agg[:, :, HEADS:2 * HEADS]
            glink(V.tensor_scalar(den, den, 1e-16, None, ALU.add))
            glink(V.reciprocal(den, den))
            for t in range(HEADS):
                last = V.tensor_tensor(gf[:, :, t * EXPERTS:(t + 1) * EXPERTS], agg[:, :, 2 * HEADS + t * EXPERTS:2 * HEADS + (t + 1) * EXPERTS],
                                       over(agg[:, :, HEADS + t], [P, TILES, EXPERTS], 2), ALU.mult)
            glink(last)
            glink(V.tensor_tensor(gf[:, :, :], gf[:, :, :], over(bgat_r[:, :], T16, 1), ALU.add))
            mean, gvar, groot = gs[:, 0, :], gs[:, 1, :], gs[:, 2, :]
            glink(V.reduce_sum(mean, gf[:, :, :], AX.X))
            glink(V.tensor_scalar(mean, mean, 1.0 / HK, None, ALU.mult))
            glink(V.tensor_tensor(gf[:, :, :], gf[:, :, :], over(mean, T16, 2), ALU.subtract))
            glink(V.tensor_tensor(gw[:, :, :], gf[:, :, :], gf[:, :, :], ALU.mult))
            glink(V.reduce_sum(gvar, gw[:, :, :], AX.X))
            glink(V.tensor_scalar(gvar, gvar, 1.0 / HK, LN_EPS, ALU.mult, ALU.add))
            glink(rsqrt("gate_newton", gvar, groot, gs[:, 3, :], gs[:, 4, :], 0, 13))
            glink(V.tensor_tensor(gf[:, :, :], gf[:, :, :], over(groot, T16, 2), ALU.mult))
            glink(V.tensor_tensor(gf[:, :, :], gf[:, :, :], over(lng_r[:, :], T16, 1), ALU.mult))
            glink(V.tensor_tensor(gf[:, :, :], gf[:, :, :], over(lnb_r[:, :], T16, 1), ALU.add))
            glink(V.reduce_sum(sc[:, :, :], gf[:, :, :].rearrange("p t (h k) -> p t k h", h=HEADS), AX.X))
            glink(V.tensor_scalar(sc[:, :, :], sc[:, :, :], 1.0 / HEADS, None, ALU.mult))
            beaten = gw[:, :, 0:12].rearrange("p t (e f) -> p t e f", e=EXPERTS)
            for f in range(EXPERTS):
                for e in range(f + 1, EXPERTS):
                    V.tensor_tensor(beaten[:, :, e, f], sc[:, :, f], sc[:, :, e], ALU.is_ge)
                    last = V.tensor_tensor(beaten[:, :, f, e - 1], sc[:, :, e], sc[:, :, f], ALU.is_gt)
            glink(last)
            cnt = gf[:, :, 0:EXPERTS]
            glink(V.reduce_sum(cnt, beaten, AX.X))
            glink(V.tensor_scalar(cnt, cnt, 1.5, None, ALU.is_lt))
            glink(V.reduce_max(mean, sc[:, :, :], AX.X))
            V.tensor_tensor(sc[:, :, :], sc[:, :, :], over(mean, [P, TILES, EXPERTS], 2), ALU.subtract).then_inc(s["gates_e"], 1)
            dve.wait_ge(s["gates_exp"], 1)
            glink(V.tensor_tensor(gates[:, :, :], gates[:, :, :], cnt, ALU.mult))
            glink(V.reduce_sum(mean, gates[:, :, :], AX.X))
            glink(V.reciprocal(mean, mean))
            V.tensor_tensor(gates[:, :, :], gates[:, :, :], over(mean, [P, TILES, EXPERTS], 2), ALU.mult).then_inc(s["gates_ready"], 1)
            dve.wait_ge(s["gates_ready"], 1)

            ebank = [bank_T[:, :], bank_A[:, :]]
            with dve.Fori(0, GROUPS, 1) as g:
                for k in range(4):
                    t = 4 * g + k
                    row = xs[:, bass.ds(t, 1), :].squeeze(1)
                    gate = gcol[:, k % 2, :]
                    dve.wait_ge(s["eo_in_psum"], t + 1)
                    V.tensor_copy(gate, gates[:, bass.ds(t, 1), :].squeeze(1)).then_inc(s["comb_chain"], 1)
                    dve.wait_ge(s["comb_chain"], 4 * t + 1)
                    for e in range(EXPERTS):
                        ins = V.scalar_tensor_tensor(row, ebank[k % 2][:, e * D:(e + 1) * D], gate[:, e:e + 1], row, ALU.mult, ALU.add)
                        if e < EXPERTS - 1:
                            ins.then_inc(s["comb_chain"], 1)
                            dve.wait_ge(s["comb_chain"], 4 * t + 2 + e)
                    ins.then_inc(s["eo_used"], 1)


_INS = ["x", "adj", "L0_gnn_epsilon", "L0_gnn_W1", "L0_gnn_b1", "L0_gnn_rms_weight", "L0_gnn_W2", "L0_gnn_b2",
        "L0_ffn_W_gat", "L0_ffn_att_src", "L0_ffn_att_dst", "L0_ffn_b_gat", "L0_ffn_ln_gamma", "L0_ffn_ln_beta",
        "L0_ffn_W1", "L0_ffn_b1", "L0_ffn_W2", "L0_ffn_b2", "L0_ffn_edge_index"]


def kernel(**inputs):
    import numpy as np
    import concourse.bacc as bacc
    from concourse import mybir as mb
    from concourse.bass_utils import run_bass_kernel_spmd

    nc = bacc.Bacc("TRN2", target_bir_lowering=False, num_devices=1)
    arrays, args = {}, []
    for name in _INS:
        a = np.ascontiguousarray(inputs[name])
        if a.ndim == 0:
            a = a.reshape(1)
        arrays[f"in_{name}"] = a
        args.append(nc.dram_tensor(f"in_{name}", a.shape, mb.dt.from_np(a.dtype), kind="ExternalInput").ap())
    args.append(nc.dram_tensor("out_x", (GRAPHS, NODES, D), mb.dt.float32, kind="ExternalOutput").ap())
    build(nc, *args)
    r = run_bass_kernel_spmd(nc, [arrays], core_ids=[0])
    return r.results[0]["out_x"]
```

```python
from contextlib import ExitStack

import concourse.bass as bass
from concourse import mybir

P = 128
GRAPHS, NODES, D = 32, 256, 128
H = 512
M = GRAPHS * NODES
TILES = M // P
EXPERTS, HEADS, F = 4, 4, 256
HK = HEADS * EXPERTS
EDGES = 524288
ECOLS = EDGES // P
ETILES = ECOLS + TILES
QUARTER = ECOLS // 4
ROW = 2 * HEADS + HK
OWN = M // P
SEG, KEEP1, REAL1, GROUP2, KEEP2, SENT = 128, 56, 24, 4, 56, 320
CELL = 16
BKEYS = P * CELL
SEG_B, KEEP_B1, GROUP_B2, KEEP_B2, OWNED = 128, 40, 4, 104, 384
CHUNKS = OWNED // P
BATCH = 16
K_REAL, K_FAR = 2048, 1 << 23
SEND = 10
PART = 80
FARCOLS = (ECOLS // SEG) * KEEP1
FB = 14
GATHER = 16
ACC = HEADS + HK
LN_EPS, RMS_EPS = 1e-5, 1e-6
LOW = -1e30
HC = H // P
FC = EXPERTS * F // P
GROUP, PAIR = 2 * P, 2
ARENA = 8 * OWNED * 2 + OWNED * ROW + 12 * OWNED
GROUPS = M // GROUP
KEPT = GROUPS // 4
EO = EXPERTS * D
BLOCK, SLOTS = 3, 4
BLOCKS = (GROUPS - KEPT) // BLOCK
VECTOR_BLOCKS = BLOCKS - 1


def build(nc, x, adj, eps, W1, b1, rms_w, W2, b2, W_gat, att_src, att_dst, b_gat, ln_g, ln_b,
          We1, be1, We2, be2, edges, out):
    fp32, i32, bf16 = mybir.dt.float32, mybir.dt.int32, mybir.dt.bfloat16
    ALU, ACT, AX = mybir.AluOpType, mybir.ActivationFunctionType, mybir.AxisListType
    ctx = ExitStack()
    with ctx:
        def sb(name, shape, dt=fp32):
            return ctx.enter_context(nc.sbuf_tensor("sb_" + name, shape, dt))

        def pb(name, shape, dt=fp32):
            return ctx.enter_context(nc.psum_tensor("ps_" + name, shape, dt))

        def sem(name):
            return ctx.enter_context(nc.semaphore(name))

        table = nc.dram_tensor("table", [M + 1, ROW], fp32, kind="Internal").ap()
        state = nc.dram_tensor("state", [M + 1, ROW], fp32, kind="Internal").ap()

        ident = sb("ident", [P, P])
        ones = sb("ones", [P, P])
        lower = sb("lower", [P, P])
        epsI = sb("epsI", [P, 4 * P])
        eps_c = sb("eps_c", [P, 1])
        w1 = sb("w1", [P, H])
        b1_c = sb("b1_c", [P, HC])
        rms_c = sb("rms_c", [P, HC])
        w2 = sb("w2", [P, HC, D])
        b2_r = sb("b2_r", [1, D])
        wcat = sb("wcat", [P, ROW])
        watt = sb("watt", [P, 2, HK])
        att_r = sb("att_r", [P, 2, HK])
        bgat_r = sb("bgat_r", [P, HK])
        lng_r = sb("lng_r", [P, HK])
        lnb_r = sb("lnb_r", [P, HK])
        we1 = sb("we1", [P, EXPERTS, F])
        be1_c = sb("be1_c", [P, FC])
        we2 = sb("we2", [P, FC, D])
        be2_r = sb("be2_r", [P, EO])
        xs = sb("xs", [P, TILES, D])
        x2nT = sb("x2nT", [P, M])
        outputs = nc.dram_tensor("outputs", [(GROUPS - KEPT) * P, PAIR * EO], fp32, kind="Internal").ap()
        bkeys = nc.dram_tensor("bkeys", [P * BKEYS, 1], i32, kind="Internal").ap()
        arena = sb("arena", [P, ARENA])

        def region(at):
            def take(shape, dt=fp32):
                n = 1
                for k in shape:
                    n *= k
                words = n if dt in (fp32, i32) else (n + 1) // 2
                t = arena[:, take.at:take.at + words]
                take.at += words
                assert take.at <= ARENA, take.at
                t = t if dt == fp32 else t.bitcast(dt)
                letters = "abcd"[:len(shape)]
                if len(shape) > 1:
                    t = t.rearrange(f"p ({' '.join(letters)}) -> p {' '.join(letters)}",
                                    **{c: k for c, k in zip(letters[1:], shape[1:])})
                return t
            take.at = at
            return take

        src = x2nT[:, 0:ECOLS].bitcast(i32)
        dst = x2nT[:, ECOLS:2 * ECOLS].bitcast(i32)
        take = region(0)
        sent = take([SENT])
        where = take([SENT], i32)
        adjs = take([2, 2, NODES])
        shared = take.at
        work = take([3, QUARTER])
        valid = take([4, QUARTER])
        real1 = take([ECOLS // SEG, REAL1])
        lev2 = take([ECOLS // SEG // GROUP2, KEEP2])
        rank_w = take([5, SENT])
        keys_at = 8 * OWNED * 2 + OWNED + OWNED * ROW - ECOLS
        assert take.at <= keys_at
        keys = region(keys_at)([ECOLS // SEG, SEG])
        take = region(shared)
        xn = take([2, 2, D])
        adjT = take([2, 2, NODES])
        aggT = take([2, NODES])
        sq = take([2, HC, NODES])
        rb = take([NODES])
        uu = take([2, HC, NODES])
        assert take.at <= keys_at
        take = region(keys_at + ECOLS)
        ss = take([2, HC, NODES])
        x2n = take([2, 2, D])
        x2nTc = take([2, NODES])
        tb = take([2, 2, ROW])
        take = region(0)
        terms = take([8, OWNED])
        ow = take([2, HEADS, OWNED])
        own = take([OWNED])
        rows = take([OWNED, ROW])
        assert take.at == keys_at + ECOLS
        idxT = take([OWNED], i32)
        dloT = take([OWNED], bf16)
        take.at += OWNED // 2
        parts_at = take.at
        bi = take([OWNED], i32)
        bw = take([8, OWNED])
        def parts_in(at):
            return region(at)([CHUNKS, BATCH, 3, ROW], bf16)

        part_words = CHUNKS * BATCH * 3 * ROW // 2
        parts = [parts_in(parts_at), parts_in(parts_at + part_words), parts_in(8 * OWNED)]
        hot_over_terms = region(0)([CHUNKS, OWN, BATCH], bf16)
        take = region(0)
        bk = take([BKEYS])
        blev1 = take([BKEYS // SEG_B, KEEP_B1])
        blev2 = take([BKEYS // SEG_B // GROUP_B2 * KEEP_B2 + OWN])
        take = region(0)
        srcs = take([ETILES], i32)
        dsts = take([ETILES], i32)
        take = region(0)
        hh = [take([FC, GROUP]) for _ in range(2)]
        eo = take([2, PAIR, EO])
        assert take.at <= 2 * 8 * OWNED
        eo_back = region(ARENA - SLOTS * BLOCK * PAIR * EO)([SLOTS, BLOCK * PAIR, EO])
        eo_kept = x2nT[:, :].rearrange("p (t c) -> p t c", c=EO)
        iota_lo = sb("iota_lo", [P, P, FB], bf16)
        far_lo = sb("far_lo", [P, FARCOLS], bf16)
        far_hi = sb("far_hi", [P, FARCOLS], bf16)
        iota_own = sb("iota_own", [P, OWN])
        bzeros = sb("bzeros", [P, 256], i32)
        self_keys = sb("self_keys", [P, OWN], i32)
        place0 = sb("place0", [P, 1])
        far = sb("far", [P, TILES])
        valid_n = sb("valid_n", [P, 4])
        count = sb("count", [P, 4])
        last_node = sb("last_node", [P, ROW])
        stage_k = sb("stage_k", [P, 2, SEND], i32)
        stage_w = sb("stage_w", [P, 2, SEND], i32)
        stage_i = sb("stage_i", [P, 2, GATHER], i32)
        stage_r = sb("stage_r", [P, 2, GATHER, ROW])
        redo = sb("redo", [P, 1], i32)
        signal = sb("signal", [P, 1])
        st = sb("st", [P, 2, 6])
        mv = sb("mv", [P, 2, 2, 2])
        var = sb("var", [P, 6])
        root = sb("root", [P, 6])
        nhalf = sb("nhalf", [P, 6])
        newt = sb("newt", [P, 6])
        st2 = sb("st2", [P, 2, 6])
        mv2 = sb("mv2", [P, 2, 2, 2])
        idx = sb("idx", [P, 2], i32)
        zrow = sb("zrow", [P, ROW])
        st0 = sb("st0", [P, ROW])
        dstf = sb("dstf", [P, 1])
        srow = sb("srow", [P, ROW])
        drow = sb("drow", [P, ROW])
        strow = sb("strow", [P, ROW])
        newrow = sb("newrow", [P, ROW])
        small = sb("small", [P, 8, HEADS])
        vals = sb("vals", [P, ACC])
        lead = sb("lead", [P, 4])
        sidx = sb("sidx", [P, 1], i32)
        late = sb("late", [P, 2 * TILES * (ROW + HK)])
        agg = late[:, 0:TILES * ROW].rearrange("p (t c) -> p t c", c=ROW)
        odd = late[0:OWN, TILES * ROW:2 * TILES * ROW].rearrange("p (t c) -> p t c", c=ROW)
        gf = late[:, 2 * TILES * ROW:TILES * (2 * ROW + HK)].rearrange("p (t c) -> p t c", c=HK)
        gw = late[:, TILES * (2 * ROW + HK):].rearrange("p (t c) -> p t c", c=HK)
        lev1 = late[:, 0:FARCOLS].rearrange("p (g n) -> p g n", n=KEEP1)
        counted = late[:, 2 * FARCOLS:2 * FARCOLS + QUARTER]
        far_i = late[:, FARCOLS:2 * FARCOLS].bitcast(i32)
        half_block = P * FB // 2
        hot_lo = [late[:, k * half_block:(k + 1) * half_block].bitcast(bf16).rearrange("p (n c) -> p n c", c=FB) for k in range(2)]
        hot_hi = [late[:, (4 + k) * half_block // 2:(5 + k) * half_block // 2].bitcast(bf16).rearrange("p (n c) -> p n c", c=FB)
                  for k in range(2)]
        hot = [late[:, 2 * TILES * ROW:2 * TILES * ROW + CHUNKS * OWN * BATCH // 2].bitcast(bf16)
               .rearrange("p (c n b) -> p c n b", c=CHUNKS, b=BATCH), hot_over_terms]
        iota_batch = w1[:, 0:OWN * BATCH // 2].bitcast(bf16).rearrange("p (n b) -> p n b", b=BATCH)
        scratch = gf.rearrange("p t c -> p (t c)")
        eq, pen = scratch[:, 0:P], scratch[:, P:2 * P]
        masked = scratch[:, 2 * P:(2 + HEADS) * P].rearrange("p (h n) -> p h n", h=HEADS)
        a_dst = sb("a_dst", [P, TILES, HEADS])
        far_e = sb("far_e", [P, TILES, HEADS])
        gs = sb("gs", [P, 5, TILES])
        sc = sb("sc", [P, TILES, EXPERTS])
        gates = sb("gates", [P, TILES, EXPERTS])

        ps_four = pb("four", [P, 4, 512])
        bank_T = ps_four[:, 0, :]
        bank_A = ps_four[:, 1, :]
        bank_O = ps_four[:, 2, :]
        bank_S = ps_four[:, 3, :]
        ps_H = pb("H", [P, 2, HC, NODES])
        ps_T = bank_T[:, :].rearrange("p (m n) -> p m n", m=2)
        ps_A, ps_Q = bank_A[:, 0:NODES], bank_A[:, NODES:NODES + 2]
        ps_O = bank_O[:, 0:2 * D].rearrange("p (u d) -> p u d", u=2)
        ps_B = bank_O[:, 2 * D:2 * D + 2 * ROW]
        ps_F = bank_O[:, 0:TILES]
        ps_R, ps_X = bank_S[:, 0:NODES], bank_S[:, NODES:2 * NODES]
        halfH = [ps_H[:, k, 2 * j:2 * j + 2, :].rearrange("p a b -> p (a b)") for k in range(2) for j in range(2)]

        sums = [ps_H[:, :, :, :].rearrange("p a b n -> p (a b n)").rearrange("p (g w) -> p g w", g=4), ps_four[:, :, :]]

        banks = [bank_T[:, :], bank_A[:, :]] + halfH + [bank_O[:, :], bank_S[:, :]]

        names = ["valid_ready", "valid_counted", "prep", "sorted_", "sent_ready", "bzero", "iotas", "hot_built",
                 "hot_used", "far_added", "merge_in", "merge_exp", "bk_loaded", "own_prep", "own_ready",
                 "idx_in_psum", "idx_done", "far_taken", "last_loaded", "terms_in_psum", "terms_ready",
                 "exp_in", "exp_done", "back_ready", "back_in_psum", "weights_back", "maxima_back", "vals_made",
                 "hots_built", "hi_ready", "rem_ready", "mid_ready", "lo_ready", "agg_in_psum", "agg_out",
                 "odd_moved", "diff_ready", "total_in_psum", "redo_ready", "staged_k", "staged_i", "rows_moved",
                 "bk_clear", "xn_ready", "adjT_in_psum", "adjT_ready", "aggT_in_psum", "aggT_ready", "h_in_psum",
                 "sq_ready", "ss_in_psum", "u_ready", "s_ready", "o_in_psum", "x1_ready", "x2n_ready",
                 "x2nT_in_psum", "x2nT_ready", "tb_in_psum", "tb_ready", "weights", "const_a", "wcat_ready",
                 "state_init", "pool_const", "edges_loaded", "edges_ready", "sorted_over", "idx_ready", "dstf_ready",
                 "eq_ready", "as_in_psum", "mnew_ready", "ee_ready", "vals_ready", "sum_in_psum", "newrow_ready",
                 "setup_chain", "edge_chain", "gate_chain", "comb_chain", "ln1_stats", "ln1_mv", "ln2_stats",
                 "ln2_mv", "ms_ready", "newton", "root_ready", "rb_in_psum", "rb_ready", "gate_newton", "agg_in",
                 "gates_e", "gates_exp", "gates_ready", "hh_in_psum", "hh_ready", "eo_in_psum", "eo_used",
                 "combined", "others_combined", "sum_chain", "gated", "iota_done", "zero_done"]
        s = {n: sem(n) for n in names}
        x_loaded = [sem(f"x_loaded{p}") for p in range(2)]
        adj_loaded = [sem(f"adj_loaded{p}") for p in range(2)]
        scattered = [sem(f"scattered{p}") for p in range(2)]
        gathered = [sem(f"gathered{p}") for p in range(2)]
        tb_stored = [sem(f"tb_stored{p}") for p in range(2)]
        src_in, dst_in, state_in, row_stored = ([sem(f"{n}{p}") for p in range(2)]
                                                for n in ("src_in", "dst_in", "state_in", "row_stored"))
        out_stored = [sem(f"out_stored{p}") for p in range(2)]
        eo_stored = [sem(f"eo_stored{p}") for p in range(2)]
        quarter_loaded = [sem(f"quarter_loaded{k}") for k in range(4)]
        eo_loaded = [sem(f"eo_loaded{k}") for k in range(SLOTS)]

        x_t = x.rearrange("g (u q) d -> g q u d", q=P)
        adj_t = adj.rearrange("g (u q) m -> g q u m", q=P)
        out_t = out.rearrange("g (u q) d -> g q u d", q=P)
        out_g = outputs.rearrange("(g p) c -> g p c", p=P)
        out_b = outputs.rearrange("(b g p) c -> b p g c", g=BLOCK, p=P)
        tab_t = table[0:M, :].rearrange("(g u q) c -> g q u c", u=2, q=P)

        FIRST, LOOP_FROM, LOOP_TO, END = -2, 6, GRAPHS - 2, GRAPHS + 5

        def piped(eng, step):
            for i in range(FIRST, LOOP_FROM):
                step(i, i % 2)
            with eng.Fori(LOOP_FROM // 2, LOOP_TO // 2) as j:
                step(2 * j, 0)
                step(2 * j + 1, 1)
            for i in range(LOOP_TO, END):
                step(i, i % 2)

        def on(i, lag):
            return not isinstance(i, int) or 0 <= i - lag < GRAPHS

        def some(eng, semaphore, value, most=GRAPHS):
            if not isinstance(value, int):
                eng.wait_ge(semaphore, value)
            elif value > 0:
                eng.wait_ge(semaphore, value if most is None else min(value, most))

        def alone(eng):
            eng.wait_ge(s["pool_const"], 2)

        def half(i, p):
            return (i - p) // 2 if isinstance(i, int) else (i - p) >> 1

        def batch_rows(k):
            return rows.rearrange("p (c n) v -> p c n v", c=CHUNKS)[:, :, k * BATCH:(k + 1) * BATCH, :]

        others = [(eo_kept[:, t, :], TILES - PAIR * KEPT + t, None) for t in range(PAIR * KEPT)]
        for b in range(VECTOR_BLOCKS, BLOCKS):
            others += [(eo_back[:, b % SLOTS, u, :], b * BLOCK * PAIR + u, b) for u in range(BLOCK * PAIR)]

        block = ctx.enter_context(nc.Block())

        @block.sync
        def _(sp):
            for c in range(4):
                for k, m in enumerate((src, dst)):
                    sp.dma_start(m[:, c * QUARTER:(c + 1) * QUARTER],
                                 edges[k, :].rearrange("(p c) -> p c", p=P)[:, c * QUARTER:(c + 1) * QUARTER]).then_inc(quarter_loaded[c], 16)
            n = 0
            for to, of in (
                (w1[:, :], W1), (b1_c[:, :], b1.rearrange("(c p) -> p c", p=P)),
                (rms_c[:, :], rms_w.rearrange("(c p) -> p c", p=P)),
                (w2[:, :, :], W2.rearrange("(c p) d -> p c d", p=P)),
                (b2_r[:, :], b2[None, :]),
                (eps_c[:, :], eps[None, :].to_broadcast([P, 1])),
                (we1[:, :, :], We1.rearrange("e d f -> d e f")),
                (be1_c[:, :], be1.rearrange("e (c p) -> p (e c)", p=P)),
                (we2[:, :, :], We2.rearrange("e (c p) d -> p (e c) d", p=P)),
                (be2_r[:, :], be2.rearrange("e d -> (e d)")[None, :].to_broadcast([P, EO])),
                (wcat[:, 2 * HEADS:ROW], W_gat),
                (att_r[:, 0, :], att_src.rearrange("h k -> (h k)")[None, :].to_broadcast([P, HK])),
                (att_r[:, 1, :], att_dst.rearrange("h k -> (h k)")[None, :].to_broadcast([P, HK])),
                (bgat_r[:, :], b_gat[None, :].to_broadcast([P, HK])),
                (lng_r[:, :], ln_g[None, :].to_broadcast([P, HK])),
                (lnb_r[:, :], ln_b[None, :].to_broadcast([P, HK])),
            ):
                with nc.allow_non_contiguous_dma(reason="small constants"):
                    sp.dma_start(to, of).then_inc(s["weights"], 16)
                n += 1
            assert n == 16
            sp.wait_ge(s["bk_clear"], 1)
            for k in range(8):
                sp.dma_start(bkeys.rearrange("(p c) one -> p (c one)", p=P)[:, k * 256:(k + 1) * 256], bzeros[:, :]).then_inc(s["bzero"], 16)

            def step(i, p):
                q = 1 - p
                if on(i, -2):
                    some(sp, x_loaded[p], 16 * half(i + 2, p), None)
                    sp.dma_start(xs[:, bass.ds(2 * (i + 2), 2), :], x_t[bass.ds(i + 2, 1), :, :, :][0]).then_inc(x_loaded[p], 16)
                if on(i, -1):
                    some(sp, s["adjT_in_psum"], i)
                    sp.dma_start(adjs[:, q, :, :], adj_t[bass.ds(i + 1, 1), :, :, :][0]).then_inc(adj_loaded[q], 16)
                if on(i, 5):
                    sp.wait_ge(s["tb_ready"], i - 4)
                    sp.dma_start(tab_t[bass.ds(i - 5, 1), :, :, :][0], tb[:, q, :, :]).then_inc(tb_stored[q], 16)

            piped(sp, step)

            for p in range(2):
                sp.wait_ge(scattered[p], 16 * SENT // 2)
            sp.dma_start(bk, bkeys.rearrange("(p c) one -> p (c one)", p=P).bitcast(fp32)).then_inc(s["bk_loaded"], 16)
            for p in range(2):
                sp.wait_ge(tb_stored[p], 16 * GRAPHS // 2)
            with nc.allow_non_contiguous_dma(reason="four columns of the table"):
                sp.dma_start(a_dst[:, :, :], table[0:M, HEADS:2 * HEADS].rearrange("(t q) c -> q t c", q=P)).then_inc(s["last_loaded"], 16)
            sp.dma_start(last_node[:, :], table[M - 1:M, :].to_broadcast([P, ROW])).then_inc(s["last_loaded"], 16)
            def ostore(g, p):
                sp.wait_ge(s["eo_used"], PAIR * g + PAIR)
                sp.dma_start(out_g[bass.ds(g, 1), :, :][0], eo[:, p, :, :].rearrange("p k c -> p (k c)")).then_inc(eo_stored[p], 16)

            with sp.Fori(0, (GROUPS - KEPT) // 2) as j:
                ostore(2 * j, 0)
                ostore(2 * j + 1, 1)
            sp.wait_ge(s["agg_out"], 8)
            sp.dma_start(agg[OWN:P, :, :], odd[:, :, :]).then_inc(s["odd_moved"], 16)

            sp.wait_ge(s["redo_ready"], 1)
            again = sp.value_load(redo[0:1, 0:1], min_val=0, max_val=1)
            with sp.If(again > 0):
                sp.wait_ge(s["sorted_over"], 1)
                sp.dma_start(srcs[:, 0:ECOLS], edges[0, :].rearrange("(p c) -> p c", p=P)).then_inc(s["edges_loaded"], 16)
                sp.dma_start(dsts[:, 0:ECOLS], edges[1, :].rearrange("(p c) -> p c", p=P)).then_inc(s["edges_loaded"], 16)
                sp.dma_start(table[M:M + 1, :], zrow[0:1, :]).then_inc(s["state_init"], 16)
                sp.dma_start(state[M:M + 1, :], st0[0:1, :]).then_inc(s["state_init"], 16)
                for t in range(TILES):
                    sp.dma_start(state[t * P:(t + 1) * P, :], st0[:, :]).then_inc(s["state_init"], 16)
                for p in range(2):
                    sp.wait_ge(row_stored[p], 16 * ETILES // 2)
                sp.dma_start(agg[:, :, :], state[0:M, :].rearrange("(t q) c -> q t c", q=P)).then_inc(s["agg_in"], 16)

            def rstore(g, n, signal):
                sp.dma_start(out_t[bass.ds(g, n), :, :, :].rearrange("g q u d -> q g u d"),
                             xs[:, bass.ds(PAIR * g, PAIR * n), :].rearrange("q (g u) d -> q g u d", g=n)).then_inc(signal, 16)

            for b in range(VECTOR_BLOCKS):
                sp.wait_ge(s["combined"], b + 1)
                if b + SLOTS < BLOCKS:
                    sp.dma_start(eo_back[:, b, :, :].rearrange("p (g k) c -> p g (k c)", g=BLOCK),
                                 out_b[b + SLOTS, :, :, :]).then_inc(eo_loaded[b], 16)
                rstore(BLOCK * b, BLOCK, out_stored[1])
                if b < KEPT // 2:
                    sp.wait_ge(s["others_combined"], 4 * (b + 1))
                    rstore(GROUPS - KEPT + 2 * b, 2, out_stored[0])
            for b in range(VECTOR_BLOCKS, BLOCKS):
                sp.wait_ge(s["others_combined"], PAIR * KEPT + BLOCK * PAIR * (b - VECTOR_BLOCKS + 1))
                rstore(BLOCK * b, BLOCK, out_stored[1])
            sp.wait_ge(out_stored[0], 16 * (KEPT // 2))
            sp.wait_ge(out_stored[1], 16 * BLOCKS)
            for p in range(2):
                sp.wait_ge(eo_stored[p], 16 * (GROUPS - KEPT) // 2)
                sp.wait_ge(tb_stored[p], 16 * GRAPHS // 2)

        @block.gpsimd
        def _(pool):
            pool.memset(ident[:, :], 0.0).then_inc(s["const_a"], 1)
            pool.memset(ones[:, :], 1.0).then_inc(s["const_a"], 1)
            pool.wait_ge(s["const_a"], 2)
            pool.affine_select(out=ident[:, :], in_=ident[:, :], compare_op=ALU.not_equal, fill=1.0,
                               base=0, pattern=[[-1, P]], channel_multiplier=1).then_inc(s["pool_const"], 1)
            pool.affine_select(out=lower[:, :], in_=ones[:, :], compare_op=ALU.is_gt, fill=0.0,
                               base=0, pattern=[[-1, P]], channel_multiplier=1).then_inc(s["pool_const"], 1)
            pool.memset(zrow[:, :], 0.0).then_inc(s["zero_done"], 1)
            pool.memset(st0[:, 0:HEADS], LOW).then_inc(s["zero_done"], 1)
            pool.memset(st0[:, HEADS:ROW], 0.0).then_inc(s["zero_done"], 1)
            pool.memset(bzeros[:, :], 0).then_inc(s["bk_clear"], 1)
            pool.iota(iota_lo[:, :, :], pattern=[[1, P], [0, FB]], base=0, channel_multiplier=0, allow_small_or_imprecise_dtypes=True).then_inc(s["iotas"], 1)
            pool.iota(iota_own[:, :], pattern=[[1, OWN]], base=0, channel_multiplier=0, allow_small_or_imprecise_dtypes=True).then_inc(s["iotas"], 1)
            pool.iota(place0[:, :], pattern=[[0, 1]], base=0, channel_multiplier=CELL, allow_small_or_imprecise_dtypes=True).then_inc(s["iotas"], 1)
            pool.iota(self_keys[:, :], pattern=[[1 << 13, OWN]], base=(K_REAL << 13) + M - 1, channel_multiplier=OWN << 13).then_inc(s["iotas"], 1)

            last_place = pool.to_reg(P * BKEYS - 1)
            pool.wait_ge(s["bzero"], 8 * 16)

            def send(j, p, n):
                pool.wait_ge(s["sent_ready"], (n >> 2) + 1)
                if not isinstance(n, int):
                    pool.wait_ge(scattered[p], 16 * SEND * n)
                pool.tensor_copy(stage_k[:, p, :], sent.bitcast(i32)[:, bass.ds(j * SEND, SEND)]).then_inc(s["staged_k"], 1)
                pool.tensor_copy(stage_w[:, p, :], where[:, bass.ds(j * SEND, SEND)]).then_inc(s["staged_k"], 1)
                both = pool.to_reg(2 * j + 2)
                alone(pool)
                pool.wait_ge(s["staged_k"], both)
                for c in range(SEND):
                    pool.indirect_dma_start(bkeys, bass.IndirectOffsetOnAxis(ap=stage_w[:, p, c:c + 1], axis=0), stage_k[:, p, c:c + 1], None,
                                            bounds_check=last_place, oob_is_err=False).then_inc(scattered[p], 16)

            send(0, 0, 0)
            send(1, 1, 0)
            with pool.Fori(1, SENT // SEND // 2) as j:
                send(2 * j, 0, j)
                send(2 * j + 1, 1, j)

            last_source = pool.to_reg(M - 1)
            for p in range(2):
                pool.wait_ge(tb_stored[p], 16 * GRAPHS // 2)

            def fetch(j, p, n):
                pool.wait_ge(s["idx_done"], (n >> 2) + 1)
                pool.tensor_copy(stage_i[:, p, :], idxT[:, bass.ds(j * GATHER, GATHER)]).then_inc(s["staged_i"], 1)
                one = pool.to_reg(j + 1)
                alone(pool)
                pool.wait_ge(s["staged_i"], one)
                for c in range(GATHER):
                    pool.indirect_dma_start(stage_r[:, p, c, :], None, table[0:M, :], bass.IndirectOffsetOnAxis(ap=stage_i[:, p, c:c + 1], axis=0),
                                            bounds_check=last_source, oob_is_err=False).then_inc(gathered[p], 16)

            def move(j, p, n):
                pool.wait_ge(gathered[p], 16 * GATHER * (n + 1))
                pool.tensor_copy(rows[:, bass.ds(j * GATHER, GATHER), :], stage_r[:, p, :, :]).then_inc(s["rows_moved"], 1)
                pool.wait_ge(s["rows_moved"], j + 1)

            fetch(0, 0, 0)
            fetch(1, 1, 0)
            BEFORE_KEYS = (OWNED * ROW - ECOLS) // (ROW * GATHER) // 2
            assert (2 * BEFORE_KEYS - 2) * GATHER * ROW <= OWNED * ROW - ECOLS
            for first, past in ((1, BEFORE_KEYS), (BEFORE_KEYS, OWNED // GATHER // 2)):
                if first > 1:
                    pool.wait_ge(s["far_taken"], 1)
                with pool.Fori(first, past) as j:
                    move(2 * j - 2, 0, j - 1)
                    fetch(2 * j, 0, j)
                    move(2 * j - 1, 1, j - 1)
                    fetch(2 * j + 1, 1, j)
            move(OWNED // GATHER - 2, 0, OWNED // GATHER // 2 - 1)
            move(OWNED // GATHER - 1, 1, OWNED // GATHER // 2 - 1)

            pool.wait_ge(s["redo_ready"], 1)
            again = pool.value_load(redo[0:1, 0:1], min_val=0, max_val=1)
            with pool.If(again > 0):
                pool.wait_ge(s["sorted_over"], 1)
                pool.iota(srcs[:, ECOLS:ETILES], pattern=[[P, TILES]], base=0, channel_multiplier=1).then_inc(s["iota_done"], 1)
                pool.iota(dsts[:, ECOLS:ETILES], pattern=[[P, TILES]], base=0, channel_multiplier=1).then_inc(s["iota_done"], 1)
                pool.wait_ge(s["state_init"], 16 * (TILES + 2))
                last_row = pool.to_reg(M)
                def gather(rows, source, column, signal):
                    pool.indirect_dma_start(rows[:, :], None, source, bass.IndirectOffsetOnAxis(ap=idx[:, column:column + 1], axis=0),
                                            bounds_check=last_row, oob_is_err=False).then_inc(signal, 16)

                def edge_tile(t, p):
                    done, indices = pool.to_reg(t + 1), pool.to_reg(2 * t + 2)
                    alone(pool)
                    pool.wait_ge(s["idx_ready"], indices)
                    gather(srow, table, 0, src_in[p])
                    gather(drow, table, 1, dst_in[p])
                    gather(strow, state, 1, state_in[p])
                    alone(pool)
                    pool.wait_ge(s["newrow_ready"], done)
                    pool.indirect_dma_start(state, bass.IndirectOffsetOnAxis(ap=sidx[:, 0:1], axis=0), newrow[:, :], None,
                                            bounds_check=last_row, oob_is_err=False).then_inc(row_stored[p], 16)

                with pool.Fori(0, ETILES // 2) as j:
                    edge_tile(2 * j, 0)
                    edge_tile(2 * j + 1, 1)

            pool.wait_ge(s["gates_ready"], 1)
            for n, (of, t, b) in enumerate(others):
                row = xs[:, t, :]
                pool.wait_ge(s["gated"], n + 1)
                pool.tensor_tensor(of[:, 0:2 * D], of[:, 0:2 * D], of[:, 2 * D:4 * D], ALU.add).then_inc(s["sum_chain"], 1)
                pool.wait_ge(s["sum_chain"], 2 * n + 1)
                pool.tensor_tensor(of[:, 0:D], of[:, 0:D], of[:, D:2 * D], ALU.add).then_inc(s["sum_chain"], 1)
                pool.wait_ge(s["sum_chain"], 2 * n + 2)
                pool.tensor_tensor(row, row, of[:, 0:D], ALU.add).then_inc(s["others_combined"], 1)

        @block.tensor
        def _(pe):
            pe.wait_ge(s["pool_const"], 2)
            pe.wait_ge(s["weights"], 16 * 16)

            def step(i, p):
                q = 1 - p
                if on(i, 0):
                    pe.wait_ge(adj_loaded[p], 16 * half(i, p) + 16)
                    some(pe, s["adjT_ready"], i)
                    for nt in range(2):
                        for mt in range(2):
                            last = nc.tensor.transpose(ps_T[:, mt, nt * P:(nt + 1) * P],
                                                       adjs[:, p, nt, mt * P:(mt + 1) * P], ident[:, :])
                    last.then_inc(s["adjT_in_psum"], 1)
                if on(i, 5):
                    pe.wait_ge(s["x2nT_ready"], i - 4)
                    pe.wait_ge(s["wcat_ready"], 2)
                    some(pe, s["tb_ready"], i - 5)
                    some(pe, s["x1_ready"], i - 3)
                    for u in range(2):
                        last = nc.tensor.matmul(ps_B[:, u * ROW:(u + 1) * ROW],
                                                x2nTc[:, q, u * P:(u + 1) * P], wcat[:, :], start=True, stop=True)
                    last.then_inc(s["tb_in_psum"], 1)
                if on(i, 1):
                    pe.wait_ge(s["aggT_ready"], i)
                    some(pe, s["u_ready"], i - 2)
                    for c in range(HC):
                        last = nc.tensor.matmul(ps_H[:, q, c, :], w1[:, c * P:(c + 1) * P], aggT[:, q, :], start=True, stop=True)
                    last.then_inc(s["h_in_psum"], 1)
                if on(i, 0):
                    pe.wait_ge(s["xn_ready"], i + 1)
                    pe.wait_ge(s["adjT_ready"], i + 1)
                    some(pe, s["aggT_ready"], i)
                    some(pe, s["ms_ready"], i + 3, None)
                    for mt in range(2):
                        last = nc.tensor.matmul(ps_A, xn[:, p, mt, :], adjT[:, p, mt, :],
                                                start=(mt == 0), stop=(mt == 1))
                    last.then_inc(s["aggT_in_psum"], 1)
                if on(i, 3):
                    pe.wait_ge(s["s_ready"], i - 2)
                    some(pe, s["x1_ready"], i - 3)
                    some(pe, s["tb_ready"], i - 4)
                    for nt in range(2):
                        nc.tensor.matmul(ps_O[:, nt, :], ones[0:1, :], b2_r[:, :], start=True, stop=False)
                        for c in range(HC):
                            last = nc.tensor.matmul(ps_O[:, nt, :], ss[:, q, c, nt * P:(nt + 1) * P], w2[:, c, :],
                                                    start=False, stop=(c == HC - 1))
                    last.then_inc(s["o_in_psum"], 1)
                if on(i, 2):
                    pe.wait_ge(s["root_ready"], i + 2)
                    some(pe, s["x2nT_ready"], i - 4)
                    some(pe, s["rb_ready"], i - 2)
                    for u in range(2):
                        last = nc.tensor.matmul(ps_R[:, u * P:(u + 1) * P], root[:, 2 + u:3 + u].to_broadcast([P, P]),
                                                ident[:, :], start=True, stop=True)
                    last.then_inc(s["rb_in_psum"], 1)
                if on(i, 4):
                    pe.wait_ge(s["x2n_ready"], i - 3)
                    some(pe, s["x2nT_ready"], i - 4)
                    for u in range(2):
                        last = nc.tensor.transpose(ps_X[:, u * P:(u + 1) * P], x2n[:, p, u, :], ident[:, :])
                    last.then_inc(s["x2nT_in_psum"], 1)
                if on(i, 1):
                    pe.wait_ge(s["sq_ready"], i)
                    some(pe, s["ms_ready"], i + 3, None)
                    some(pe, s["aggT_ready"], i + 1)
                    for u in range(2):
                        for c in range(HC):
                            last = nc.tensor.matmul(ps_Q[:, u:u + 1], sq[:, q, c, u * P:(u + 1) * P], ones[:, 0:1],
                                                    start=(c == 0), stop=(c == HC - 1))
                    last.then_inc(s["ss_in_psum"], 1)

            piped(pe, step)

            for c in range(CHUNKS):
                pe.wait_ge(s["own_ready"], c + 1)
                for k in range(2):
                    last = nc.tensor.transpose(halfH[c][:, k * P:(k + 1) * P], bw[:, k, c * P:(c + 1) * P], ident[:, :])
                last.then_inc(s["idx_in_psum"], 1)
            obank = [bank_T[:, :], bank_A[:, :]]
            pe.wait_ge(s["idx_done"], CHUNKS)

            def experts(g, p, outs):
                def counts(b):
                    pe.wait_ge(s["hot_built"], 4 * g + b + 1)
                    for c in range(FB):
                        last = nc.tensor.matmul(ps_F, hot_lo[b % 2][:, :, c], hot_hi[b % 2][:, :, c],
                                                start=(isinstance(g, int) and g + b + c == 0),
                                                stop=(isinstance(g, int) and g == GROUPS - 1 and b == 3 and c == FB - 1))
                    last.then_inc(s["hot_used"], 1)

                more = not isinstance(g, int) or g < GROUPS
                for k in range(PAIR):
                    if more:
                        for e in (2 * k, 2 * k + 1):
                            some(pe, s["hh_ready"], 4 * g + e - 3, None)
                            for c in range(2):
                                last = nc.tensor.matmul(halfH[e][:, c * GROUP:(c + 1) * GROUP], we1[:, e, c * P:(c + 1) * P],
                                                        x2nT[:, bass.ds(g * GROUP, GROUP)], start=True, stop=True)
                            last.then_inc(s["hh_in_psum"], 1)
                        counts(2 * k)
                    if outs:
                        pe.wait_ge(s["hh_ready"], 4 * g)
                        some(pe, s["eo_used"], 2 * (g - 1) + k - 1, None)
                        for j in range(FC):
                            last = nc.tensor.matmul(obank[k][:, (j // 2) * D:(j // 2 + 1) * D], hh[1 - p][:, j, k * P:(k + 1) * P],
                                                    we2[:, j, :], start=(j % 2 == 0), stop=(j % 2 == 1))
                        last.then_inc(s["eo_in_psum"], 1)
                    if more:
                        counts(2 * k + 1)

            experts(0, 0, False)
            experts(1, 1, True)
            experts(2, 0, True)
            experts(3, 1, True)
            with pe.Fori(2, GROUPS // 2 - 1) as j:
                experts(2 * j, 0, True)
                experts(2 * j + 1, 1, True)
            experts(GROUPS - 2, 0, True)
            experts(GROUPS - 1, 1, True)
            experts(GROUPS, 0, True)
            pe.wait_ge(s["eo_used"], TILES)
            pe.wait_ge(s["far_added"], 1)
            pe.wait_ge(s["diff_ready"], 1)
            nc.tensor.matmul(bank_S[:, 0:1], ones[:, :], count[:, 3:4], start=True, stop=True).then_inc(s["total_in_psum"], 1)
            pe.wait_ge(s["redo_ready"], 1)
            pe.wait_ge(s["rows_moved"], OWNED // GATHER)
            pe.wait_ge(s["idx_done"], CHUNKS)
            for n in range(2 * HEADS):
                for c in range(CHUNKS):
                    last = nc.tensor.transpose(banks[n % 8][:, c * P:(c + 1) * P], rows[:, c * P:(c + 1) * P, n], ident[:, :])
                last.then_inc(s["terms_in_psum"], 1)
            for k in range(2 * HEADS):
                pe.wait_ge(s["back_ready"], 1)
                if k == HEADS:
                    pe.wait_ge(s["exp_done"], 1)
                wt = terms[:, (k + HEADS) % (2 * HEADS), :]
                for c in range(CHUNKS):
                    last = nc.tensor.transpose(banks[k][:, c * P:(c + 1) * P], wt[:, c * P:(c + 1) * P], ident[:, :])
                last.then_inc(s["back_in_psum"], 1)
            for k in range(P // BATCH):
                pe.wait_ge(s["hots_built"], k + 1)
                pe.wait_ge(s["lo_ready"], k + 1)
                if k >= 2:
                    pe.wait_ge(s["agg_out"], k - 1)
                for b in range(BATCH):
                    at = b % 4 * 3 * ROW
                    for c in range(CHUNKS):
                        last = nc.tensor.matmul(sums[k % 2][0:OWN, b // 4, at:at + 3 * ROW], hot[k % 2][:, c, :, b],
                                                parts[k % 3][:, c, b, :, :].rearrange("p s v -> p (s v)"),
                                                start=(c == 0), stop=(c == CHUNKS - 1))
                last.then_inc(s["agg_in_psum"], 1)
            again = pe.value_load(redo[0:1, 0:1], min_val=0, max_val=1)
            with pe.If(again > 0):
                def edge_tile(t, p, j):
                    pe.wait_ge(s["dstf_ready"], t + 1)
                    pe.wait_ge(src_in[p], 16 * j + 16)
                    nc.tensor.matmul(bank_T[:, 0:P], dstf[:, 0:1].to_broadcast([P, P]), ident[:, :], start=True, stop=True)
                    for h in range(HEADS):
                        last = nc.tensor.matmul(halfH[0][:, h * P:(h + 1) * P], srow[:, h:h + 1].to_broadcast([P, P]),
                                                ident[:, :], start=True, stop=True)
                    last.then_inc(s["as_in_psum"], 1)
                    pe.wait_ge(s["vals_ready"], t + 1)
                    nc.tensor.matmul(bank_S[:, 0:ACC], eq[:, :], vals[:, :], start=True, stop=True).then_inc(s["sum_in_psum"], 1)

                with pe.Fori(0, ETILES // 2) as j:
                    edge_tile(2 * j, 0, j)
                    edge_tile(2 * j + 1, 1, j)

        @block.scalar
        def _(act):
            for c in range(4):
                act.wait_ge(s["valid_ready"], c + 1)
                if c:
                    act.wait_ge(s["valid_counted"], c)
                nc.scalar.activation(counted, valid[:, c, :], ACT.Identity, accum_out=valid_n[:, c:c + 1]).then_inc(s["valid_counted"], 1)
            act.wait_ge(s["weights"], 16 * 16)
            act.wait_ge(s["pool_const"], 2)

            def step(i, p):
                q = 1 - p
                if on(i, 1):
                    act.wait_ge(s["h_in_psum"], i)
                    some(act, s["ss_in_psum"], i - 2)
                    for c in range(HC):
                        last = nc.scalar.activation(sq[:, q, c, :], ps_H[:, q, c, :], ACT.Square, bias=b1_c[:, c:c + 1])
                    last.then_inc(s["sq_ready"], 1)
                if on(i, 0):
                    act.wait_ge(s["aggT_in_psum"], i + 1)
                    some(act, s["h_in_psum"], i - 1)
                    nc.scalar.activation(aggT[:, p, :], ps_A, ACT.Identity).then_inc(s["aggT_ready"], 1)
                if on(i, 2):
                    act.wait_ge(s["rb_in_psum"], i - 1)
                    some(act, s["x2nT_in_psum"], i - 3)
                    some(act, s["u_ready"], i - 2)
                    nc.scalar.activation(rb[:, :], ps_R, ACT.Identity).then_inc(s["rb_ready"], 1)
                if on(i, 4):
                    act.wait_ge(s["x2nT_in_psum"], i - 3)
                    some(act, s["tb_in_psum"], i - 5)
                    nc.scalar.activation(x2nTc[:, p, :], ps_X, ACT.Identity)
                    nc.scalar.activation(x2nT[:, bass.ds((i - 4) * NODES, NODES)], ps_X,
                                         ACT.Identity).then_inc(s["x2nT_ready"], 1)
                if on(i, 2):
                    act.wait_ge(s["u_ready"], i - 1)
                    some(act, s["o_in_psum"], i - 3)
                    for c in range(HC):
                        last = nc.scalar.activation(ss[:, p, c, :], uu[:, p, c, :], ACT.Silu, scale=rms_c[:, c:c + 1])
                    last.then_inc(s["s_ready"], 1)

            piped(act, step)

            def experts(g, p):
                some(act, s["eo_in_psum"], 2 * g - 2, None)
                for e in range(EXPERTS):
                    act.wait_ge(s["hh_in_psum"], 4 * g + e + 1)
                    for c in range(2):
                        last = nc.scalar.activation(hh[p][:, 2 * e + c, :], halfH[e][:, c * GROUP:(c + 1) * GROUP], ACT.Gelu,
                                                    bias=be1_c[:, 2 * e + c:2 * e + c + 1])
                    last.then_inc(s["hh_ready"], 1)

            experts(0, 0)
            experts(1, 1)
            with act.Fori(1, GROUPS // 2) as j:
                experts(2 * j, 0)
                experts(2 * j + 1, 1)

            for n in range(8):
                act.wait_ge(s["terms_in_psum"], n + 1)
                nc.scalar.activation(terms[:, n, :], banks[n][:, 0:OWNED], ACT.Identity).then_inc(s["terms_ready"], 1)
            act.wait_ge(s["exp_in"], 1)
            nc.scalar.activation(terms[:, 0:HEADS, :], terms[:, 0:HEADS, :], ACT.Exp).then_inc(s["exp_done"], 1)
            for k in range(HEADS, 2 * HEADS):
                act.wait_ge(s["back_in_psum"], k + 1)
                nc.scalar.activation(rows[:, :, k], banks[k][:, 0:OWNED], ACT.Identity).then_inc(s["weights_back"], 1)
            for k in range(HEADS):
                nc.scalar.activation(rows[:, :, k], banks[k][:, 0:OWNED], ACT.Identity).then_inc(s["maxima_back"], 1)

            act.wait_ge(s["maxima_back"], HEADS)
            act.wait_ge(s["vals_made"], 1)

            def hi(k):
                if k >= 3:
                    act.wait_ge(s["agg_in_psum"], k - 2)
                nc.scalar.activation(parts[k % 3][:, :, :, 0, :], batch_rows(k), ACT.Identity).then_inc(s["hi_ready"], 1)

            hi(0)
            hi(1)
            for k in range(P // BATCH):
                act.wait_ge(s["rem_ready"], k + 1)
                nc.scalar.activation(parts[k % 3][:, :, :, 1, :], batch_rows(k), ACT.Identity).then_inc(s["mid_ready"], 1)
                if k + 2 < P // BATCH:
                    hi(k + 2)
            act.wait_ge(s["merge_in"], 1)
            nc.scalar.activation(agg[:, :, 0:HEADS], agg[:, :, 0:HEADS], ACT.Exp)
            nc.scalar.activation(far_e[:, :, :], far_e[:, :, :], ACT.Exp).then_inc(s["merge_exp"], 1)

            act.wait_ge(s["redo_ready"], 1)
            again = act.value_load(redo[0:1, 0:1], min_val=0, max_val=1)
            with act.If(again > 0):
                with act.Fori(0, ETILES) as t:
                    act.wait_ge(s["mnew_ready"], t + 1)
                    nc.scalar.activation(small[:, 4:6, :], small[:, 2:4, :], ACT.Exp).then_inc(s["ee_ready"], 1)

            act.wait_ge(s["agg_out"], 8)
            for b in range(SLOTS):
                act.dma_start(eo_back[:, b, :, :].rearrange("p (g k) c -> p g (k c)", g=BLOCK), out_b[b, :, :, :]).then_inc(eo_loaded[b], 16)
            act.wait_ge(s["gates_e"], 1)
            nc.scalar.activation(gates[:, :, :], sc[:, :, :], ACT.Exp).then_inc(s["gates_exp"], 1)

            act.wait_ge(s["gates_ready"], 1)
            for of, t, b in others:
                if b is not None:
                    act.wait_ge(eo_loaded[b % SLOTS], 16 * (b // SLOTS) + 16)
                for e in range(EXPERTS):
                    at = slice(e * D, (e + 1) * D)
                    last = nc.scalar.activation(of[:, at], of[:, at], ACT.Identity, scale=gates[:, t, e:e + 1])
                last.then_inc(s["gated"], 1)

        @block.vector
        def _(dve):
            V = nc.vector
            prep_n = [0]

            def plink(ins):
                prep_n[0] += 1
                ins.then_inc(s["prep"], 1)
                dve.wait_ge(s["prep"], prep_n[0])

            w = [work[:, k, :] for k in range(3)]
            for c in range(4):
                dve.wait_ge(quarter_loaded[c], 32)
                at = slice(c * QUARTER, (c + 1) * QUARTER)
                kc = keys.rearrange("p g n -> p (g n)")[:, at].bitcast(i32)
                sc_, dc, vc = src[:, at], dst[:, at], valid[:, c, :]
                V.tensor_scalar(vc, dc, float(M), None, ALU.is_lt).then_inc(s["valid_ready"], 1)
                dve.wait_ge(s["valid_ready"], c + 1)
                plink(V.scalar_tensor_tensor(w[1], sc_, float(M - 1), vc, ALU.is_lt, ALU.mult))
                V.tensor_tensor(w[0], sc_, w[1], ALU.mult)
                plink(V.tensor_tensor(w[2], vc, w[1], ALU.subtract))
                plink(V.scalar_tensor_tensor(w[2], dc, float(K_FAR), w[2], ALU.add, ALU.mult))
                V.scalar_tensor_tensor(dc, dc, float(K_REAL), w[1], ALU.add, ALU.mult)
                plink(V.tensor_tensor(w[2].bitcast(i32), w[2], w[0], ALU.add))
                plink(V.scalar_tensor_tensor(kc, dc, 13, w[2].bitcast(i32), ALU.logical_shift_left, ALU.bitwise_or))

            sorts = [0]

            def top(sources, outs, passes):
                for n in range(passes):
                    marks = []
                    for x_, o in zip(sources, outs):
                        V.max(o[:, 8 * n:8 * n + 8], x_).then_inc(s["sorted_"], 1)
                        sorts[0] += 1
                        marks.append(sorts[0])
                    for x_, o, mark in zip(sources, outs, marks):
                        dve.wait_ge(s["sorted_"], mark)
                        V.match_replace(x_, o[:, 8 * n:8 * n + 8], x_, 0.0).then_inc(s["sorted_"], 1)
                        sorts[0] += 1
                    dve.wait_ge(s["sorted_"], sorts[0])

            def take_keys(first, past):
                for g in range(0, ECOLS // SEG, 4):
                    top([keys[:, g + u, :] for u in range(4)], [lev1[:, g + u, first:past] for u in range(4)], (past - first) // 8)

            take_keys(0, REAL1)
            first_real = 2.0 ** -125
            assert K_REAL << 13 == 1 << 24
            plink(V.scalar_tensor_tensor(real1, lev1[:, :, 0:REAL1], first_real, lev1[:, :, 0:REAL1], ALU.is_ge, ALU.mult))
            for g in range(0, 8, 4):
                top([real1[:, GROUP2 * (g + u):GROUP2 * (g + u + 1), :].rearrange("p a b -> p (a b)") for u in range(4)],
                    [lev2[:, g + u, :] for u in range(4)], KEEP2 // 8)
            owner, same, rank, place, bad = (rank_w[:, k, :] for k in range(5))
            V.memset(same[:, 0:1], 0.0)
            dve.wait_ge(s["iotas"], 4)
            for k in range(SENT // PART):
                first, past = k * PART, (k + 1) * PART
                at, new = slice(first, past), slice(max(first, 1), past)
                top([lev2.rearrange("p a b -> p (a b)")], [sent[:, at]], PART // 8)
                plink(V.tensor_scalar(where[:, at], sent[:, at].bitcast(i32), 19, None, ALU.logical_shift_right))
                plink(V.tensor_scalar(owner[:, at], where[:, at], -float(K_REAL // OWN), None, ALU.add))
                V.tensor_scalar(bad[:, at], owner[:, at], 0.0, float(1 << 22), ALU.is_lt, ALU.mult)
                plink(V.tensor_tensor(same[:, new], owner[:, new], owner[:, new.start - 1:past - 1], ALU.is_equal))
                plink(V.tensor_tensor_scan(rank[:, 0:past], same[:, 0:past], same[:, 0:past], 0.0, ALU.mult, ALU.add))
                plink(V.tensor_scalar(place[:, at], rank[:, at], CELL - 0.5, float(1 << 22), ALU.is_gt, ALU.mult))
                V.tensor_tensor(bad[:, at], bad[:, at], rank[:, at], ALU.add)
                plink(V.scalar_tensor_tensor(place[:, at], owner[:, at], float(BKEYS), place[:, at], ALU.mult, ALU.add))
                plink(V.tensor_tensor(place[:, at], place[:, at], bad[:, at], ALU.add))
                V.tensor_scalar(where[:, at], place[:, at], place0[:, 0:1], None, ALU.add).then_inc(s["sent_ready"], 1)
            setup = [0]

            def link1(ins):
                setup[0] += 1
                ins.then_inc(s["setup_chain"], 1)
                dve.wait_ge(s["setup_chain"], setup[0])

            dve.wait_ge(s["weights"], 16 * 16)
            dve.wait_ge(s["pool_const"], 2)
            link1(V.memset(epsI[:, :], 0.0))
            for k in (0, 3):
                link1(V.tensor_scalar(epsI[:, k * P:(k + 1) * P], ident[:, :], eps_c[:, 0:1], None, ALU.mult))
            for k in range(2):
                link1(V.tensor_tensor(watt[:, k, :], wcat[:, 2 * HEADS:ROW], att_r[:, k, :], ALU.mult))
                V.reduce_sum(wcat[:, k * HEADS:(k + 1) * HEADS],
                             watt[:, k, :].rearrange("p (h k) -> p h k", h=HEADS), AX.X).then_inc(s["wcat_ready"], 1)
            link1(V.memset(var[:, :], 1.0))

            def link(name, value, ins):
                ins.then_inc(s[name], 1)
                dve.wait_ge(s[name], value)

            def mean_var(k, n, src, stats, mvs):
                for u in range(2):
                    last = V.bn_stats(stats[:, u, :], src[u])
                last.then_inc(s[f"{k}_stats"], 1)
                alone(dve)
                dve.wait_ge(s[f"{k}_stats"], n)
                for u in range(2):
                    last = V.bn_aggr(mvs[:, u, :], stats[:, u, :])
                last.then_inc(s[f"{k}_mv"], 1)

            def rsqrt(name, v, y, w, scratch, count, fillers=()):
                n, fillers = [0], list(fillers)

                def chain(ins):
                    n[0] += 1
                    ins.then_inc(s[name], 1)
                    if fillers:
                        fillers.pop(0)()
                    dve.wait_ge(s[name], count * NEWTON_LINKS + n[0])

                chain(V.tensor_scalar(y.bitcast(i32), v.bitcast(i32), 1, None, ALU.logical_shift_right))
                V.tensor_scalar(w, v, -0.5, None, ALU.mult)
                chain(V.tensor_scalar(y.bitcast(i32), y.bitcast(i32), -1.0, float(0x5F3759DF), ALU.mult, ALU.add))
                for it in range(3):
                    chain(V.tensor_tensor(scratch, y, y, ALU.mult))
                    chain(V.tensor_tensor(scratch, scratch, w, ALU.mult))
                    last = V.scalar_tensor_tensor(y, scratch, 1.5, y, ALU.add, ALU.mult)
                    if it < 2:
                        chain(last)
                assert n[0] == NEWTON_LINKS and not fillers
                return last

            NEWTON_LINKS = 10

            def tiles(g):
                return [xs[:, bass.ds(2 * g + u, 1), :].squeeze(1) for u in range(2)]

            def step(i, p):
                q = 1 - p
                peeled = isinstance(i, int)
                if on(i, 0):
                    dve.wait_ge(s["adjT_in_psum"], i + 1)
                    if peeled:
                        some(dve, s["aggT_in_psum"], i - 1)
                    V.tensor_tensor(adjT[:, p, :, :].rearrange("p a b -> p (a b)"), bank_T[:, :], epsI[:, :], ALU.add).then_inc(s["adjT_ready"], 1)
                if on(i, -1):
                    if peeled:
                        dve.wait_ge(s["ln1_mv"], i + 2)
                    last = V.tensor_scalar(var[:, 0:2], mv[:, q, :, 1], LN_EPS, None, ALU.add)
                if on(i, 2):
                    if peeled:
                        dve.wait_ge(s["ss_in_psum"], i - 1)
                    last = V.tensor_scalar(var[:, 2:4], ps_Q, 1.0 / H, RMS_EPS, ALU.mult, ALU.add)
                if on(i, 4):
                    dve.wait_ge(s["ln2_mv"], i - 3)
                    last = V.tensor_scalar(var[:, 4:6], mv2[:, p, :, 1], LN_EPS, None, ALU.add)

                fillers = []
                if on(i, 5):
                    def table_out():
                        dve.wait_ge(s["tb_in_psum"], i - 4)
                        some(dve, tb_stored[q], 16 * half(i - 5, q), None)
                        V.tensor_copy(tb[:, q, :, :], ps_B.rearrange("p (u c) -> p u c", u=2)).then_inc(s["tb_ready"], 1)

                    fillers.append(table_out)
                if on(i, -2):
                    def load_stats():
                        alone(dve)
                        dve.wait_ge(x_loaded[p], 16 * half(i + 2, p) + 16)
                        V.bn_stats(st[:, 0, :], tiles(i + 2)[0])

                    def aggregate():
                        alone(dve)
                        dve.wait_ge(s["ln1_stats"], i + 3)
                        V.bn_aggr(mv[:, p, 0, :], st[:, 0, :])

                    fillers += [load_stats,
                                lambda: V.bn_stats(st[:, 1, :], tiles(i + 2)[1]).then_inc(s["ln1_stats"], 1)]
                if on(i, -2):
                    fillers += [aggregate, lambda: V.bn_aggr(mv[:, p, 1, :], st[:, 1, :]).then_inc(s["ln1_mv"], 1)]
                if on(i, -1) or on(i, 2) or on(i, 4):
                    link("ms_ready", i + 3, last)
                    if peeled:
                        some(dve, s["rb_in_psum"], i - 2)
                    rsqrt("newton", var[:, :], root[:, :], nhalf[:, :], newt[:, :], i + 1, fillers).then_inc(s["root_ready"], 1)
                    dve.wait_ge(s["root_ready"], i + 2)
                else:
                    V.tensor_copy(newt[:, 0:1], var[:, 0:1]).then_inc(s["ms_ready"], 1)
                    for filler in fillers:
                        filler()
                if on(i, 4):
                    if peeled:
                        some(dve, s["x2nT_in_psum"], i - 5)
                    for u in range(2):
                        last = V.tensor_scalar(x2n[:, p, u, :], tiles(i - 4)[u], mv2[:, p, u, 0:1], root[:, 4 + u:5 + u], ALU.subtract, ALU.mult)
                    last.then_inc(s["x2n_ready"], 1)
                if on(i, -1):
                    if peeled:
                        some(dve, s["aggT_in_psum"], i)
                    for u in range(2):
                        last = V.tensor_scalar(xn[:, q, u, :], tiles(i + 1)[u], mv[:, q, u, 0:1], root[:, u:u + 1], ALU.subtract, ALU.mult)
                    last.then_inc(s["xn_ready"], 1)
                if on(i, 3):
                    xg = xs[:, bass.ds(2 * (i - 3), 2), :]
                    dve.wait_ge(s["o_in_psum"], i - 2)
                    V.tensor_tensor(xg, xg, ps_O, ALU.add).then_inc(s["x1_ready"], 1)
                if on(i, 2):
                    dve.wait_ge(s["rb_ready"], i - 1)
                    if peeled:
                        some(dve, s["s_ready"], i - 3)
                    for c in range(HC):
                        last = V.scalar_tensor_tensor(uu[:, p, c, :], ps_H[:, p, c, :], b1_c[:, c:c + 1], rb[:, :], ALU.add, ALU.mult)
                    last.then_inc(s["u_ready"], 1)
                if on(i, 3):
                    alone(dve)
                    dve.wait_ge(s["x1_ready"], i - 2)
                    mean_var("ln2", i - 2, tiles(i - 3), st2, mv2[:, q, :, :])

            piped(dve, step)

            def slink(ins):
                own_n[0] += 1
                ins.then_inc(s["own_prep"], 1)
                dve.wait_ge(s["own_prep"], own_n[0])

            own_n = [0]
            dve.wait_ge(s["bk_loaded"], 16)
            segs = bk.rearrange("p (g n) -> p g n", n=SEG_B)
            for g in range(0, BKEYS // SEG_B, 4):
                top([segs[:, g + u, :] for u in range(4)], [blev1[:, g + u, :] for u in range(4)], KEEP_B1 // 8)
            top([blev1[:, GROUP_B2 * u:GROUP_B2 * (u + 1), :].rearrange("p a b -> p (a b)") for u in range(4)],
                [blev2[:, u * KEEP_B2:(u + 1) * KEEP_B2] for u in range(4)], KEEP_B2 // 8)
            slink(V.tensor_copy(blev2[:, 4 * KEEP_B2:4 * KEEP_B2 + OWN], self_keys[:, :].bitcast(fp32)))
            index, dlo, self_, nself, empty, lastw, nlast, tmp = (bw[:, k, :] for k in range(8))
            for c in range(CHUNKS):
                at = slice(c * P, (c + 1) * P)
                top([blev2], [own[:, at]], P // 8)
                ki = own[:, at].bitcast(i32)
                V.tensor_scalar(bi[:, at], ki, 13, None, ALU.logical_shift_right)
                slink(V.tensor_scalar(index[:, at].bitcast(i32), ki, M - 1, None, ALU.bitwise_and))
                V.tensor_scalar(tmp[:, at], bi[:, at], -float(K_REAL + M - 1), None, ALU.add)
                slink(V.tensor_scalar(self_[:, at], index[:, at].bitcast(i32), float(M - 1), None, ALU.is_equal))
                V.tensor_scalar(bi[:, at], bi[:, at], OWN - 1, None, ALU.bitwise_and)
                slink(V.tensor_tensor(tmp[:, at], tmp[:, at], self_[:, at], ALU.mult))
                V.tensor_copy(dlo[:, at], bi[:, at])
                V.tensor_tensor(index[:, at], index[:, at].bitcast(i32), tmp[:, at], ALU.add).then_inc(s["own_ready"], 1)
                dve.wait_ge(s["idx_in_psum"], c + 1)
                V.tensor_copy(dloT[:, at], halfH[c][:, P:2 * P])
                V.tensor_copy(idxT[:, at], halfH[c][:, 0:P]).then_inc(s["idx_done"], 1)
            slink(V.tensor_scalar(empty, own, 0.0, None, ALU.is_equal))
            V.reduce_sum(count[:, 0:1], empty, AX.X)
            slink(V.tensor_scalar(nself, self_, -1.0, 1.0, ALU.mult, ALU.add))
            V.memset(lastw[:, OWNED - 1:OWNED], 1.0)
            slink(V.tensor_copy(lastw[:, 0:OWNED - 1], self_[:, 1:OWNED]))
            slink(V.tensor_scalar(nlast, lastw, -1.0, 1.0, ALU.mult, ALU.add))
            take_keys(REAL1, KEEP1)
            k1 = lev1.rearrange("p a b -> p (a b)").bitcast(i32)
            V.tensor_scalar(far_i, k1, P - 1, None, ALU.bitwise_and).then_inc(s["far_taken"], 1)
            dve.wait_ge(s["far_taken"], 1)
            plink(V.tensor_copy(far_lo[:, :], far_i))
            plink(V.tensor_scalar(far_i, k1, 7, None, ALU.logical_shift_right))
            plink(V.tensor_scalar(far_hi[:, :], far_i, -float(K_FAR >> 7), None, ALU.add))

            obank = [bank_T[:, :], bank_A[:, :]]

            def hot_block(b, k):
                if not isinstance(b, int) or b < FARCOLS // FB:
                    some(dve, s["hot_used"], b - 1, None)
                    V.tensor_tensor(hot_lo[k], far_lo[:, bass.ds(b * FB, FB)].unsqueeze(1).to_broadcast([P, P, FB]),
                                    iota_lo[:, :, :], ALU.is_equal)
                    V.tensor_tensor(hot_hi[k], far_hi[:, bass.ds(b * FB, FB)].unsqueeze(1).to_broadcast([P, OWN, FB]),
                                    iota_lo[:, 0:OWN, :], ALU.is_equal).then_inc(s["hot_built"], 1)

            def hots(g):
                for k in range(PAIR):
                    hot_block(4 * g + 2 * k + 2, 0)
                    if not isinstance(g, int) or g > 0:
                        eout(g - 1, k)
                    hot_block(4 * g + 2 * k + 3, 1)

            def eout(g, k):
                dve.wait_ge(s["eo_in_psum"], PAIR * g + k + 1)
                V.tensor_tensor(eout.to(g, k), obank[k], be2_r[:, :], ALU.add).then_inc(s["eo_used"], 1)

            def in_buffer(p):
                return lambda g, k: eo[:, p, k, :]

            def kept(g, k):
                return eo_kept[:, bass.ds(PAIR * (g - GROUPS + KEPT) + k, 1), :].squeeze(1)

            hot_block(0, 0)
            hot_block(1, 1)
            hots(0)
            eout.to = in_buffer(0)
            hots(1)
            eout.to = in_buffer(1)
            hots(2)
            with dve.Fori(1, (GROUPS - KEPT) // 2) as j:
                for p in range(2):
                    dve.wait_ge(eo_stored[p], 16 * j)
                    eout.to = in_buffer(p)
                    hots(2 * j + p + 1)
            eout.to = kept
            with dve.Fori((GROUPS - KEPT) // 2, GROUPS // 2 - 1) as j:
                hots(2 * j + 1)
                hots(2 * j + 2)
            hots(GROUPS - 1)
            eout(GROUPS - 1, 0)
            eout(GROUPS - 1, 1)
            dve.wait_ge(s["hot_used"], 4 * GROUPS)
            V.tensor_copy(far[:, :], ps_F).then_inc(s["far_added"], 1)
            dve.wait_ge(s["far_added"], 1)
            dve.wait_ge(s["valid_counted"], 4)
            V.reduce_sum(count[:, 1:2], valid_n[:, :], AX.X)
            slink(V.reduce_sum(count[:, 2:3], far[:, :], AX.X))
            slink(V.tensor_tensor(count[:, 3:4], count[:, 0:1], count[:, 1:2], ALU.add))
            slink(V.tensor_tensor(count[:, 3:4], count[:, 3:4], count[:, 2:3], ALU.subtract))
            V.tensor_scalar(count[:, 3:4], count[:, 3:4], float(OWN - OWNED), None, ALU.add).then_inc(s["diff_ready"], 1)
            dve.wait_ge(s["total_in_psum"], 1)
            V.tensor_scalar(redo[:, :], bank_S[:, 0:1], 0.5, None, ALU.is_gt).then_inc(s["redo_ready"], 1)
            far_s, far_h = last_node[:, 0:HEADS], last_node[:, 2 * HEADS:ROW]
            NH = [P, TILES, HEADS]
            dve.wait_ge(s["last_loaded"], 32)
            slink(V.tensor_tensor(far_e[:, :, :], a_dst[:, :, :], far_s.unsqueeze(1).to_broadcast(NH), ALU.add))
            slink(V.scalar_tensor_tensor(far_e[:, :, :], far_e[:, :, :], 0.2, far_e[:, :, :], ALU.mult, ALU.max))
            slink(V.tensor_scalar(gs[:, 0, :], far[:, :], 0.5, None, ALU.is_lt))
            slink(V.tensor_scalar(gs[:, 0, :], gs[:, 0, :], LOW, None, ALU.mult))
            slink(V.tensor_tensor(far_e[:, :, :], far_e[:, :, :], gs[:, 0, :].unsqueeze(2).to_broadcast(NH), ALU.add))
            slink(V.tensor_scalar(empty, empty, LOW, None, ALU.mult))
            slink(V.tensor_scalar(tmp, self_, LOW, None, ALU.mult))
            for p in range(2):
                dve.wait_ge(eo_stored[p], 16 * (GROUPS - KEPT) // 2)

            def hots_of(k):
                for c in range(CHUNKS):
                    last = V.tensor_tensor(hot[k % 2][:, c, :, :],
                                           dloT[:, c * P + BATCH * k:c * P + BATCH * (k + 1)].unsqueeze(1).to_broadcast([P, OWN, BATCH]),
                                           iota_batch, ALU.is_equal)
                last.then_inc(s["hots_built"], 1)

            slink(V.tensor_copy(iota_batch, iota_own[:, :].unsqueeze(2).to_broadcast([P, OWN, BATCH])))
            hots_of(0)

            SH = [P, HEADS, OWNED]

            def each(m):
                return m.unsqueeze(1).to_broadcast(SH)

            a_s, a_d = terms[:, 0:HEADS, :], terms[:, HEADS:2 * HEADS, :]
            w0, w1_ = (ow[:, k, :, :] for k in range(2))
            dve.wait_ge(s["terms_ready"], 8)
            slink(V.tensor_tensor(a_d, a_d, each(self_), ALU.mult))
            for h in range(HEADS):
                V.tensor_tensor_scan(w0[:, h, :], nself, a_d[:, h, :], 0.0, ALU.mult, ALU.add)
            slink(V.tensor_tensor(a_s, a_s, each(empty), ALU.add))
            for h in range(HEADS):
                last = V.tensor_tensor_scan(a_d[:, h, :], tmp, a_s[:, h, :], LOW, ALU.add, ALU.max)
            slink(last)
            slink(V.tensor_tensor(a_d, a_d, each(lastw), ALU.mult))
            for h in range(HEADS):
                last = V.tensor_tensor_scan(w1_[:, h, ::-1], nlast[:, ::-1], a_d[:, h, ::-1], 0.0, ALU.mult, ALU.add)
            slink(V.tensor_tensor(a_s, a_s, w0, ALU.add))
            slink(V.tensor_tensor(w1_, w1_, w0, ALU.add))
            V.scalar_tensor_tensor(a_s, a_s, 0.2, a_s, ALU.mult, ALU.max)
            slink(V.scalar_tensor_tensor(w1_, w1_, 0.2, w1_, ALU.mult, ALU.max))
            V.tensor_tensor(a_s, a_s, w1_, ALU.subtract).then_inc(s["exp_in"], 1)
            V.tensor_tensor(a_d, w1_, each(self_), ALU.mult).then_inc(s["back_ready"], 1)
            for h in range(HEADS):
                at = slice(2 * HEADS + h * EXPERTS, 2 * HEADS + (h + 1) * EXPERTS)
                dve.wait_ge(s["weights_back"], h + 1)
                last = V.tensor_tensor(rows[:, :, at], rows[:, :, at],
                                       rows[:, :, HEADS + h].unsqueeze(2).to_broadcast([P, OWNED, EXPERTS]), ALU.mult)
            last.then_inc(s["vals_made"], 1)

            def remainder(k):
                dve.wait_ge(s["hi_ready"], k + 1)
                V.tensor_tensor(batch_rows(k), batch_rows(k), parts[k % 3][:, :, :, 0, :], ALU.subtract).then_inc(s["rem_ready"], 1)

            def lowest(k):
                dve.wait_ge(s["mid_ready"], k + 1)
                V.tensor_tensor(parts[k % 3][:, :, :, 2, :], batch_rows(k), parts[k % 3][:, :, :, 1, :], ALU.subtract).then_inc(s["lo_ready"], 1)

            def take_bank(k):
                dve.wait_ge(s["agg_in_psum"], k + 1)
                by_part = sums[k % 2][0:OWN, :, 0:4 * 3 * ROW].rearrange("p g (t u s v) -> p g t u s v", u=2, s=3, v=ROW)
                tiles_ = slice(BATCH // 2 * k, BATCH // 2 * (k + 1))
                outs = [m[0:OWN, tiles_, :].rearrange("p (g t) v -> p g t v", g=4) for m in (agg, odd)]
                for u, o in enumerate(outs):
                    last = V.reduce_sum(o, by_part[:, :, :, u, :, :].rearrange("p g t s v -> p g t v s"), AX.X)
                last.then_inc(s["agg_out"], 1)

            dve.wait_ge(s["maxima_back"], HEADS)
            hots_of(1)
            remainder(0)
            for k in range(P // BATCH):
                if k + 1 < P // BATCH:
                    remainder(k + 1)
                lowest(k)
                if k >= 1:
                    take_bank(k - 1)
                    if k + 1 < P // BATCH:
                        hots_of(k + 1)
            take_bank(P // BATCH - 1)
            dve.wait_ge(s["odd_moved"], 16)
            dve.wait_ge(s["agg_out"], 8)
            old_m, den_n, acc_n = agg[:, :, 0:HEADS], agg[:, :, HEADS:2 * HEADS], agg[:, :, 2 * HEADS:ROW]
            slink(V.tensor_tensor(a_dst[:, :, :], old_m, far_e[:, :, :], ALU.max))
            V.tensor_tensor(old_m, old_m, a_dst[:, :, :], ALU.subtract)
            V.tensor_tensor(far_e[:, :, :], far_e[:, :, :], a_dst[:, :, :], ALU.subtract).then_inc(s["merge_in"], 1)
            dve.wait_ge(s["merge_exp"], 1)
            V.tensor_tensor(den_n, den_n, old_m, ALU.mult)
            slink(V.tensor_tensor(far_e[:, :, :], far_e[:, :, :], far[:, :].unsqueeze(2).to_broadcast(NH), ALU.mult))
            for h in range(HEADS):
                at = slice(h * EXPERTS, (h + 1) * EXPERTS)
                V.tensor_tensor(acc_n[:, :, at], acc_n[:, :, at], old_m[:, :, h].unsqueeze(2).to_broadcast([P, TILES, EXPERTS]), ALU.mult)
                last = V.tensor_tensor(gf[:, :, at], far_e[:, :, h].unsqueeze(2).to_broadcast([P, TILES, EXPERTS]),
                                       far_h[:, at].unsqueeze(1).to_broadcast([P, TILES, EXPERTS]), ALU.mult)
            slink(last)
            slink(V.tensor_tensor(den_n, den_n, far_e[:, :, :], ALU.add))
            slink(V.tensor_tensor(acc_n, acc_n, gf[:, :, :], ALU.add))

            dve.wait_ge(s["redo_ready"], 1)
            again = dve.value_load(redo[0:1, 0:1], min_val=0, max_val=1)
            with dve.If(again > 0):
                V.memset(signal[:, :], 0.0).then_inc(s["sorted_over"], 1)
                dve.wait_ge(s["edges_loaded"], 32)
                V.tensor_scalar(srcs[:, 0:ECOLS], srcs[:, 0:ECOLS], M - 1, None, ALU.min).then_inc(s["edges_ready"], 1)
                V.tensor_scalar(dsts[:, 0:ECOLS], dsts[:, 0:ECOLS], M, None, ALU.min).then_inc(s["edges_ready"], 1)
                dve.wait_ge(s["edges_ready"], 2)
                dve.wait_ge(s["iota_done"], 2)
                LINKS = 11
                def edge_tile(t, p, j):
                    k = [0]

                    def chain(ins):
                        k[0] += 1
                        ins.then_inc(s["edge_chain"], 1)
                        dve.wait_ge(s["edge_chain"], LINKS * t + k[0])

                    some(dve, row_stored[1 - p], 16 * j + 16 * p, None)
                    V.tensor_copy(idx[:, 0:1], srcs[:, bass.ds(t, 1)]).then_inc(s["idx_ready"], 1)
                    V.tensor_copy(idx[:, 1:2], dsts[:, bass.ds(t, 1)]).then_inc(s["idx_ready"], 1)
                    V.tensor_copy(dstf[:, :], dsts[:, bass.ds(t, 1)]).then_inc(s["dstf_ready"], 1)
                    dve.wait_ge(s["dstf_ready"], t + 1)
                    dve.wait_ge(s["as_in_psum"], t + 1)
                    V.tensor_scalar(eq[:, :], bank_T[:, 0:P], dstf[:, 0:1], None, ALU.is_equal).then_inc(s["eq_ready"], 1)
                    dve.wait_ge(s["eq_ready"], t + 1)
                    chain(V.tensor_scalar(pen[:, :], eq[:, :], -1.0, -LOW, ALU.add, ALU.mult))
                    chain(V.tensor_tensor(masked[:, :, :], halfH[0].rearrange("p (h n) -> p h n", h=HEADS),
                                          pen[:, :].unsqueeze(1).to_broadcast([P, HEADS, P]), ALU.add))
                    chain(V.reduce_max(small[:, 0, :], masked[:, :, :], AX.X))
                    for signal in (src_in, dst_in, state_in):
                        dve.wait_ge(signal[p], 16 * j + 16)
                    V.tensor_tensor(small[:, 1, :], srow[:, 0:HEADS], drow[:, HEADS:2 * HEADS], ALU.add)
                    chain(V.tensor_tensor(small[:, 0, :], small[:, 0, :], drow[:, HEADS:2 * HEADS], ALU.add))
                    chain(V.scalar_tensor_tensor(small[:, 6:8, :], small[:, 0:2, :], 0.2, small[:, 0:2, :], ALU.mult, ALU.max))
                    chain(V.tensor_tensor(newrow[:, 0:HEADS], small[:, 6, :], strow[:, 0:HEADS], ALU.max))
                    V.tensor_tensor(small[:, 2, :], small[:, 7, :], newrow[:, 0:HEADS], ALU.subtract)
                    V.tensor_tensor(small[:, 3, :], strow[:, 0:HEADS], newrow[:, 0:HEADS], ALU.subtract).then_inc(s["mnew_ready"], 1)
                    chain(V.tensor_tensor(masked[:, 0, :], eq[:, :], lower[:, :], ALU.mult))
                    chain(V.reduce_sum(lead[:, 0:1], masked[:, 0, :], AX.X))
                    chain(V.tensor_scalar(lead[:, 1:2], lead[:, 0:1], 1.0, float(1 << 20), ALU.min, ALU.mult))
                    V.tensor_tensor(sidx[:, :], lead[:, 1:2], dstf[:, :], ALU.add)
                    dve.wait_ge(s["ee_ready"], t + 1)
                    V.tensor_copy(vals[:, 0:HEADS], small[:, 4, :])
                    V.tensor_tensor(vals[:, HEADS:ACC].rearrange("p (h k) -> p h k", h=HEADS),
                                    srow[:, 2 * HEADS:ROW].rearrange("p (h k) -> p h k", h=HEADS),
                                    small[:, 4, :].unsqueeze(2).to_broadcast([P, HEADS, EXPERTS]), ALU.mult).then_inc(s["vals_ready"], 1)
                    V.tensor_tensor(newrow[:, HEADS:2 * HEADS], strow[:, HEADS:2 * HEADS], small[:, 5, :], ALU.mult)
                    chain(V.tensor_tensor(newrow[:, 2 * HEADS:ROW].rearrange("p (h k) -> p h k", h=HEADS),
                                          strow[:, 2 * HEADS:ROW].rearrange("p (h k) -> p h k", h=HEADS),
                                          small[:, 5, :].unsqueeze(2).to_broadcast([P, HEADS, EXPERTS]), ALU.mult))
                    dve.wait_ge(s["sum_in_psum"], t + 1)
                    chain(V.tensor_tensor(newrow[:, HEADS:ROW], newrow[:, HEADS:ROW], bank_S[:, 0:ACC], ALU.add))
                    V.tensor_copy(lead[:, 2:3], lead[:, 0:1]).then_inc(s["newrow_ready"], 1)
                    assert k[0] == LINKS, k[0]

                edge_tile(0, 0, 0)
                edge_tile(1, 1, 0)
                with dve.Fori(1, ETILES // 2) as j:
                    edge_tile(2 * j, 0, j)
                    edge_tile(2 * j + 1, 1, j)
                dve.wait_ge(s["agg_in"], 16)


            gates_n = [0]

            def glink(ins):
                gates_n[0] += 1
                ins.then_inc(s["gate_chain"], 1)
                dve.wait_ge(s["gate_chain"], gates_n[0])

            def heads(t):
                return t.rearrange("p t (h k) -> p t h k", h=HEADS)

            def over(t, shape, axis):
                return t.unsqueeze(axis).to_broadcast(shape)

            T16 = [P, TILES, HK]
            den = agg[:, :, HEADS:2 * HEADS]
            glink(V.tensor_scalar(den, den, 1e-16, None, ALU.add))
            glink(V.reciprocal(den, den))
            for t in range(HEADS):
                last = V.tensor_tensor(gf[:, :, t * EXPERTS:(t + 1) * EXPERTS], agg[:, :, 2 * HEADS + t * EXPERTS:2 * HEADS + (t + 1) * EXPERTS],
                                       over(agg[:, :, HEADS + t], [P, TILES, EXPERTS], 2), ALU.mult)
            glink(last)
            glink(V.tensor_tensor(gf[:, :, :], gf[:, :, :], over(bgat_r[:, :], T16, 1), ALU.add))
            mean, gvar, groot = gs[:, 0, :], gs[:, 1, :], gs[:, 2, :]
            glink(V.reduce_sum(mean, gf[:, :, :], AX.X))
            glink(V.tensor_scalar(mean, mean, 1.0 / HK, None, ALU.mult))
            glink(V.tensor_tensor(gf[:, :, :], gf[:, :, :], over(mean, T16, 2), ALU.subtract))
            glink(V.tensor_tensor(gw[:, :, :], gf[:, :, :], gf[:, :, :], ALU.mult))
            glink(V.reduce_sum(gvar, gw[:, :, :], AX.X))
            glink(V.tensor_scalar(gvar, gvar, 1.0 / HK, LN_EPS, ALU.mult, ALU.add))
            glink(rsqrt("gate_newton", gvar, groot, gs[:, 3, :], gs[:, 4, :], 0))
            glink(V.tensor_tensor(gf[:, :, :], gf[:, :, :], over(groot, T16, 2), ALU.mult))
            glink(V.tensor_tensor(gf[:, :, :], gf[:, :, :], over(lng_r[:, :], T16, 1), ALU.mult))
            glink(V.tensor_tensor(gf[:, :, :], gf[:, :, :], over(lnb_r[:, :], T16, 1), ALU.add))
            glink(V.reduce_sum(sc[:, :, :], gf[:, :, :].rearrange("p t (h k) -> p t k h", h=HEADS), AX.X))
            glink(V.tensor_scalar(sc[:, :, :], sc[:, :, :], 1.0 / HEADS, None, ALU.mult))
            beaten = gw[:, :, 0:12].rearrange("p t (e f) -> p t e f", e=EXPERTS)
            for f in range(EXPERTS):
                for e in range(f + 1, EXPERTS):
                    V.tensor_tensor(beaten[:, :, e, f], sc[:, :, f], sc[:, :, e], ALU.is_ge)
                    last = V.tensor_tensor(beaten[:, :, f, e - 1], sc[:, :, e], sc[:, :, f], ALU.is_gt)
            glink(last)
            cnt = gf[:, :, 0:EXPERTS]
            glink(V.reduce_sum(cnt, beaten, AX.X))
            glink(V.tensor_scalar(cnt, cnt, 1.5, None, ALU.is_lt))
            glink(V.reduce_max(mean, sc[:, :, :], AX.X))
            V.tensor_tensor(sc[:, :, :], sc[:, :, :], over(mean, [P, TILES, EXPERTS], 2), ALU.subtract).then_inc(s["gates_e"], 1)
            dve.wait_ge(s["gates_exp"], 1)
            glink(V.tensor_tensor(gates[:, :, :], gates[:, :, :], cnt, ALU.mult))
            glink(V.reduce_sum(mean, gates[:, :, :], AX.X))
            glink(V.reciprocal(mean, mean))
            V.tensor_tensor(gates[:, :, :], gates[:, :, :], over(mean, [P, TILES, EXPERTS], 2), ALU.mult).then_inc(s["gates_ready"], 1)
            dve.wait_ge(s["gates_ready"], 1)

            for b in range(VECTOR_BLOCKS):
                first = b * BLOCK * PAIR
                dve.wait_ge(eo_loaded[b % SLOTS], 16 * (b // SLOTS) + 16)
                for e in range(EXPERTS):
                    for u in range(BLOCK * PAIR):
                        row = xs[:, first + u, :]
                        if e:
                            dve.wait_ge(s["comb_chain"], (b * (EXPERTS - 1) + e - 1) * BLOCK * PAIR + u + 1)
                        last = V.scalar_tensor_tensor(row, eo_back[:, b % SLOTS, u, e * D:(e + 1) * D], gates[:, first + u, e:e + 1],
                                                      row, ALU.mult, ALU.add)
                        if e < EXPERTS - 1:
                            last.then_inc(s["comb_chain"], 1)
                last.then_inc(s["combined"], 1)


_INS = ["x", "adj", "L0_gnn_epsilon", "L0_gnn_W1", "L0_gnn_b1", "L0_gnn_rms_weight", "L0_gnn_W2", "L0_gnn_b2",
        "L0_ffn_W_gat", "L0_ffn_att_src", "L0_ffn_att_dst", "L0_ffn_b_gat", "L0_ffn_ln_gamma", "L0_ffn_ln_beta",
        "L0_ffn_W1", "L0_ffn_b1", "L0_ffn_W2", "L0_ffn_b2", "L0_ffn_edge_index"]


def kernel(**inputs):
    import numpy as np
    import concourse.bacc as bacc
    from concourse import mybir as mb
    from concourse.bass_utils import run_bass_kernel_spmd

    nc = bacc.Bacc("TRN2", target_bir_lowering=False, num_devices=1)
    arrays, args = {}, []
    for name in _INS:
        a = np.ascontiguousarray(inputs[name])
        if a.ndim == 0:
            a = a.reshape(1)
        arrays[f"in_{name}"] = a
        args.append(nc.dram_tensor(f"in_{name}", a.shape, mb.dt.from_np(a.dtype), kind="ExternalInput").ap())
    args.append(nc.dram_tensor("out_x", (GRAPHS, NODES, D), mb.dt.float32, kind="ExternalOutput").ap())
    build(nc, *args)
    r = run_bass_kernel_spmd(nc, [arrays], core_ids=[0])
    return r.results[0]["out_x"]
```
